# Optimizing a Trainium2 kernel written in Bass

```python
import numpy as np
import jax
import jax.numpy as jnp

def _softmax(x, axis=-1):
    return jax.nn.softmax(x, axis=axis)

def _gelu(x):
    return jax.nn.gelu(x, approximate=True)

def _silu(x):
    return jax.nn.silu(x)

def _sigmoid(x):
    return jax.nn.sigmoid(x)

def _layernorm(x, axis=-1, eps=1e-05):
    m = jnp.mean(x, axis=axis, keepdims=True)
    v = jnp.var(x, axis=axis, keepdims=True)
    return (x - m) / jnp.sqrt(v + eps)

def _scatter_add(tgt, idx, src, axis=0):
    return tgt.at[idx].add(src)

def _segment_sum(src, seg, n):
    return jax.ops.segment_sum(src, seg, n)
kernel_name = 'mk_gnn_resnorm_d4_gnn_r16_a83871'

def setup_inputs(seed: int=0):
    np.random.seed(seed)
    _w = jnp.asarray

    def _rec_inputs():
        import jax
        import jax.numpy as jnp
        _gk = jax.random.key(seed)
        x = -0.0003713 + 1 * jax.random.normal(jax.random.fold_in(_gk, 1), (3125, 256), jnp.float32)
        src = jax.random.randint(jax.random.fold_in(_gk, 2), (100000,), 0, 3125, jnp.int32)
        dst = jnp.minimum((3125 * jax.random.uniform(jax.random.fold_in(_gk, 3), (100000,)) ** 2.0).astype(jnp.int32), 49999)
        _o = jnp.argsort(dst, stable=True)
        src = src[_o]
        dst = dst[_o]
        edge_attr_128 = -5.16925e-05 + 1.00005 * jax.random.normal(jax.random.fold_in(_gk, 12), (100000, 128), jnp.float32)
        edge_weight = jax.random.uniform(jax.random.fold_in(_gk, 14), (100000,), jnp.float32, 0.0, 0.999998)
        edge_weight_n2 = jax.random.uniform(jax.random.fold_in(_gk, 15), (100000,), jnp.float32, 0.0, 0.999998)
        return (x, src, dst, edge_attr_128, edge_weight, edge_weight_n2)
    x, src, dst, edge_attr_128, edge_weight, edge_weight_n2 = _rec_inputs()

    def _L0_gnn_setup():
        import jax, jax.numpy as jnp
        import numpy as np
        N = 3125
        E = 50000
        D = 256

        def gcn_conv(x, W, src, dst, n):
            h = x @ W
            ones = jnp.ones(src.shape[0], dtype=h.dtype)
            deg = jax.ops.segment_sum(ones, dst, num_segments=n)
            dinv = jnp.where(deg > 0, jax.lax.rsqrt(deg), 0.0)
            norm = dinv[src] * dinv[dst]
            msgs = h[src] * norm[:, None]
            return jax.ops.segment_sum(msgs, dst, num_segments=n)
        key = jax.random.key(seed)
        k1, k2, k3, k4 = jax.random.split(key, 4)
        x = jax.random.normal(k1, (N, D), dtype=jnp.float32)
        edge_index = jax.random.randint(k2, (2, E), 0, N, dtype=jnp.int64)
        scale = 1.0 / np.sqrt(D)
        W1 = jax.random.normal(k3, (D, D), dtype=jnp.float32) * scale
        W2 = jax.random.normal(k4, (D, D), dtype=jnp.float32) * scale
        return {'x': x, 'edge_index': edge_index, 'W1': W1, 'W2': W2}
    _L0_gnn_all = _L0_gnn_setup()
    _L0_gnn_in = {k: v for k, v in _L0_gnn_all.items() if k in ('W1', 'W2')}
    del _L0_gnn_all

    def _L1_gnn_setup():
        import jax, jax.numpy as jnp
        import numpy as np
        N_NODES = 3125
        N_EDGES = 50000
        IN_DIM = 256
        OUT_DIM = 256
        HEADS = 1
        EDGE_DIM = 128
        NEG_SLOPE = 0.01
        key = jax.random.key(seed)
        ks = jax.random.split(key, 8)
        x = jax.random.normal(ks[0], (N_NODES, IN_DIM), dtype=jnp.float32)
        edge_index = jax.random.randint(ks[1], (2, N_EDGES), 0, N_NODES, dtype=jnp.int64)
        edge_attr = jax.random.normal(ks[2], (N_EDGES, EDGE_DIM), dtype=jnp.float32)
        hc = HEADS * OUT_DIM
        Wn = jax.random.normal(ks[3], (hc, IN_DIM), dtype=jnp.float32) / np.sqrt(IN_DIM)
        bn = jnp.zeros((hc,), dtype=jnp.float32)
        We = jax.random.normal(ks[4], (hc, EDGE_DIM), dtype=jnp.float32) / np.sqrt(EDGE_DIM)
        be = jnp.zeros((hc,), dtype=jnp.float32)
        attn = jax.random.normal(ks[5], (1, HEADS, OUT_DIM), dtype=jnp.float32) * np.sqrt(2.0 / (HEADS * OUT_DIM + 1))
        return {'x': x, 'edge_index': edge_index, 'edge_attr': edge_attr, 'Wn': Wn, 'bn': bn, 'We': We, 'be': be, 'attn': attn}
    _L1_gnn_all = _L1_gnn_setup()
    _L1_gnn_in = {k: v for k, v in _L1_gnn_all.items() if k in ('Wn', 'bn', 'We', 'be', 'attn')}
    del _L1_gnn_all

    def _L2_gnn_setup():
        import jax, jax.numpy as jnp
        import numpy as np
        N_NODES = 6250
        N_EDGES = 50000
        DIM = 256
        EPS = 1e-05
        key = jax.random.key(seed)
        ks = jax.random.split(key, 12)
        H = DIM
        s = 1.0 / np.sqrt(H)
        s2 = 1.0 / np.sqrt(2 * H)
        return {'feat': jax.random.normal(ks[0], (N_NODES, DIM), dtype=jnp.float32), 'src': jax.random.randint(ks[1], (N_EDGES,), 0, N_NODES, dtype=jnp.int32), 'dst': jax.random.randint(ks[2], (N_EDGES,), 0, N_NODES, dtype=jnp.int32), 'iw': jax.random.uniform(ks[3], (N_EDGES,), dtype=jnp.float32), 'ow': jax.random.uniform(ks[4], (N_EDGES,), dtype=jnp.float32), 'gamma': jnp.ones((DIM,), jnp.float32), 'beta': jnp.zeros((DIM,), jnp.float32), 'W_in': jax.random.uniform(ks[5], (H, H), jnp.float32, -s, s), 'b_in': jax.random.uniform(ks[6], (H,), jnp.float32, -s, s), 'W_out': jax.random.uniform(ks[7], (H, H), jnp.float32, -s, s), 'b_out': jax.random.uniform(ks[8], (H,), jnp.float32, -s, s), 'W_x2i': jax.random.uniform(ks[9], (2 * H, 2 * H), jnp.float32, -s2, s2), 'b_x2i': jax.random.uniform(ks[10], (2 * H,), jnp.float32, -s2, s2), 'W_h2h': jax.random.uniform(ks[11], (H, 2 * H), jnp.float32, -s, s)}
    _L2_gnn_all = _L2_gnn_setup()
    _L2_gnn_in = {k: v for k, v in _L2_gnn_all.items() if k in ('gamma', 'beta', 'W_in', 'b_in', 'W_out', 'b_out', 'W_x2i', 'b_x2i', 'W_h2h')}
    del _L2_gnn_all

    def _L3_gnn_setup():
        import jax, jax.numpy as jnp
        import numpy as np
        N_NODES = 6250
        N_EDGES = 100000
        IN_DIM = 256
        HID0 = 128
        HID1 = 64

        def _glorot(key, shape):
            fan_in, fan_out = (shape[0], shape[1])
            lim = (6.0 / (fan_in + fan_out)) ** 0.5
            return jax.random.uniform(key, shape, jnp.float32, -lim, lim)

        def gcn_conv(x, edge_index, W, b):
            n = x.shape[0]
            loop = jnp.arange(n, dtype=edge_index.dtype)
            row = jnp.concatenate([edge_index[0], loop])
            col = jnp.concatenate([edge_index[1], loop])
            deg = jax.ops.segment_sum(jnp.ones_like(col, jnp.float32), col, num_segments=n)
            dis = jnp.where(deg > 0, jax.lax.rsqrt(jnp.maximum(deg, 1e-12)), 0.0)
            norm = dis[row] * dis[col]
            h = x @ W
            msg = h[row] * norm[:, None]
            out = jax.ops.segment_sum(msg, col, num_segments=n)
            return out + b
        key = jax.random.key(seed)
        ks = jax.random.split(key, 8)
        x = jax.random.normal(ks[0], (N_NODES, IN_DIM), jnp.float32)
        edge_index = jax.random.randint(ks[1], (2, N_EDGES), 0, N_NODES, jnp.int32)
        return {'x': x, 'edge_index': edge_index, 'W_conv': _glorot(ks[2], (IN_DIM, HID0)), 'b_conv': jnp.zeros((HID0,), jnp.float32), 'W_lin': _glorot(ks[3], (HID0, HID1)), 'b_lin': jnp.zeros((HID1,), jnp.float32), 'W_dec1': _glorot(ks[4], (HID1, HID0)), 'b_dec1': jnp.zeros((HID0,), jnp.float32), 'W_dec2': _glorot(ks[5], (HID0, IN_DIM)), 'b_dec2': jnp.zeros((IN_DIM,), jnp.float32)}
    _L3_gnn_all = _L3_gnn_setup()
    _L3_gnn_in = {k: v for k, v in _L3_gnn_all.items() if k in ('W_conv', 'b_conv', 'W_lin', 'b_lin', 'W_dec1', 'b_dec1', 'W_dec2', 'b_dec2')}
    del _L3_gnn_all
    return {'x': x, 'src': src, 'dst': dst, 'edge_attr_128': edge_attr_128, 'edge_weight': edge_weight, 'edge_weight_n2': edge_weight_n2, 'L0_gnn_W1': _L0_gnn_in['W1'], 'L0_gnn_W2': _L0_gnn_in['W2'], 'L1_gnn_Wn': _L1_gnn_in['Wn'], 'L1_gnn_bn': _L1_gnn_in['bn'], 'L1_gnn_We': _L1_gnn_in['We'], 'L1_gnn_be': _L1_gnn_in['be'], 'L1_gnn_attn': _L1_gnn_in['attn'], 'L2_gnn_gamma': _L2_gnn_in['gamma'], 'L2_gnn_beta': _L2_gnn_in['beta'], 'L2_gnn_W_in': _L2_gnn_in['W_in'], 'L2_gnn_b_in': _L2_gnn_in['b_in'], 'L2_gnn_W_out': _L2_gnn_in['W_out'], 'L2_gnn_b_out': _L2_gnn_in['b_out'], 'L2_gnn_W_x2i': _L2_gnn_in['W_x2i'], 'L2_gnn_b_x2i': _L2_gnn_in['b_x2i'], 'L2_gnn_W_h2h': _L2_gnn_in['W_h2h'], 'L3_gnn_W_conv': _L3_gnn_in['W_conv'], 'L3_gnn_b_conv': _L3_gnn_in['b_conv'], 'L3_gnn_W_lin': _L3_gnn_in['W_lin'], 'L3_gnn_b_lin': _L3_gnn_in['b_lin'], 'L3_gnn_W_dec1': _L3_gnn_in['W_dec1'], 'L3_gnn_b_dec1': _L3_gnn_in['b_dec1'], 'L3_gnn_W_dec2': _L3_gnn_in['W_dec2'], 'L3_gnn_b_dec2': _L3_gnn_in['b_dec2']}

def reference(x, src, dst, edge_attr_128, edge_weight, edge_weight_n2, L0_gnn_W1, L0_gnn_W2, L1_gnn_Wn, L1_gnn_bn, L1_gnn_We, L1_gnn_be, L1_gnn_attn, L2_gnn_gamma, L2_gnn_beta, L2_gnn_W_in, L2_gnn_b_in, L2_gnn_W_out, L2_gnn_b_out, L2_gnn_W_x2i, L2_gnn_b_x2i, L2_gnn_W_h2h, L3_gnn_W_conv, L3_gnn_b_conv, L3_gnn_W_lin, L3_gnn_b_lin, L3_gnn_W_dec1, L3_gnn_b_dec1, L3_gnn_W_dec2, L3_gnn_b_dec2):
    import jax
    import jax.numpy as jnp

    def _L0_gnn_ref(x, edge_index, W1, W2):
        import jax, jax.numpy as jnp
        import numpy as np
        N = 3125
        E = 50000
        D = 256

        def gcn_conv(x, W, src, dst, n):
            h = x @ W
            ones = jnp.ones(src.shape[0], dtype=h.dtype)
            deg = jax.ops.segment_sum(ones, dst, num_segments=n)
            dinv = jnp.where(deg > 0, jax.lax.rsqrt(deg), 0.0)
            norm = dinv[src] * dinv[dst]
            msgs = h[src] * norm[:, None]
            return jax.ops.segment_sum(msgs, dst, num_segments=n)
        n = x.shape[0]
        loops = jnp.arange(n, dtype=edge_index.dtype)
        src = jnp.concatenate([edge_index[0], loops])
        dst = jnp.concatenate([edge_index[1], loops])
        h = gcn_conv(x, W1, src, dst, n)
        h = jax.nn.relu(h)
        return gcn_conv(h, W2, src, dst, n)

    def _L1_gnn_ref(x, edge_index, edge_attr, Wn, bn, We, be, attn):
        import jax, jax.numpy as jnp
        import numpy as np
        N_NODES = 3125
        N_EDGES = 50000
        IN_DIM = 256
        OUT_DIM = 256
        HEADS = 1
        EDGE_DIM = 128
        NEG_SLOPE = 0.01
        N = x.shape[0]
        H, C = (attn.shape[1], attn.shape[2])
        src, dst = (edge_index[0], edge_index[1])
        h = x @ Wn.T + bn
        e = edge_attr @ We.T + be
        xj = h[src].reshape(-1, H, C)
        ee = e.reshape(-1, H, C)
        a = jax.nn.leaky_relu(jnp.sum((xj + ee) * attn, axis=-1), NEG_SLOPE)
        m = jax.ops.segment_max(a, dst, num_segments=N)
        a = jnp.exp(a - m[dst])
        denom = jax.ops.segment_sum(a, dst, num_segments=N)
        a = a / (denom[dst] + 1e-16)
        msg = (xj * a[..., None]).reshape(-1, H * C)
        out = jax.ops.segment_sum(msg, dst, num_segments=N)
        return jax.nn.relu(out)

    def _L2_gnn_ref(feat, src, dst, iw, ow, gamma, beta, W_in, b_in, W_out, b_out, W_x2i, b_x2i, W_h2h):
        import jax, jax.numpy as jnp
        import numpy as np
        N_NODES = 6250
        N_EDGES = 50000
        DIM = 256
        EPS = 1e-05
        N = feat.shape[0]
        num_steps = 1
        mean = jnp.mean(feat, axis=0)
        var = jnp.var(feat, axis=0)
        h = (feat - mean) * jax.lax.rsqrt(var + EPS) * gamma + beta
        for _ in range(num_steps):
            feat_in = h @ W_in + b_in
            feat_out = h @ W_out + b_out
            a_in = jax.ops.segment_sum(feat_in[src] * iw[:, None], dst, num_segments=N)
            a_out = jax.ops.segment_sum(feat_out[dst] * ow[:, None], src, num_segments=N)
            a = jnp.concatenate((a_in, a_out), axis=1)
            xi = a @ W_x2i + b_x2i
            hh = h @ W_h2h
            i_i, i_n = jnp.split(xi, 2, axis=1)
            h_i, h_n = jnp.split(hh, 2, axis=1)
            input_gate = jax.nn.sigmoid(i_i + h_i)
            new_gate = jnp.tanh(i_n + h_n)
            h = new_gate + input_gate * (h - new_gate)
        return h

    def _L3_gnn_ref(x, edge_index, W_conv, b_conv, W_lin, b_lin, W_dec1, b_dec1, W_dec2, b_dec2):
        import jax, jax.numpy as jnp
        import numpy as np
        N_NODES = 6250
        N_EDGES = 100000
        IN_DIM = 256
        HID0 = 128
        HID1 = 64

        def _glorot(key, shape):
            fan_in, fan_out = (shape[0], shape[1])
            lim = (6.0 / (fan_in + fan_out)) ** 0.5
            return jax.random.uniform(key, shape, jnp.float32, -lim, lim)

        def gcn_conv(x, edge_index, W, b):
            n = x.shape[0]
            loop = jnp.arange(n, dtype=edge_index.dtype)
            row = jnp.concatenate([edge_index[0], loop])
            col = jnp.concatenate([edge_index[1], loop])
            deg = jax.ops.segment_sum(jnp.ones_like(col, jnp.float32), col, num_segments=n)
            dis = jnp.where(deg > 0, jax.lax.rsqrt(jnp.maximum(deg, 1e-12)), 0.0)
            norm = dis[row] * dis[col]
            h = x @ W
            msg = h[row] * norm[:, None]
            out = jax.ops.segment_sum(msg, col, num_segments=n)
            return out + b
        h = gcn_conv(x, edge_index, W_conv, b_conv)
        h = jax.nn.relu(h)
        z = h @ W_lin + b_lin
        d = jax.nn.relu(z @ W_dec1 + b_dec1)
        out = d @ W_dec2 + b_dec2
        return out
    edge_index = jnp.stack([src, dst])
    x = _layernorm(x + _L0_gnn_ref(x, edge_index, L0_gnn_W1, L0_gnn_W2), axis=-1)
    x = _layernorm(x + _L1_gnn_ref(x, edge_index, edge_attr_128, L1_gnn_Wn, L1_gnn_bn, L1_gnn_We, L1_gnn_be, L1_gnn_attn), axis=-1)
    x = _layernorm(x + _L2_gnn_ref(x, src, dst, edge_weight, edge_weight_n2, L2_gnn_gamma, L2_gnn_beta, L2_gnn_W_in, L2_gnn_b_in, L2_gnn_W_out, L2_gnn_b_out, L2_gnn_W_x2i, L2_gnn_b_x2i, L2_gnn_W_h2h), axis=-1)
    x = _layernorm(x + _L3_gnn_ref(x, edge_index, L3_gnn_W_conv, L3_gnn_b_conv, L3_gnn_W_lin, L3_gnn_b_lin, L3_gnn_W_dec1, L3_gnn_b_dec1, L3_gnn_W_dec2, L3_gnn_b_dec2), axis=-1)
    return x

_drawn_inputs = setup_inputs


def setup_inputs(seed=0):
    import zlib

    import numpy as np

    out = dict(_drawn_inputs(seed))
    spreads = {'L1_gnn_bn': (0.0, 0.1),
     'L1_gnn_be': (0.0, 0.8),
     'L2_gnn_gamma': (1.0, 0.2),
     'L2_gnn_beta': (0.0, 0.1),
     'L3_gnn_b_conv': (0.0, 0.1),
     'L3_gnn_b_lin': (0.0, 0.1),
     'L3_gnn_b_dec1': (0.0, 0.1),
     'L3_gnn_b_dec2': (0.0, 0.1)}
    factors = {'L2_gnn_b_x2i': 7.795}
    for name, (base, spread) in spreads.items():
        noise = np.random.default_rng([zlib.crc32(name.encode()), seed]).standard_normal(out[name].shape)
        drawn = base * np.exp(spread * noise) if base else spread * noise
        out[name] = jnp.asarray(drawn.astype(out[name].dtype))
    for name, factor in factors.items():
        out[name] = (out[name] * factor).astype(out[name].dtype)
    return out
```

```python
import concourse.bass as bass
from concourse import mybir
from contextlib import ExitStack

fp32 = mybir.dt.float32
bf16 = mybir.dt.bfloat16
i32 = mybir.dt.int32
ALU = mybir.AluOpType
ACT = mybir.ActivationFunctionType
AX = mybir.AxisListType
ds = bass.ds

N = 3125
E = 100000
D = 256
DE = 128
P = 125
NB = N // P
EC = E // P
L = 128
BUCKETS = NB * NB
G = 4
NC = (E + BUCKETS * (L - 1)) // L + (G - 1) * NB
NC = -(-NC // G) * G
NG = NC // G
F = 8
SRC, DST, WIN, WOUT, EDGE = range(5)
TS = 128
BIG = 1.0e30
MAGIC = 12582912.0
EPS = 1e-5


class Steps:

    def __init__(self, sems, unroll, amount=1, i0=0):
        self.sems, self.unroll, self.amount, self.i0 = sems, unroll, amount, i0

    def from_turn(self, i0):
        return Steps(self.sems, self.unroll, self.amount, i0)

    def sem(self, j):
        return self.sems[j % len(self.sems)]

    def _count(self, i, j):
        s = len(self.sems)
        return (i + self.i0) * len(range(j % s, self.unroll, s)) + j // s

    def after(self, eng, i, j):
        eng.wait_ge(self.sem(j), (self._count(i, j) + 1) * self.amount)

    def freed(self, eng, i, j):
        eng.wait_ge(self.sem(j), self._count(i, j) * self.amount)


class Chain:

    def __init__(self, eng, sem, start=0):
        self.eng, self.sem, self.start, self.n = eng, sem, start, 0

    def __call__(self, ins):
        self.n += 1
        ins.then_inc(self.sem, 1)
        self.eng.wait_ge(self.sem, self.start + self.n)


class Scope:

    def __init__(self, nc, ctx, tag):
        self.nc, self.ctx, self.tag = nc, ctx, tag
        self.sems = []

    def sb(self, name, shape, dt=fp32):
        return self.ctx.enter_context(self.nc.sbuf_tensor(f"{self.tag}_{name}", shape, dt))

    def ps(self, name, shape, dt=fp32):
        return self.ctx.enter_context(self.nc.psum_tensor(f"{self.tag}_{name}", shape, dt))

    def sem(self, name):
        self.sems.append(self.ctx.enter_context(self.nc.semaphore(f"{self.tag}_{name}")))
        return self.sems[-1]

    def steps(self, name, slots=2, unroll=5, amount=1):
        return Steps([self.sem(f"{name}{s}") for s in range(slots)], unroll, amount)


def clear_semaphores(nc, scope):
    with nc.Block() as block:

        @block.gpsimd
        def _(pool):
            for sem in scope.sems:
                pool.sem_clear(sem)


def phase_order(nc, k, src, dst, w_in, w_out, edge_attr, we, be, attn):
    ctx = ExitStack()
    with ctx:
        s = Scope(nc, ctx, "ord")
        sblk, dblk = s.sb("sblk", [P, EC]), s.sb("dblk", [P, EC])
        key = s.sb("key", [P, EC])
        pay = s.sb("pay", [P, EC, 4])
        base = s.sb("base", [NB, NB])
        attnc = s.sb("attnc", [128, 2])
        attnb = s.sb("attnb", [128, 2, P])
        we_sb = s.sb("we_sb", [128, 2, DE])
        bec = s.sb("bec", [128, 2])
        vrow = s.sb("vrow", [P, DE])
        becol = s.sb("becol", [P, 1])
        tri = s.sb("tri", [P, P])
        ptri = s.sb("ptri", [NB, 32])
        iop = s.sb("iop", [128, 1])
        io25 = s.sb("io25", [P, NB])

        with ExitStack() as inner:
            a = Scope(nc, inner, "cnt")
            raws, rawd = a.sb("raws", [P, EC], i32), a.sb("rawd", [P, EC], i32)
            win, wout = a.sb("win", [P, EC]), a.sb("wout", [P, EC])
            node = a.sb("node", [P, EC])
            tmp = a.sb("tmp", [P, EC])
            ohs, ohd = a.sb("ohs", [P, EC, NB], bf16), a.sb("ohd", [P, EC, NB], bf16)
            empty = a.sb("empty", [128, NC // 12, F])
            keyt = a.sb("keyt", [100, 2, 8, P])
            m4 = a.sb("m4", [4 * NB, 4 * NB])
            tot = a.sb("tot", [NB, NB])
            nch = a.sb("nch", [NB, NB])
            inc = a.sb("inc", [NB, NB])
            one25 = a.sb("one25", [NB, NB])
            grp = a.sb("grp", [NB, 1])
            g0 = a.sb("g0", [NB, 1])
            first = a.sb("first", [NB, NB])
            ioc = a.sb("ioc", [NB, NC])
            acc = a.sb("acc", [NB, NC])
            row = a.sb("row", [1, NC])
            rq = a.sb("rq", [1, NC])
            pT = a.ps("pT", [128, 16, 128])
            pM = a.ps("pM", [128, 512])
            pK = a.ps("pK", [128, 512])
            pR = a.ps("pR", [128, 1024])
            loaded, consts, filled = a.sem("loaded"), a.sem("consts"), a.sem("filled")
            dve_chain, keyed, hot, turned = a.sem("dve_chain"), a.sem("keyed"), a.sem("hot"), a.sem("turned")
            copied, stored, counted, summed, m4ed = (a.sem(n) for n in ("copied", "stored", "counted", "summed", "m4ed"))
            grouped, prefixed, listed, rowed, packed = (a.sem(n) for n in ("grouped", "prefixed", "listed", "rowed", "packed"))
            spread, vdone = a.sem("spread"), a.sem("vdone")
            pool_chain = a.sem("pool_chain")
            with nc.Block() as block:

                @block.sync
                def _(sp):
                    sp.dma_start(raws[:, :], src.rearrange("(p c) -> p c", p=P)).then_inc(loaded, 16)
                    sp.dma_start(rawd[:, :], dst.rearrange("(p c) -> p c", p=P)).then_inc(loaded, 16)
                    sp.dma_start(win[:, :], w_in.rearrange("(p c) -> p c", p=P)).then_inc(loaded, 16)
                    sp.dma_start(wout[:, :], w_out.rearrange("(p c) -> p c", p=P)).then_inc(loaded, 16)
                    sp.dma_start(attnc[:, :], attn.rearrange("o h (t c) -> c (o h t)", t=2),
                                 allow_slow_non_contiguous=True).then_inc(loaded, 16)
                    sp.dma_start(bec[:, :], be.rearrange("(t c) -> c t", t=2),
                                 allow_slow_non_contiguous=True).then_inc(loaded, 16)
                    sp.dma_start(we_sb[:, :, :], we.rearrange("(t c) k -> c t k", t=2)).then_inc(loaded, 16)
                    sp.wait_ge(filled, 1)
                    for q in range(12):
                        w = NC // 12
                        sp.dma_start(k["slots"][:, q * w:(q + 1) * w, :], empty[:, :, :]).then_inc(stored, 16)
                    sp.wait_ge(copied, 2)
                    for t, name in enumerate(("key_rows", "dblk_rows")):
                        sp.dma_start(k[name].rearrange("(q c) p -> c q p", q=8),
                                     keyt[:, t, :, :]).then_inc(stored, 16)
                    sp.wait_ge(stored, 14 * 16)

                @block.gpsimd
                def _(pool):
                    def made(ins):
                        ins.then_inc(consts, 1)

                    made(nc.gpsimd.iota(k["iota"][:, :], [[1, P]], 0, 0, allow_small_or_imprecise_dtypes=True))
                    made(nc.gpsimd.iota(k["iota_bf"][:, :], [[1, P]], 0, 0, allow_small_or_imprecise_dtypes=True))
                    made(nc.gpsimd.iota(iop[:, :], [[0, 1]], 0, 1, allow_small_or_imprecise_dtypes=True))
                    made(nc.gpsimd.iota(io25[:, :], [[1, NB]], 0, 0, allow_small_or_imprecise_dtypes=True))
                    made(nc.gpsimd.iota(ioc[:, :], [[1, NC]], 0, 0, allow_small_or_imprecise_dtypes=True))
                    made(nc.gpsimd.memset(k["ones"][:, :], 1.0))
                    made(nc.gpsimd.memset(one25[:, :], 1.0))
                    made(nc.gpsimd.memset(k["zeros_bf"][:, :], 0.0))
                    made(nc.gpsimd.memset(acc[:, :], 0.0))
                    nc.gpsimd.memset(empty[:, :, :], -1.0).then_inc(filled, 1)
                    nc.gpsimd.memset(k["ident"][:, :], 0.0).then_inc(pool_chain, 1)
                    nc.gpsimd.memset(tri[:, :], 1.0).then_inc(pool_chain, 1)
                    nc.gpsimd.memset(ptri[:, :], 1.0).then_inc(pool_chain, 1)
                    pool.wait_ge(pool_chain, 3)
                    made(nc.gpsimd.affine_select(out=k["ident"][:, :], in_=k["ident"][:, :], compare_op=ALU.not_equal,
                                                 fill=1.0, base=0, pattern=[[-1, 128]], channel_multiplier=1))
                    made(nc.gpsimd.affine_select(out=tri[:, :], in_=tri[:, :], compare_op=ALU.is_gt,
                                                 fill=0.0, base=0, pattern=[[-1, P]], channel_multiplier=1))
                    made(nc.gpsimd.affine_select(out=ptri[:, :], in_=ptri[:, :], compare_op=ALU.is_gt,
                                                 fill=0.0, base=0, pattern=[[1, 32]], channel_multiplier=-1))

                @block.vector
                def _(dve):
                    chain = Chain(dve, dve_chain)
                    v = nc.vector
                    dve.wait_ge(loaded, 7 * 16)
                    dve.wait_ge(consts, 12)
                    for t in range(2):
                        ins = v.tensor_scalar(attnb[:, t, :], k["ones"][:, :], attnc[:, t:t + 1], None, ALU.mult)
                    ins.then_inc(spread, 1)
                    for raw, blk, f in ((raws, sblk, SRC), (rawd, dblk, DST)):
                        chain(v.tensor_copy(node[:, :], raw[:, :]))
                        chain(v.tensor_scalar(tmp[:, :], node[:, :], -float(P // 2), 1.0 / P, ALU.add, ALU.mult))
                        chain(v.tensor_scalar(tmp[:, :], tmp[:, :], MAGIC, None, ALU.add))
                        chain(v.tensor_scalar(blk[:, :], tmp[:, :], -MAGIC, None, ALU.add))
                        chain(v.scalar_tensor_tensor(pay[:, :, f], blk[:, :], -float(P), node[:, :], ALU.mult, ALU.add))
                    v.scalar_tensor_tensor(key[:, :], dblk[:, :], float(NB), sblk[:, :], ALU.mult, ALU.add).then_inc(keyed, 1)
                    for blk, oh in ((sblk, ohs), (dblk, ohd)):
                        v.tensor_tensor(oh[:, :, :], blk[:, :].unsqueeze(2).to_broadcast([P, EC, NB]),
                                        io25[:, :].unsqueeze(1).to_broadcast([P, EC, NB]), ALU.is_equal).then_inc(hot, 1)
                    dve.wait_ge(counted, 1)
                    v.tensor_copy(m4[:, :], pM[0:4 * NB, 0:4 * NB]).then_inc(m4ed, 1)
                    dve.wait_ge(summed, 1)
                    chain(v.tensor_copy(tot[:, :], pK[0:NB, 0:NB]))
                    chain(v.tensor_scalar(nch[:, :], tot[:, :], (L - 1) / 2.0, 1.0 / L, ALU.add, ALU.mult))
                    chain(v.tensor_scalar(nch[:, :], nch[:, :], MAGIC, None, ALU.add))
                    chain(v.tensor_scalar(nch[:, :], nch[:, :], -MAGIC, None, ALU.add))
                    chain(v.tensor_tensor_scan(inc[:, :], one25[:, :], nch[:, :], 0.0, ALU.mult, ALU.add))
                    chain(v.tensor_scalar(grp[:, :], inc[:, NB - 1:NB], (G - 1) / 2.0, 1.0 / G, ALU.add, ALU.mult))
                    chain(v.tensor_scalar(grp[:, :], grp[:, :], MAGIC, None, ALU.add))
                    chain(v.tensor_scalar(grp[:, :], grp[:, :], -MAGIC, None, ALU.add))
                    v.tensor_scalar(grp[:, :], grp[:, :], 1.0, None, ALU.max).then_inc(grouped, 1)
                    dve.wait_ge(prefixed, 1)
                    chain(v.tensor_copy(k["group_start"][0:1, 0:NB + 1], pK[0:1, 128:128 + NB + 1]))
                    chain(v.tensor_copy(g0[:, :], pK[0:NB, 256:257]))
                    chain(v.tensor_tensor(first[:, :], inc[:, :], nch[:, :], ALU.subtract))
                    chain(v.scalar_tensor_tensor(first[:, :], g0[:, :].to_broadcast([NB, NB]), float(G), first[:, :], ALU.mult, ALU.add))
                    chain(v.tensor_scalar(base[:, :], first[:, :], float(L), None, ALU.mult))
                    for q in range(NB):
                        chain(v.scalar_tensor_tensor(acc[:, :], ioc[:, :], first[:, q:q + 1], acc[:, :], ALU.is_ge, ALU.add))
                    dve.sem_inc(listed, 1)
                    dve.wait_ge(vdone, 1)
                    chain(v.tensor_copy(vrow[:, :], pK[0:P, 384:512]))
                    chain(v.tensor_copy(becol[:, :], pM[0:P, 256:257]))
                    for h in range(3):
                        w = NC // 3
                        dve.wait_ge(rowed, h + 1)
                        chain(v.tensor_copy(row[:, h * w:(h + 1) * w], pR[0:1, (h % 2) * 512:(h % 2) * 512 + w]))
                        dve.sem_inc(packed, 1)
                    chain(v.tensor_scalar(row[:, :], row[:, :], -1.0, None, ALU.add))
                    chain(v.tensor_scalar(rq[:, :], row[:, :], -float(NB // 2), 1.0 / NB, ALU.add, ALU.mult))
                    chain(v.tensor_scalar(rq[:, :], rq[:, :], MAGIC, None, ALU.add))
                    chain(v.tensor_scalar(rq[:, :], rq[:, :], -MAGIC, None, ALU.add))
                    chain(v.scalar_tensor_tensor(row[:, :], rq[:, :], -float(NB), row[:, :], ALU.mult, ALU.add))
                    chain(v.tensor_scalar(k["tile_at"][:, :], row[:, :], float(TS), None, ALU.mult))

                @block.scalar
                def _(act):
                    act.wait_ge(loaded, 7 * 16)
                    nc.scalar.copy(pay[:, :, WIN], win[:, :])
                    nc.scalar.copy(pay[:, :, WOUT], wout[:, :])
                    for t in range(2):
                        act.wait_ge(turned, t + 1)
                        nc.scalar.copy(keyt[:, t, :, :], pT[0:100, 8 * t:8 * t + 8, 0:P]).then_inc(copied, 1)

                @block.tensor
                def _(pe):
                    t_ = nc.tensor
                    pe.wait_ge(spread, 1)
                    for t in range(2):
                        t_.matmul(pK[0:P, 384:512], attnb[:, t, :], we_sb[:, t, :], start=(t == 0), stop=(t == 1))
                    for t in range(2):
                        ins = t_.matmul(pM[0:P, 256:257], attnb[:, t, :], bec[:, t:t + 1], start=(t == 0), stop=(t == 1))
                    ins.then_inc(vdone, 1)
                    pe.wait_ge(keyed, 1)
                    for t, what in enumerate((key, dblk)):
                        for q in range(8):
                            ins = t_.transpose(pT[0:100, 8 * t + q, 0:P], what[:, 100 * q:100 * q + 100], k["ident"][0:P, 0:P])
                        ins.then_inc(turned, 1)
                    pe.wait_ge(hot, 2)
                    t_.matmul(pM[0:4 * NB, 0:4 * NB], k["zeros_bf"][0:P, 0:4 * NB], k["zeros_bf"][0:P, 0:4 * NB],
                              start=True, stop=False, skip_group_check=True)
                    with pe.Fori(0, EC // 8) as i:
                        for j in range(2):
                            c = 8 * i + 4 * j
                            t_.matmul(pM[0:4 * NB, 0:4 * NB], ohd[:, ds(c, 4), :].rearrange("p a b -> p (a b)"),
                                      ohs[:, ds(c, 4), :].rearrange("p a b -> p (a b)"),
                                      start=False, stop=False, skip_group_check=True)
                    t_.matmul(pM[0:4 * NB, 0:4 * NB], k["zeros_bf"][0:P, 0:4 * NB], k["zeros_bf"][0:P, 0:4 * NB],
                              start=False, stop=True, skip_group_check=True).then_inc(counted, 1)
                    pe.wait_ge(m4ed, 1)
                    for j in range(4):
                        ins = t_.matmul(pK[0:NB, 0:NB], k["ident"][0:4 * NB, NB * j:NB * j + NB],
                                        m4[:, NB * j:NB * j + NB], start=(j == 0), stop=(j == 3))
                    ins.then_inc(summed, 1)
                    pe.wait_ge(grouped, 1)
                    t_.matmul(pK[0:1, 128:128 + NB + 1], grp[:, :], ptri[:, 0:NB + 1], start=True, stop=True)
                    t_.matmul(pK[0:NB, 256:257], ptri[:, 0:NB], grp[:, :], start=True, stop=True).then_inc(prefixed, 1)
                    pe.wait_ge(listed, 1)
                    for h in range(3):
                        w = NC // 3
                        if h == 2:
                            pe.wait_ge(packed, 1)
                        t_.matmul(pR[0:1, (h % 2) * 512:(h % 2) * 512 + w], k["ones"][0:NB, 0:1],
                                  acc[:, h * w:(h + 1) * w], start=True, stop=True).then_inc(rowed, 1)
            clear_semaphores(nc, a)

        with ExitStack() as inner:
            b = Scope(nc, inner, "put")
            C = k["columns"]
            rows = b.sb("rows", [P, 2, C * P])
            drow = b.sb("drow", [NB, 2, C * P])
            ohdT = b.sb("ohdT", [NB, 2, C * P])
            ohd, ohs = b.sb("ohd", [P, 2, C, NB], bf16), b.sb("ohs", [P, 2, C, NB], bf16)
            ea = b.sb("ea", [P, 2, C, DE])
            prod = b.sb("prod", [P, 2, C, DE])
            junk = b.sb("junk", [P, C, P], bf16)
            pre = b.sb("pre", [NB, 2, C, NB])
            rank = b.sb("rank", [P, 2, C])
            hit = b.sb("hit", [P, 2, C, NB])
            col = b.sb("col", [P, 2, C])
            pos = b.sb("pos", [P, 2, C])
            chk = b.sb("chk", [P, 2, C])
            index = b.sb("index", [P, 2, C], i32)
            stage = [b.sb(f"stage{h}", [P, C, F]) for h in range(2)]
            pK = b.ps("pK", [128, 512])
            pL = b.ps("pL", [128, 2, 512])
            loaded = b.steps("loaded", 2, 2, 16)
            hot = b.steps("hot", 2, 2)
            ranked = b.steps("ranked", 2, 2)
            looked = b.steps("looked", 2, 2)
            placed = b.steps("placed", 2, 2)
            staged = b.steps("staged", 2, 2)
            sent = k["sent"]
            counted, copied, cleared = b.sem("counted"), b.sem("copied"), b.sem("cleared")
            dve_chain, passed = b.sem("dve_chain"), b.sem("passed")
            slots = k["slots"].rearrange("l c f -> (l c) f")
            PER = 13
            with nc.Block() as block:

                @block.sync
                def _(sp):
                    keys_v = k["key_rows"].rearrange("(g c) p -> g (c p)", c=C)
                    dblk_v = k["dblk_rows"].rearrange("(g c) p -> g (c p)", c=C)
                    ea_v = edge_attr.rearrange("(p c) k -> p c k", p=P)
                    with sp.Fori(0, EC // C // 2) as i:
                        for h in range(2):
                            ranked.freed(sp, i, h)
                            hot.freed(sp, i, h)
                            g = 2 * i + h
                            sp.dma_start(rows[:, h, :], keys_v[ds(g, 1), :].to_broadcast([P, C * P])).then_inc(loaded.sem(h), 16)
                            sp.dma_start(drow[:, h, :], dblk_v[ds(g, 1), :].to_broadcast([NB, C * P])).then_inc(loaded.sem(h), 16)
                            sp.dma_start(ea[:, h, :, :], ea_v[:, ds(g * C, C), :]).then_inc(loaded.sem(h), 16)

                @block.vector
                def _(dve):
                    v = nc.vector
                    for h in range(2):
                        v.memset(stage[h][:, :, :], 0.0).then_inc(cleared, 1)
                    dve.wait_ge(cleared, 2)
                    with dve.Fori(0, EC // C // 2) as i:
                        for h in range(2):
                            g = 2 * i + h
                            chain = Chain(dve, dve_chain, g * PER)
                            dve.wait_ge(loaded.sem(h), 48 * i + 48)
                            looked.freed(dve, i, h)
                            v.tensor_scalar(ohdT[:, h, :], drow[:, h, :], iop[0:NB, :], None, ALU.is_equal)
                            v.tensor_tensor(ohd[:, h, :, :], dblk[:, ds(g * C, C)].unsqueeze(2).to_broadcast([P, C, NB]),
                                            io25[:, :].unsqueeze(1).to_broadcast([P, C, NB]), ALU.is_equal)
                            chain(v.tensor_tensor(ohs[:, h, :, :], sblk[:, ds(g * C, C)].unsqueeze(2).to_broadcast([P, C, NB]),
                                                  io25[:, :].unsqueeze(1).to_broadcast([P, C, NB]), ALU.is_equal))
                            dve.sem_inc(hot.sem(h), 1)
                            for j in range(C):
                                ins = v.scalar_tensor_tensor(junk[:, j, :], rows[:, h, j * P:(j + 1) * P], key[:, ds(g * C + j, 1)],
                                                             tri[:, :], ALU.is_equal, ALU.mult, accum_out=rank[:, h, j:j + 1])
                                chain(ins) if j == C - 1 else None
                            chain(v.tensor_tensor(prod[:, h, :, :], ea[:, h, :, :], vrow[:, :].unsqueeze(1).to_broadcast([P, C, DE]), ALU.mult))
                            chain(v.tensor_reduce(col[:, h, :], prod[:, h, :, :], AX.X, ALU.add))
                            dve.sem_inc(ranked.sem(h), 1)
                            sent.freed(dve, i, h)
                            chain(v.tensor_scalar(stage[h][:, :, EDGE], col[:, h, :], becol[:, :], None, ALU.add))
                            looked.after(dve, i, h)
                            chain(v.tensor_tensor(hit[:, h, :, :], pL[0:P, h, 0:C * NB].rearrange("p (c s) -> p c s", s=NB),
                                                  ohs[:, h, :, :], ALU.mult))
                            chain(v.tensor_reduce(pos[:, h, :], hit[:, h, :, :], AX.X, ALU.add))
                            chain(v.tensor_tensor(pos[:, h, :], pos[:, h, :], rank[:, h, :], ALU.add))
                            chain(v.tensor_scalar(chk[:, h, :], pos[:, h, :], -(L - 1) / 2.0, 1.0 / L, ALU.add, ALU.mult))
                            chain(v.tensor_scalar(chk[:, h, :], chk[:, h, :], MAGIC, None, ALU.add))
                            chain(v.tensor_scalar(chk[:, h, :], chk[:, h, :], -MAGIC, None, ALU.add))
                            chain(v.scalar_tensor_tensor(pos[:, h, :], chk[:, h, :], -float(L), pos[:, h, :], ALU.mult, ALU.add))
                            chain(v.scalar_tensor_tensor(index[:, h, :], pos[:, h, :], float(NC), chk[:, h, :], ALU.mult, ALU.add))
                            assert chain.n == PER, chain.n
                            dve.sem_inc(placed.sem(h), 1)

                @block.scalar
                def _(act):
                    act.wait_ge(cleared, 2)
                    with act.Fori(0, EC // C // 2) as i:
                        for h in range(2):
                            g = 2 * i + h
                            looked.freed(act, i, h)
                            for j in range(C):
                                act.wait_ge(counted, g * C + j + 1)
                                nc.scalar.copy(pre[:, h, j, :], pK[0:NB, 0:NB]).then_inc(copied, 1)
                            sent.freed(act, i, h)
                            nc.scalar.copy(stage[h][:, :, 0:4], pay[:, ds(g * C, C), :]).then_inc(staged.sem(h), 1)

                @block.tensor
                def _(pe):
                    t_ = nc.tensor
                    t_.matmul(pK[0:NB, 0:NB], k["ident"][0:NB, 0:NB], base[:, :], start=True, stop=False,
                              skip_group_check=True).then_inc(counted, 1)
                    with pe.Fori(0, EC // C // 2) as i:
                        for h in range(2):
                            g = 2 * i + h
                            hot.after(pe, i, h)
                            placed.freed(pe, i, h)
                            for j in range(C):
                                pe.wait_ge(copied, g * C + j + 1)
                                t_.matmul(pK[0:NB, 0:NB], ohd[:, h, j, :], ohs[:, h, j, :], start=False, stop=False,
                                          skip_group_check=True).then_inc(counted, 1)
                                ins = t_.matmul(pL[0:P, h, NB * j:NB * j + NB], ohdT[:, h, j * P:(j + 1) * P], pre[:, h, j, :],
                                                start=True, stop=True)
                            ins.then_inc(looked.sem(h), 1)

                @block.gpsimd
                def _(pool):
                    with pool.Fori(0, EC // C // 2) as i:
                        for h in range(2):
                            placed.after(pool, i, h)
                            staged.after(pool, i, h)
                            pool.sem_inc(passed, 1)
                            for j in range(C):
                                nc.gpsimd.indirect_dma_start(
                                    slots, bass.IndirectOffsetOnAxis(index[:, h, j:j + 1], 0),
                                    stage[h][:, j, :], None).then_inc(sent.sem(h), 16)
                    for h in range(2):
                        pool.wait_ge(sent.sem(h), 16 * C * (EC // C // 2))
            clear_semaphores(nc, b)


class Norm:

    CHAINED = 5

    def __init__(self, s):
        self.stats, self.mv = s.sb("stats", [P, 2, 6]), s.sb("mv", [P, 2, 2])
        self.ve, self.sd, self.rs = s.sb("ve", [P, 2]), s.sb("sd", [P, 2]), s.sb("rs", [P, 2])
        self.shifted = s.steps("shifted")
        self.rooted = s.steps("rooted")
        self.passed = s.sem("passed")

    def on_dve(self, nc, dve, chain, i, j, r, y):
        h, v = j % 2, nc.vector
        chain(v.bn_stats(self.stats[:, h, :], r))
        dve.sem_inc(self.passed, 1)
        chain(v.bn_aggr(self.mv[:, h, :], self.stats[:, h, :]))
        chain(v.tensor_scalar(self.ve[:, h:h + 1], self.mv[:, h, 1:2], EPS, None, ALU.add))
        dve.sem_inc(self.shifted.sem(j), 1)
        self.rooted.after(dve, i, j)
        chain(v.reciprocal(self.rs[:, h:h + 1], self.sd[:, h:h + 1]))
        chain(v.tensor_scalar(y, r, self.mv[:, h, 0:1], self.rs[:, h:h + 1], ALU.subtract, ALU.mult))

    def on_act(self, nc, act, i, j):
        h = j % 2
        self.shifted.after(act, i, j)
        nc.scalar.activation(self.sd[:, h:h + 1], self.ve[:, h:h + 1], ACT.Sqrt).then_inc(self.rooted.sem(j), 1)


def load_rows(sp, rows, sem):
    for tile, vector in rows:
        sp.dma_start(tile[:, :], vector.partition_broadcast(P)).then_inc(sem, 16)


def group_range(eng, k, d):
    g0 = eng.value_load(k["group_start"][0:1, ds(d, 1)], min_val=0, max_val=NG - 1)
    g1 = eng.value_load(k["group_start"][0:1, ds(d + 1, 1)], min_val=1, max_val=NG)
    return g0, g1


def word(k, c, f):
    return k["edges"][:, ds(c, 1), f:f + 1].rearrange("p a b -> p (a b)")


class Build:

    def __init__(self, s, name, dt):
        self.name = f"{s.tag}_{name}"
        self.left, self.right = s.sb(f"{name}_left", [L, G, P], dt), s.sb(f"{name}_right", [L, G, P], dt)
        self.hot = s.steps(f"{name}_hot", 2, 2)
        self.used = s.steps(f"{name}_used", 2, 2)

    def on_dve(self, nc, dve, k, g0, g1, iota, lf, rf, weight, before_group=None):
        with dve.Fori(g0, g1) as g:
            if before_group:
                before_group(g)
            for h in range(2):
                self.used.freed(dve, g, h)
                for j in (2 * h, 2 * h + 1):
                    c = g * G + j
                    nc.vector.tensor_scalar(self.left[:, j, :], iota[:, :], word(k, c, lf), None, ALU.is_equal)
                    w = weight(c)
                    if w is None:
                        ins = nc.vector.tensor_scalar(self.right[:, j, :], iota[:, :], word(k, c, rf), None, ALU.is_equal)
                    else:
                        ins = nc.vector.tensor_scalar(self.right[:, j, :], iota[:, :], word(k, c, rf), w,
                                                      ALU.is_equal, ALU.mult)
                ins.then_inc(self.hot.sem(h), 1)

    def on_pe(self, nc, pe, k, ps, g0, g1):
        t_ = nc.tensor
        for q in range(7):
            t_.matmul(ps[:, 512 * q:512 * q + 512], k["zeros_bf"][:, 0:128], k["zeros_bf"][:, :], start=True, stop=False,
                      skip_group_check=True)
        with pe.Fori(g0, g1) as g:
            with ExitStack() as regs:
                at_regs = [regs.enter_context(t_.register(f"{self.name}_at{n}")) for n in range(G)]
                t_.load(at_regs, k["tile_at"][0:1, ds(g * G, G)])
                for h in range(2):
                    self.hot.after(pe, g, h)
                    for j in (2 * h, 2 * h + 1):
                        at = t_.snap(at_regs[j], min_val=0, max_val=(NB - 1) * TS)
                        ins = t_.matmul(ps[0:P, ds(at, P)], self.left[:, j, :], self.right[:, j, :], start=False, stop=False,
                                        skip_group_check=True)
                    ins.then_inc(self.used.sem(h), 1)

    def complete(self, eng, g1):
        for h in range(2):
            self.used.freed(eng, g1, h)


def tiles_of(ps):
    return ps[0:P, 0:NB * TS].rearrange("p (s q) -> p s q", q=TS)


HALF = 12


def phase_adjacency(nc, k):
    ctx = ExitStack()
    with ctx:
        s = Scope(nc, ctx, "adj")
        T = s.sb("T", [P, NB, P])
        deg, root = s.sb("deg", [P, NB]), s.sb("root", [P, NB])
        ps = s.ps("ps", [128, 4096])
        build = Build(s, "b", bf16)
        loaded, moved, summed, read, stored, ended, rooted = (
            s.sem(n) for n in ("loaded", "moved", "summed", "read", "stored", "ended", "rooted"))
        with nc.Block() as block:

            @block.sync
            def _(sp):
                sp.dma_start(k["edges"][:, :, :], k["slots"]).then_inc(loaded, 16)
                with sp.Fori(0, NB) as d:
                    sp.wait_ge(moved, 2 * d + 2)
                    sp.dma_start(k["counts"][ds(d, 1)].rearrange("o p n -> (o p) n"),
                                 T[:, :, :].rearrange("p s q -> p (s q)")).then_inc(stored, 16)
                sp.wait_ge(stored, 16 * NB)

            @block.vector
            def _(dve):
                dve.wait_ge(loaded, 16)
                with dve.Fori(0, NB) as d:
                    g0, g1 = group_range(dve, k, d)
                    build.on_dve(nc, dve, k, g0, g1, k["iota_bf"], SRC, DST, lambda c: None)
                    build.complete(dve, g1)
                    dve.wait_ge(stored, 16 * d)
                    dve.wait_ge(summed, d)
                    nc.vector.tensor_copy(T[:, HALF:NB, :], tiles_of(ps)[:, HALF:NB, 0:P]).then_inc(moved, 1)
                    dve.wait_ge(summed, d + 1)
                    nc.vector.tensor_scalar(deg[:, ds(d, 1)], ps[0:P, 3584:3585], 1.0, None, ALU.add).then_inc(read, 1)
                dve.wait_ge(rooted, 1)
                nc.vector.reciprocal(k["dinv"][:, :], root[:, :]).then_inc(ended, 1)
                dve.wait_ge(ended, 1)

            @block.scalar
            def _(act):
                with act.Fori(0, NB) as d:
                    g0, g1 = group_range(act, k, d)
                    build.complete(act, g1)
                    act.wait_ge(stored, 16 * d)
                    act.wait_ge(summed, d)
                    nc.scalar.copy(T[:, 0:HALF, :], tiles_of(ps)[:, 0:HALF, 0:P]).then_inc(moved, 1)
                act.wait_ge(read, NB)
                nc.scalar.activation(root[:, :], deg[:, :], ACT.Sqrt).then_inc(rooted, 1)

            @block.tensor
            def _(pe):
                with pe.Fori(0, NB) as d:
                    g0, g1 = group_range(pe, k, d)
                    build.on_pe(nc, pe, k, ps, g0, g1)
                    pe.wait_ge(moved, 2 * d + 2)
                    pe.wait_ge(read, d)
                    for q in range(NB):
                        ins = nc.tensor.matmul(ps[0:P, 3584:3585], T[:, q, :], k["ones"][0:P, 0:1], start=(q == 0), stop=(q == NB - 1))
                    ins.then_inc(summed, 1)
        clear_semaphores(nc, s)


def phase_gemm(nc, k, tag, src, kc, weights, width, out, out_width, rows, chained, epilogue, prepare=None):
    ctx = ExitStack()
    i0 = 5 * k["gemm_turn"]
    k["gemm_turn"] += 1
    st = k["gemm_steps"]
    with ctx:
        s = Scope(nc, ctx, tag)
        x = s.sb("x", [P, 2, kc * 128])
        xt = s.sb("xt", [128, 2, kc, P])
        w = s.sb("w", [128, kc, width])
        y = s.sb("y", [P, 2, out_width])
        tiles = {name: s.sb(name, [P, vec.shape[-1]]) for name, vec in rows.items()}
        pt = s.ps("pt", [128, 2, 512])
        po = s.ps("po", [128, 2, 512])
        ready, chain_sem, prepared = s.sem("ready"), s.sem("chain"), s.sem("prepared")
        n_ready = 16 * (len(weights) + len(rows))
        with nc.Block() as block:

            @block.sync
            def _(sp):
                for wd, c0, n in weights:
                    sp.dma_start(w[:, :, c0:c0 + n], wd.rearrange("(t c) n -> c t n", c=128)).then_inc(ready, 16)
                load_rows(sp, [(tiles[name], vec) for name, vec in rows.items()], ready)
                with sp.Fori(0, 5) as i:
                    for j in range(5):
                        st["turned"].freed(sp, i + i0, j)
                        sp.dma_start(x[:, j % 2, :], src[ds(5 * i + j, 1)].rearrange("o p n -> (o p) n")).then_inc(st["loaded"].sem(j), 16)

            @block.gpsimd
            def _(pool):
                with pool.Fori(0, 5) as i:
                    for j in range(5):
                        st["finished"].after(pool, i + i0, j)
                        pool.dma_start(out[ds(5 * i + j, 1)].rearrange("o p n -> (o p) n"), y[:, j % 2, :]).then_inc(st["stored"].sem(j), 16)
                for j in range(2):
                    st["stored"].freed(pool, i0 + 5, j)

            @block.scalar
            def _(act):
                with act.Fori(0, 5) as i:
                    for j in range(5):
                        st["turned"].after(act, i + i0, j)
                        st["multiplied"].freed(act, i + i0, j)
                        nc.scalar.copy(xt[:, j % 2, :, :], pt[:, j % 2, 0:kc * 128].rearrange("p (t q) -> p t q", q=128)[:, :, 0:P]
                                       ).then_inc(st["copied"].sem(j), 1)

            @block.tensor
            def _(pe):
                t_ = nc.tensor

                def turn(i, j):
                    st["loaded"].after(pe, i + i0, j)
                    st["copied"].freed(pe, i + i0, j)
                    for t in range(kc):
                        ins = t_.transpose(pt[:, j % 2, 128 * t:128 * t + P], x[:, j % 2, 128 * t:128 * t + 128], k["ident"][0:P, 0:P])
                    ins.then_inc(st["turned"].sem(j), 1)

                def multiply(i, j):
                    st["copied"].after(pe, i + i0, j)
                    st["finished"].freed(pe, i + i0, j)
                    for t in range(kc):
                        ins = t_.matmul(po[0:P, j % 2, 0:width], xt[:, j % 2, t, :], w[:, t, :], start=(t == 0), stop=(t == kc - 1))
                    ins.then_inc(st["multiplied"].sem(j), 1)

                pe.wait_ge(ready, n_ready)
                with pe.Fori(0, 5) as i:
                    turn(i, 0)
                    for j in range(5):
                        if j < 4:
                            turn(i, j + 1)
                        multiply(i, j)

            @block.vector
            def _(dve):
                dve.wait_ge(ready, n_ready)
                if prepare:
                    prepare(dve, y, prepared)
                with dve.Fori(0, 5) as i:
                    for j in range(5):
                        b = 5 * i + j
                        chain = Chain(dve, chain_sem, b * chained)
                        st["multiplied"].after(dve, i + i0, j)
                        st["stored"].freed(dve, i + i0, j)
                        epilogue(dve, chain, b, po[0:P, j % 2, :], y[:, j % 2, :], tiles)
                        assert chain.n == chained, (tag, chain.n)
                        dve.sem_inc(st["finished"].sem(j), 1)
        clear_semaphores(nc, s)


def phase_apply(nc, k, tag, table, width, out, rows, chained, epilogue, resid=None, norm=False):
    ctx = ExitStack()
    i0 = 5 * k["apply_turn"]
    k["apply_turn"] += 1
    st = k["apply_steps"]
    with ctx:
        s = Scope(nc, ctx, tag)
        H = s.sb("H", [P, NB, width])
        T = [s.sb(f"T{h}", [P, NB, P]) for h in range(2)]
        X = s.sb("X", [P, NB, D]) if resid is not None else None
        y = s.sb("y", [P, 2, width])
        tmp = s.sb("tmp", [P, 2, width])
        tiles = {name: s.sb(name, [P, vec.shape[-1]]) for name, vec in rows.items()}
        po = s.ps("po", [128, 2, 512])
        nm = Norm(s) if norm else None
        ready, chain_sem = s.sem("ready"), s.sem("chain")
        n_ready = 16 * (1 + len(rows) + (resid is not None))
        with nc.Block() as block:

            @block.sync
            def _(sp):
                sp.dma_start(H[:, :, :], table.rearrange("b p n -> p b n")).then_inc(ready, 16)
                if resid is not None:
                    sp.dma_start(X[:, :, :], resid.rearrange("b p n -> p b n")).then_inc(ready, 16)
                load_rows(sp, [(tiles[name], vec) for name, vec in rows.items()], ready)
                with sp.Fori(0, 5) as i:
                    for j in range(5):
                        st["summed"].freed(sp, i + i0, j)
                        sp.dma_start(T[j % 2][:, :, :].rearrange("p s q -> p (s q)"),
                                     k["counts"][ds(5 * i + j, 1)].rearrange("o p n -> (o p) n")).then_inc(st["loaded"].sem(j), 16)

            @block.gpsimd
            def _(pool):
                with pool.Fori(0, 5) as i:
                    for j in range(5):
                        st["finished"].after(pool, i + i0, j)
                        pool.dma_start(out[ds(5 * i + j, 1)].rearrange("o p n -> (o p) n"), y[:, j % 2, :]).then_inc(st["stored"].sem(j), 16)
                for j in range(2):
                    st["stored"].freed(pool, i0 + 5, j)

            @block.tensor
            def _(pe):
                pe.wait_ge(ready, n_ready)
                with pe.Fori(0, 5) as i:
                    for j in range(5):
                        st["loaded"].after(pe, i + i0, j)
                        st["finished"].freed(pe, i + i0, j)
                        for q in range(NB):
                            ins = nc.tensor.matmul(po[0:P, j % 2, 0:width], T[j % 2][:, q, :], H[:, q, :],
                                                   start=(q == 0), stop=(q == NB - 1))
                        ins.then_inc(st["summed"].sem(j), 1)

            if norm:
                @block.scalar
                def _(act):
                    with act.Fori(0, 5) as i:
                        for j in range(5):
                            nm.on_act(nc, act, i, j)

            @block.vector
            def _(dve):
                dve.wait_ge(ready, n_ready)
                with dve.Fori(0, 5) as i:
                    for j in range(5):
                        b = 5 * i + j
                        chain = Chain(dve, chain_sem, b * chained)
                        st["summed"].after(dve, i + i0, j)
                        st["stored"].freed(dve, i + i0, j)
                        at = (lambda A: A[:, ds(b, 1), :].rearrange("p a n -> p (a n)"))
                        t = tmp[:, j % 2, :]
                        chain(nc.vector.tensor_tensor(t, po[0:P, j % 2, 0:width], at(H), ALU.add))
                        epilogue(dve, chain, i, j, b, t, y[:, j % 2, :], tiles, at(X) if X is not None else None, nm)
                        assert chain.n == chained, (tag, chain.n)
                        dve.sem_inc(st["finished"].sem(j), 1)
        clear_semaphores(nc, s)


def phase_attention(nc, k, x1, x2):
    ctx = ExitStack()
    with ctx:
        s = Scope(nc, ctx, "att")
        H = s.sb("H", [P, NB, D + 1])
        T = s.sb("T", [P, NB, P])
        hst = s.sb("hst", [NB, P])
        hsb = s.sb("hsb", [L, NB, TS])
        X = s.sb("X", [P, 1, D])
        y, r = s.sb("y", [P, D]), s.sb("r", [P, D])
        junk = s.sb("junk", [L, G, P], bf16)
        junk2 = s.sb("junk2", [L, G, P], bf16)
        z4, m4 = s.sb("z4", [L, G]), s.sb("m4", [L, G])
        logit = s.sb("logit", [L, NC])
        shifted = s.sb("shifted", [L, NC])
        prob = s.sb("prob", [L, NC])
        far = s.sb("far", [L, G, P])
        top4, top = s.sb("top4", [L, G, P]), s.sb("top", [L, P])
        mcol, mdiag, mrow = s.sb("mcol", [P, 1]), s.sb("mdiag", [P, P]), s.sb("mrow", [L, P])
        ones = s.sb("ones", [P, L])
        den = s.sb("den", [P, 1])
        ps = s.ps("ps", [128, 4096])
        build = Build(s, "b", fp32)
        stats, mv, ve, sd, rs = (s.sb(n, [P, w]) for n, w in (("stats", 6), ("mv", 2), ("ve", 1), ("sd", 1), ("rs", 1)))
        ready, hs_turned, hs_copied, hs_out, hs_in = (s.sem(n) for n in ("ready", "hs_turned", "hs_copied", "hs_out", "hs_in"))
        chain_a, chain_b, chain_d, minus, passed, cleared = (
            s.sem(n) for n in ("chain_a", "chain_b", "chain_d", "minus", "passed", "cleared"))
        exped, topped, turned, diagonal, spread, moved, summed = (
            s.sem(n) for n in ("exped", "topped", "turned", "diagonal", "spread", "moved", "summed"))
        xin, varied, rooted, finished, stored = (s.sem(n) for n in ("xin", "varied", "rooted", "finished", "stored"))
        DC = 14
        with nc.Block() as block:

            @block.sync
            def _(sp):
                sp.dma_start(H[:, :, :], k["table"][:, :, 0:D + 1].rearrange("b p n -> p b n")).then_inc(ready, 16)
                sp.wait_ge(hs_copied, 1)
                sp.dma_start(k["hs_row"], hst[:, :]).then_inc(hs_out, 16)
                sp.wait_ge(hs_out, 16)
                sp.dma_start(hsb[:, :, 0:P], k["hs_row"].partition_broadcast(L)).then_inc(hs_in, 16)
                with sp.Fori(0, NB) as d:
                    sp.wait_ge(finished, d)
                    sp.dma_start(X[:, :, :], x1[ds(d, 1)].rearrange("o p n -> p o n")).then_inc(xin, 16)
                    sp.wait_ge(finished, d + 1)
                    sp.dma_start(x2[ds(d, 1)].rearrange("o p n -> (o p) n"), y[:, :]).then_inc(stored, 16)
                sp.wait_ge(stored, 16 * NB)

            @block.scalar
            def _(act):
                act.wait_ge(hs_turned, 1)
                nc.scalar.copy(hst[:, :], ps[0:NB, 0:P]).then_inc(hs_copied, 1)
                with act.Fori(0, NB) as d:
                    g0, g1 = group_range(act, k, d)
                    with act.Fori(g0, g1) as g:
                        act.wait_ge(minus, g + 1)
                        nc.scalar.activation(prob[:, ds(g * G, G)], shifted[:, ds(g * G, G)], ACT.Exp).then_inc(exped, 1)
                    build.complete(act, g1)
                    act.wait_ge(summed, d)
                    nc.scalar.copy(T[:, 0:HALF, :], tiles_of(ps)[:, 0:HALF, 0:P]).then_inc(moved, 1)
                    act.wait_ge(varied, d + 1)
                    nc.scalar.activation(sd[:, :], ve[:, :], ACT.Sqrt).then_inc(rooted, 1)

            @block.tensor
            def _(pe):
                t_ = nc.tensor
                t_.transpose(ps[0:NB, 0:P], k["hs"][:, :], k["ident"][0:P, 0:P]).then_inc(hs_turned, 1)
                pe.wait_ge(ready, 16)
                pe.wait_ge(hs_copied, 1)
                with pe.Fori(0, NB) as d:
                    g0, g1 = group_range(pe, k, d)
                    pe.wait_ge(topped, d + 1)
                    pe.wait_ge(finished, d)
                    t_.transpose(ps[0:P, 3584:3712], top[:, :], k["ident"][:, :]).then_inc(turned, 1)
                    pe.wait_ge(diagonal, d + 1)
                    t_.matmul(ps[0:L, 3712:3712 + P], ones[:, :], mdiag[:, :], start=True, stop=True).then_inc(spread, 1)
                    build.on_pe(nc, pe, k, ps, g0, g1)
                    pe.wait_ge(moved, 2 * d + 2)
                    for q in range(NB):
                        ins = t_.matmul(ps[0:P, 3584:3584 + D + 1], T[:, q, :], H[:, q, :], start=(q == 0), stop=(q == NB - 1))
                    ins.then_inc(summed, 1)

            @block.vector
            def _(dve):
                v = nc.vector
                v.memset(ones[:, :], 1.0).then_inc(cleared, 1)
                dve.wait_ge(cleared, 1)
                dve.wait_ge(hs_in, 16)
                hsf = hsb[:, :, :].rearrange("p b q -> p (b q)")
                with dve.Fori(0, NB) as d:
                    g0, g1 = group_range(dve, k, d)
                    chain = Chain(dve, chain_d, d * DC)
                    chain(v.memset(top4[:, :, :], -BIG))
                    dve.sem_inc(passed, 1)
                    with dve.Fori(g0, g1) as g:
                        c1 = Chain(dve, chain_a, g * 5)
                        with ExitStack() as regs:
                            at_regs = [regs.enter_context(v.register(f"logit_at{n}")) for n in range(G)]
                            v.load(at_regs, k["tile_at"][0:1, ds(g * G, G)])
                            for j in range(G):
                                at = v.snap(at_regs[j], min_val=0, max_val=(NB - 1) * TS)
                                ins = v.scalar_tensor_tensor(junk[:, j, :], k["iota"][:, :], word(k, g * G + j, SRC), hsf[:, ds(at, P)],
                                                             ALU.is_equal, ALU.mult, accum_out=z4[:, j:j + 1])
                            c1(ins)
                        c1(v.tensor_tensor(z4[:, :], z4[:, :], k["edges"][:, ds(g * G, G), EDGE], ALU.add))
                        c1(v.scalar_tensor_tensor(logit[:, ds(g * G, G)], z4[:, :], 0.01, z4[:, :], ALU.mult, ALU.max))
                        for j in range(G):
                            ins = v.tensor_scalar(far[:, j, :], k["iota"][:, :], word(k, g * G + j, DST), -BIG, ALU.not_equal, ALU.mult)
                        c1(ins)
                        for j in range(G):
                            ins = v.scalar_tensor_tensor(top4[:, j, :], far[:, j, :], logit[:, ds(g * G + j, 1)], top4[:, j, :],
                                                         ALU.add, ALU.max)
                        c1(ins)
                    chain(v.tensor_reduce(top[:, :], top4[:, :, :].rearrange("p j q -> p q j"), AX.X, ALU.max))
                    dve.sem_inc(topped, 1)
                    dve.wait_ge(turned, d + 1)
                    chain(v.tensor_reduce(mcol[:, :], ps[0:P, 3584:3712], AX.X, ALU.max))
                    chain(v.tensor_scalar(mdiag[:, :], k["ident"][0:P, 0:P], mcol[:, :], None, ALU.mult))
                    dve.sem_inc(diagonal, 1)
                    dve.wait_ge(spread, d + 1)
                    chain(v.tensor_copy(mrow[:, :], ps[0:L, 3712:3712 + P]))
                    dve.sem_inc(passed, 1)
                    with dve.Fori(g0, g1) as g:
                        c2 = Chain(dve, chain_b, g * 2)
                        for j in range(G):
                            ins = v.scalar_tensor_tensor(junk2[:, j, :], k["iota"][:, :], word(k, g * G + j, DST), mrow[:, :],
                                                         ALU.is_equal, ALU.mult, accum_out=m4[:, j:j + 1])
                        c2(ins)
                        c2(v.tensor_tensor(shifted[:, ds(g * G, G)], logit[:, ds(g * G, G)], m4[:, :], ALU.subtract))
                        dve.sem_inc(minus, 1)
                    build.on_dve(nc, dve, k, g0, g1, k["iota"], SRC, DST, lambda c: prob[:, ds(c, 1)],
                                 before_group=lambda g: dve.wait_ge(exped, g + 1))
                    build.complete(dve, g1)
                    dve.wait_ge(summed, d)
                    v.tensor_copy(T[:, HALF:NB, :], tiles_of(ps)[:, HALF:NB, 0:P]).then_inc(moved, 1)
                    dve.wait_ge(summed, d + 1)
                    chain(v.tensor_scalar(den[:, :], ps[0:P, 3584 + D:3585 + D], 1e-16, None, ALU.add))
                    chain(v.reciprocal(den[:, :], den[:, :]))
                    chain(v.tensor_scalar(r[:, :], ps[0:P, 3584:3584 + D], den[:, :], 0.0, ALU.mult, ALU.max))
                    dve.wait_ge(xin, 16 * d + 16)
                    chain(v.tensor_tensor(r[:, :], r[:, :], X[:, 0, :], ALU.add))
                    chain(v.bn_stats(stats[:, :], r[:, :]))
                    dve.sem_inc(passed, 1)
                    chain(v.bn_aggr(mv[:, :], stats[:, :]))
                    chain(v.tensor_scalar(ve[:, :], mv[:, 1:2], EPS, None, ALU.add))
                    dve.sem_inc(varied, 1)
                    dve.wait_ge(rooted, d + 1)
                    chain(v.reciprocal(rs[:, :], sd[:, :]))
                    dve.wait_ge(stored, 16 * d)
                    chain(v.tensor_scalar(y[:, :], r[:, :], mv[:, 0:1], rs[:, :], ALU.subtract, ALU.mult))
                    assert chain.n == DC, chain.n
                    dve.sem_inc(finished, 1)
        clear_semaphores(nc, s)


def phase_batch_norm(nc, k, x2, gamma, beta):
    ctx = ExitStack()
    with ctx:
        s = Scope(nc, ctx, "bn")
        X, Q = s.sb("X", [P, NB, D]), s.sb("Q", [P, NB, D])
        mean, scale, root = s.sb("mean", [P, D]), s.sb("scale", [P, D]), s.sb("root", [P, D])
        gm, bt = s.sb("gm", [P, D]), s.sb("bt", [P, D])
        pm, pv = s.ps("pm", [P, D]), s.ps("pv", [P, D])
        loaded, meaned, centred, squared, varied, shifted, rooted, chain_sem, done, stored = (
            s.sem(n) for n in ("loaded", "meaned", "centred", "squared", "varied", "shifted", "rooted", "chain", "done", "stored"))
        with nc.Block() as block:

            @block.sync
            def _(sp):
                sp.dma_start(X[:, :, :], x2.rearrange("b p n -> p b n")).then_inc(loaded, 16)
                load_rows(sp, [(gm, gamma), (bt, beta)], loaded)
                sp.wait_ge(done, 1)
                sp.dma_start(k["cat"][:, :, 2 * D:3 * D].rearrange("b p n -> p b n"), Q[:, :, :]).then_inc(stored, 16)
                sp.wait_ge(stored, 16)

            @block.tensor
            def _(pe):
                pe.wait_ge(loaded, 48)
                for q in range(NB):
                    ins = nc.tensor.matmul(pm[:, :], k["ones"][0:P, :], X[:, q, :], start=(q == 0), stop=(q == NB - 1))
                ins.then_inc(meaned, 1)
                pe.wait_ge(squared, 1)
                for q in range(NB):
                    ins = nc.tensor.matmul(pv[:, :], k["ones"][0:P, :], Q[:, q, :], start=(q == 0), stop=(q == NB - 1))
                ins.then_inc(varied, 1)

            @block.scalar
            def _(act):
                act.wait_ge(centred, 1)
                nc.scalar.activation(Q[:, :, :], X[:, :, :], ACT.Square).then_inc(squared, 1)
                act.wait_ge(shifted, 1)
                nc.scalar.activation(root[:, :], scale[:, :], ACT.Sqrt).then_inc(rooted, 1)

            @block.vector
            def _(dve):
                v = nc.vector
                chain = Chain(dve, chain_sem)
                wide = (lambda t: t[:, :].unsqueeze(1).to_broadcast([P, NB, D]))
                dve.wait_ge(loaded, 48)
                dve.wait_ge(meaned, 1)
                chain(v.tensor_scalar(mean[:, :], pm[:, :], 1.0 / N, None, ALU.mult))
                v.tensor_tensor(X[:, :, :], X[:, :, :], wide(mean), ALU.subtract).then_inc(centred, 1)
                dve.wait_ge(varied, 1)
                v.tensor_scalar(scale[:, :], pv[:, :], 1.0 / N, EPS, ALU.mult, ALU.add).then_inc(shifted, 1)
                dve.wait_ge(rooted, 1)
                chain(v.reciprocal(scale[:, :], root[:, :]))
                chain(v.tensor_tensor(scale[:, :], scale[:, :], gm[:, :], ALU.mult))
                chain(v.tensor_tensor(Q[:, :, :], X[:, :, :], wide(scale), ALU.mult))
                v.tensor_tensor(Q[:, :, :], Q[:, :, :], wide(bt), ALU.add).then_inc(done, 1)
        clear_semaphores(nc, s)


def phase_gated(nc, k, table):
    ctx = ExitStack()
    with ctx:
        s = Scope(nc, ctx, "gat")
        FI, FO = s.sb("FI", [P, NB, D]), s.sb("FO", [P, NB, D])
        out = s.sb("out", [P, NB, D])
        ain = s.sb("ain", [P, D])
        T = s.sb("T", [P, NB, P])
        ps = s.ps("ps", [128, 4096])
        b_in, b_out = Build(s, "i", fp32), Build(s, "o", fp32)
        loaded, cleared, moved_i, moved_o, summed_i, read_i, stored = (
            s.sem(n) for n in ("loaded", "cleared", "moved_i", "moved_o", "summed_i", "read_i", "stored"))
        multiplied = s.steps("multiplied", 2, NB)
        added = s.steps("added", 2, NB)
        at = (lambda A, d: A[:, ds(d, 1), :].rearrange("p a n -> p (a n)"))
        slot = (lambda h: ps[0:P, 3584 - 512 * (h % 2):3840 - 512 * (h % 2)])
        with nc.Block() as block:

            @block.sync
            def _(sp):
                sp.dma_start(FI[:, :, :], table[:, :, 0:D].rearrange("b p n -> p b n")).then_inc(loaded, 16)
                sp.dma_start(FO[:, :, :], table[:, :, D:2 * D].rearrange("b p n -> p b n")).then_inc(loaded, 16)
                with sp.Fori(0, NB) as d:
                    sp.wait_ge(read_i, d + 1)
                    sp.dma_start(k["cat"][ds(d, 1), :, 0:D].rearrange("o p n -> (o p) n"), ain[:, :]).then_inc(stored, 16)
                for h in range(2):
                    added.freed(sp, NB, h)
                sp.dma_start(k["cat"][:, :, D:2 * D].rearrange("b p n -> p b n"), out[:, :, :]).then_inc(stored, 16)
                sp.wait_ge(stored, 16 * NB + 16)

            @block.tensor
            def _(pe):
                t_ = nc.tensor
                pe.wait_ge(loaded, 32)
                with pe.Fori(0, NB) as d:
                    g0, g1 = group_range(pe, k, d)
                    for h in range(2):
                        added.freed(pe, d, h)
                    b_in.on_pe(nc, pe, k, ps, g0, g1)
                    pe.wait_ge(moved_i, 2 * d + 2)
                    for q in range(NB):
                        ins = t_.matmul(slot(0), T[:, q, :], FI[:, q, :], start=(q == 0), stop=(q == NB - 1))
                    ins.then_inc(summed_i, 1)
                    b_out.on_pe(nc, pe, k, ps, g0, g1)
                    pe.wait_ge(moved_o, 2 * d + 2)
                    pe.wait_ge(read_i, d + 1)
                    for q in range(NB):
                        added.freed(pe, d, q)
                        t_.matmul(slot(q), T[:, q, :], at(FO, d), start=True, stop=True).then_inc(multiplied.sem(q), 1)

            @block.scalar
            def _(act):
                with act.Fori(0, NB) as d:
                    g0, g1 = group_range(act, k, d)
                    b_in.complete(act, g1)
                    for h in range(2):
                        multiplied.freed(act, d, h)
                    nc.scalar.copy(T[:, 0:HALF, :], tiles_of(ps)[:, 0:HALF, 0:P]).then_inc(moved_i, 1)
                    act.wait_ge(summed_i, d + 1)
                    b_out.complete(act, g1)
                    nc.scalar.copy(T[:, 0:HALF, :], tiles_of(ps)[:, 0:HALF, 0:P]).then_inc(moved_o, 1)

            @block.vector
            def _(dve):
                v = nc.vector
                v.memset(out[:, :, :], 0.0).then_inc(cleared, 1)
                dve.wait_ge(cleared, 1)
                with dve.Fori(0, NB) as d:
                    g0, g1 = group_range(dve, k, d)
                    b_in.on_dve(nc, dve, k, g0, g1, k["iota"], SRC, DST, lambda c: word(k, c, WIN))
                    b_in.complete(dve, g1)
                    for h in range(2):
                        multiplied.freed(dve, d, h)
                    v.tensor_copy(T[:, HALF:NB, :], tiles_of(ps)[:, HALF:NB, 0:P]).then_inc(moved_i, 1)
                    b_out.on_dve(nc, dve, k, g0, g1, k["iota"], DST, SRC, lambda c: word(k, c, WOUT))
                    dve.wait_ge(summed_i, d + 1)
                    dve.wait_ge(stored, 16 * d)
                    v.tensor_copy(ain[:, :], slot(0)).then_inc(read_i, 1)
                    b_out.complete(dve, g1)
                    v.tensor_copy(T[:, HALF:NB, :], tiles_of(ps)[:, HALF:NB, 0:P]).then_inc(moved_o, 1)
                    for h in range(2):
                        added.freed(dve, d, h)
                    for q in range(NB):
                        multiplied.after(dve, d, q)
                        v.tensor_tensor(out[:, q, :], out[:, q, :], slot(q), ALU.add).then_inc(added.sem(q), 1)
        clear_semaphores(nc, s)


def phase_gates(nc, k, x2, w_x2i, b_x2i, w_h2h, x3):
    ctx = ExitStack()
    KC = 3 * D // 128
    with ctx:
        s = Scope(nc, ctx, "upd")
        x = s.sb("x", [P, 2, 3 * D])
        xt = s.sb("xt", [128, 2, KC, P])
        w = s.sb("w", [128, KC, 2 * D])
        X, Hn = s.sb("X", [P, NB, D]), s.sb("Hn", [P, NB, D])
        bias = s.sb("bias", [P, 2 * D])
        pre, gate = s.sb("pre", [P, 2, 2 * D]), s.sb("gate", [P, 2, 2 * D])
        r, y = s.sb("r", [P, 2, D]), s.sb("y", [P, 2, D])
        pt, po = s.ps("pt", [128, 2, 1024]), s.ps("po", [128, 2, 512])
        nm = Norm(s)
        ready, chain_sem = s.sem("ready"), s.sem("chain")
        i0 = 5 * k["gemm_turn"]
        k["gemm_turn"] += 1
        loaded, turned, copied, multiplied, finished, stored = (
            k["gemm_steps"][n].from_turn(i0) for n in ("loaded", "turned", "copied", "multiplied", "finished", "stored"))
        biased, gated = s.steps("biased"), s.steps("gated")
        PER = 5 + Norm.CHAINED
        with nc.Block() as block:

            @block.sync
            def _(sp):
                sp.dma_start(w[:, 0:4, :], w_x2i.rearrange("(t c) n -> c t n", c=128)).then_inc(ready, 16)
                sp.dma_start(w[:, 4:6, :], w_h2h.rearrange("(t c) n -> c t n", c=128)).then_inc(ready, 16)
                load_rows(sp, [(bias, b_x2i)], ready)
                sp.dma_start(X[:, :, :], x2.rearrange("b p n -> p b n")).then_inc(ready, 16)
                sp.dma_start(Hn[:, :, :], k["cat"][:, :, 2 * D:3 * D].rearrange("b p n -> p b n")).then_inc(ready, 16)
                with sp.Fori(0, 5) as i:
                    for j in range(5):
                        turned.freed(sp, i, j)
                        sp.dma_start(x[:, j % 2, :], k["cat"][ds(5 * i + j, 1)].rearrange("o p n -> (o p) n")).then_inc(loaded.sem(j), 16)

            @block.gpsimd
            def _(pool):
                with pool.Fori(0, 5) as i:
                    for j in range(5):
                        finished.after(pool, i, j)
                        pool.dma_start(x3[ds(5 * i + j, 1)].rearrange("o p n -> (o p) n"), y[:, j % 2, :]).then_inc(stored.sem(j), 16)
                for j in range(2):
                    stored.freed(pool, 5, j)

            @block.tensor
            def _(pe):
                t_ = nc.tensor

                def turn(i, j):
                    loaded.after(pe, i, j)
                    copied.freed(pe, i, j)
                    for t in range(KC):
                        ins = t_.transpose(pt[:, j % 2, 128 * t:128 * t + P], x[:, j % 2, 128 * t:128 * t + 128], k["ident"][0:P, 0:P])
                    ins.then_inc(turned.sem(j), 1)

                pe.wait_ge(ready, 80)
                with pe.Fori(0, 5) as i:
                    turn(i, 0)
                    for j in range(5):
                        if j < 4:
                            turn(i, j + 1)
                        copied.after(pe, i, j)
                        biased.freed(pe, i, j)
                        for t in range(KC):
                            ins = t_.matmul(po[0:P, j % 2, :], xt[:, j % 2, t, :], w[:, t, :], start=(t == 0), stop=(t == KC - 1))
                        ins.then_inc(multiplied.sem(j), 1)

            @block.scalar
            def _(act):
                def copy(i, j):
                    turned.after(act, i, j)
                    multiplied.freed(act, i, j)
                    nc.scalar.copy(xt[:, j % 2, :, :], pt[:, j % 2, 0:KC * 128].rearrange("p (t q) -> p t q", q=128)[:, :, 0:P]
                                   ).then_inc(copied.sem(j), 1)

                with act.Fori(0, 5) as i:
                    copy(i, 0)
                    for j in range(5):
                        if j < 4:
                            copy(i, j + 1)
                        biased.after(act, i, j)
                        finished.freed(act, i, j)
                        nc.scalar.activation(gate[:, j % 2, 0:D], pre[:, j % 2, 0:D], ACT.Sigmoid)
                        nc.scalar.activation(gate[:, j % 2, D:2 * D], pre[:, j % 2, D:2 * D], ACT.Tanh).then_inc(gated.sem(j), 1)
                        nm.on_act(nc, act, i, j)

            @block.vector
            def _(dve):
                v = nc.vector
                dve.wait_ge(ready, 80)
                with dve.Fori(0, 5) as i:
                    for j in range(5):
                        b, h = 5 * i + j, j % 2
                        chain = Chain(dve, chain_sem, b * PER)
                        at = (lambda A: A[:, ds(b, 1), :].rearrange("p a n -> p (a n)"))
                        multiplied.after(dve, i, j)
                        gated.freed(dve, i, j)
                        chain(v.tensor_tensor(pre[:, h, :], po[0:P, h, :], bias[:, :], ALU.add))
                        dve.sem_inc(biased.sem(j), 1)
                        gated.after(dve, i, j)
                        new = gate[:, h, D:2 * D]
                        chain(v.tensor_tensor(r[:, h, :], at(Hn), new, ALU.subtract))
                        chain(v.tensor_tensor(r[:, h, :], r[:, h, :], gate[:, h, 0:D], ALU.mult))
                        chain(v.tensor_tensor(r[:, h, :], r[:, h, :], new, ALU.add))
                        chain(v.tensor_tensor(r[:, h, :], r[:, h, :], at(X), ALU.add))
                        stored.freed(dve, i, j)
                        nm.on_dve(nc, dve, chain, i, j, r[:, h, :], y[:, h, :])
                        assert chain.n == PER
                        dve.sem_inc(finished.sem(j), 1)
        clear_semaphores(nc, s)


def phase_decoder(nc, k, h3, w_lin, b_lin, w_dec1, b_dec1, w_dec2, b_dec2, x3, out):
    ctx = ExitStack()
    HID0, HID1 = w_lin.shape
    with ctx:
        s = Scope(nc, ctx, "dec")
        x = s.sb("x", [P, 2, HID0])
        ht, zt, dt = s.sb("ht", [HID0, 2, P]), s.sb("zt", [HID1, 2, P]), s.sb("dt", [HID0, 2, P])
        wl, w1, w2 = s.sb("wl", [HID0, HID1]), s.sb("w1", [HID1, HID0]), s.sb("w2", [HID0, D])
        bl, b1, b2 = s.sb("bl", [HID1, 1]), s.sb("b1", [HID0, 1]), s.sb("b2", [P, D])
        X = s.sb("X", [P, NB, D])
        r, y = s.sb("r", [P, 2, D]), s.sb("y", [P, 2, D])
        pt, pz, pd, po = (s.ps(n, [128, 2, 512]) for n in ("pt", "pz", "pd", "po"))
        nm = Norm(s)
        ready, chain_sem = s.sem("ready"), s.sem("chain")
        i0 = 5 * k["gemm_turn"]
        k["gemm_turn"] += 1
        loaded, turned, copied, multiplied, finished, stored = (
            k["gemm_steps"][n].from_turn(i0) for n in ("loaded", "turned", "copied", "multiplied", "finished", "stored"))
        lined, z_ready, decoded, d_ready = (s.steps(n) for n in ("lined", "z_ready", "decoded", "d_ready"))
        PER = 2 + Norm.CHAINED
        with nc.Block() as block:

            @block.sync
            def _(sp):
                sp.dma_start(wl[:, :], w_lin).then_inc(ready, 16)
                sp.dma_start(w1[:, :], w_dec1).then_inc(ready, 16)
                sp.dma_start(w2[:, :], w_dec2).then_inc(ready, 16)
                sp.dma_start(bl[:, :], b_lin.unsqueeze(1)).then_inc(ready, 16)
                sp.dma_start(b1[:, :], b_dec1.unsqueeze(1)).then_inc(ready, 16)
                load_rows(sp, [(b2, b_dec2)], ready)
                sp.dma_start(X[:, :, :], x3.rearrange("b p n -> p b n")).then_inc(ready, 16)
                with sp.Fori(0, 5) as i:
                    for j in range(5):
                        turned.freed(sp, i, j)
                        sp.dma_start(x[:, j % 2, :], h3[ds(5 * i + j, 1)].rearrange("o p n -> (o p) n")).then_inc(loaded.sem(j), 16)

            @block.gpsimd
            def _(pool):
                with pool.Fori(0, 5) as i:
                    for j in range(5):
                        finished.after(pool, i, j)
                        pool.dma_start(out[ds(5 * i + j, 1)].rearrange("o p n -> (o p) n"), y[:, j % 2, :]).then_inc(stored.sem(j), 16)
                for j in range(2):
                    stored.freed(pool, 5, j)

            @block.tensor
            def _(pe):
                t_ = nc.tensor

                def turn(i, j):
                    loaded.after(pe, i, j)
                    copied.freed(pe, i, j)
                    t_.transpose(pt[:, j % 2, 0:P], x[:, j % 2, :], k["ident"][0:P, 0:P]).then_inc(turned.sem(j), 1)

                pe.wait_ge(ready, 16 * 7)
                with pe.Fori(0, 5) as i:
                    turn(i, 0)
                    for j in range(5):
                        h = j % 2
                        if j < 4:
                            turn(i, j + 1)
                        copied.after(pe, i, j)
                        z_ready.freed(pe, i, j)
                        t_.matmul(pz[0:HID1, h, 0:P], wl[:, :], ht[:, h, :], start=True, stop=True).then_inc(lined.sem(j), 1)
                        z_ready.after(pe, i, j)
                        d_ready.freed(pe, i, j)
                        t_.matmul(pd[0:HID0, h, 0:P], w1[:, :], zt[:, h, :], start=True, stop=True).then_inc(decoded.sem(j), 1)
                        d_ready.after(pe, i, j)
                        finished.freed(pe, i, j)
                        t_.matmul(po[0:P, h, 0:D], dt[:, h, :], w2[:, :], start=True, stop=True).then_inc(multiplied.sem(j), 1)

            @block.scalar
            def _(act):
                act.wait_ge(ready, 16 * 7)
                with act.Fori(0, 5) as i:
                    for j in range(5):
                        h = j % 2
                        turned.after(act, i, j)
                        lined.freed(act, i, j)
                        nc.scalar.copy(ht[:, h, :], pt[:, h, 0:P]).then_inc(copied.sem(j), 1)
                        lined.after(act, i, j)
                        decoded.freed(act, i, j)
                        nc.scalar.activation(zt[:, h, :], pz[0:HID1, h, 0:P], ACT.Identity, bias=bl[:, :]).then_inc(z_ready.sem(j), 1)
                        decoded.after(act, i, j)
                        multiplied.freed(act, i, j)
                        nc.scalar.activation(dt[:, h, :], pd[0:HID0, h, 0:P], ACT.Relu, bias=b1[:, :]).then_inc(d_ready.sem(j), 1)
                        nm.on_act(nc, act, i, j)

            @block.vector
            def _(dve):
                v = nc.vector
                dve.wait_ge(ready, 16 * 7)
                with dve.Fori(0, 5) as i:
                    for j in range(5):
                        b, h = 5 * i + j, j % 2
                        chain = Chain(dve, chain_sem, b * PER)
                        multiplied.after(dve, i, j)
                        chain(v.tensor_tensor(r[:, h, :], po[0:P, h, 0:D], b2[:, :], ALU.add))
                        chain(v.tensor_tensor(r[:, h, :], r[:, h, :], X[:, ds(b, 1), :].rearrange("p a n -> p (a n)"), ALU.add))
                        stored.freed(dve, i, j)
                        nm.on_dve(nc, dve, chain, i, j, r[:, h, :], y[:, h, :])
                        assert chain.n == PER
                        dve.sem_inc(finished.sem(j), 1)
        clear_semaphores(nc, s)


def build_program(nc, a, out):
    ctx = ExitStack()
    with ctx:
        s = Scope(nc, ctx, "all")

        def dram(name, shape):
            return nc.dram_tensor(name, shape, fp32).ap()

        k = {
            "iota": s.sb("iota", [128, P]), "iota_bf": s.sb("iota_bf", [128, P], bf16),
            "ones": s.sb("ones", [128, P]), "zeros_bf": s.sb("zeros_bf", [128, 512], bf16),
            "ident": s.sb("ident", [128, 128]),
            "group_start": s.sb("group_start", [1, 32], i32), "tile_at": s.sb("tile_at", [1, NC], i32),
            "dinv": s.sb("dinv", [P, NB]), "hs": s.sb("hs", [P, NB]),
            "slots": dram("slots", [L, NC, F]), "key_rows": dram("key_rows", [EC, P]), "dblk_rows": dram("dblk_rows", [EC, P]),
            "counts": dram("counts", [NB, P, NB * P]), "hs_row": dram("hs_row", [NB, P]),
            "table": dram("table", [NB, P, 2 * D]), "cat": dram("cat", [NB, P, 3 * D]),
            "columns": 8, "sent": s.steps("sent", 2, 2, 16 * 8), "gemm_turn": 0, "apply_turn": 0,
        }
        k["gemm_steps"] = {n: s.steps(f"gemm_{n}", amount=16 if n in ("loaded", "stored") else 1)
                           for n in ("loaded", "turned", "copied", "multiplied", "finished", "stored")}
        k["apply_steps"] = {n: s.steps(f"apply_{n}", amount=16 if n in ("loaded", "stored") else 1)
                            for n in ("loaded", "summed", "finished", "stored")}
        x0 = a["x"].rearrange("(b p) n -> b p n", p=P)
        t1, t2, t3 = dram("t1", [NB, P, D]), dram("t2", [NB, P, D]), dram("t3", [NB, P, D + 1])
        h1, x1, x2, x3 = (dram(n, [NB, P, D]) for n in ("h1", "x1", "x2", "x3"))
        t4, h3 = dram("t4", [NB, P, DE]), dram("h3", [NB, P, DE])
        v = nc.vector

        phase_order(nc, k, a["src"], a["dst"], a["edge_weight"], a["edge_weight_n2"], a["edge_attr_128"],
                    a["L1_gnn_We"], a["L1_gnn_be"], a["L1_gnn_attn"])
        with ExitStack() as inner:
            k["edges"] = inner.enter_context(nc.sbuf_tensor("edges", [L, NC, F], fp32))
            phase_adjacency(nc, k)

            def scaled(width):
                def epilogue(dve, chain, b, po, y, tiles):
                    chain(v.tensor_scalar(y, po[:, 0:width], k["dinv"][:, ds(b, 1)], None, ALU.mult))
                return epilogue

            def hidden(dve, chain, i, j, b, t, y, tiles, x, nm):
                chain(v.tensor_scalar(y, t, k["dinv"][:, ds(b, 1)], 0.0, ALU.mult, ALU.max))

            def normed(dve, chain, i, j, b, t, y, tiles, x, nm):
                chain(v.scalar_tensor_tensor(t, t, k["dinv"][:, ds(b, 1)], x, ALU.mult, ALU.add))
                nm.on_dve(nc, dve, chain, i, j, t, y)

            phase_gemm(nc, k, "w1", x0, 2, [(a["L0_gnn_W1"], 0, D)], D, t1, D, {}, 1, scaled(D))
            phase_apply(nc, k, "c1", t1, D, h1, {}, 2, hidden)
            phase_gemm(nc, k, "w2", h1, 2, [(a["L0_gnn_W2"], 0, D)], D, t2, D, {}, 1, scaled(D))
            phase_apply(nc, k, "c2", t2, D, x1, {}, 2 + Norm.CHAINED, normed, resid=x0, norm=True)

            def with_logit(dve, chain, b, po, y, tiles):
                chain(v.tensor_tensor(y[:, 0:D], po[:, 0:D], tiles["bn"][:, :], ALU.add))
                chain(v.scalar_tensor_tensor(po[:, 0:D], y[:, 0:D], 1.0, tiles["attn"][:, :], ALU.mult, ALU.mult,
                                             accum_out=k["hs"][:, ds(b, 1)]))

            def ones_column(dve, y, sem):
                for h in range(2):
                    v.memset(y[:, h, D:D + 1], 1.0).then_inc(sem, 1)
                dve.wait_ge(sem, 2)

            phase_gemm(nc, k, "wn", x1, 2, [(a["L1_gnn_WnT"], 0, D)], D, t3, D + 1,
                       {"bn": a["L1_gnn_bn"], "attn": a["L1_gnn_attn"].rearrange("o h n -> (o h n)")}, 2, with_logit, ones_column)
            k["table"], wide = t3, k["table"]
            phase_attention(nc, k, x1, x2)

            phase_batch_norm(nc, k, x2, a["L2_gnn_gamma"], a["L2_gnn_beta"])

            def biased(dve, chain, b, po, y, tiles):
                chain(v.tensor_tensor(y[:, 0:D], po[:, 0:D], tiles["bi"][:, :], ALU.add))
                chain(v.tensor_tensor(y[:, D:2 * D], po[:, D:2 * D], tiles["bo"][:, :], ALU.add))

            phase_gemm(nc, k, "wio", k["cat"][:, :, 2 * D:3 * D], 2, [(a["L2_gnn_W_in"], 0, D), (a["L2_gnn_W_out"], D, D)], 2 * D,
                       wide, 2 * D, {"bi": a["L2_gnn_b_in"], "bo": a["L2_gnn_b_out"]}, 2, biased)
            phase_gated(nc, k, wide)
        phase_gates(nc, k, x2, a["L2_gnn_W_x2i"], a["L2_gnn_b_x2i"], a["L2_gnn_W_h2h"], x3)

        def relued(dve, chain, i, j, b, t, y, tiles, x, nm):
            chain(v.scalar_tensor_tensor(t, t, k["dinv"][:, ds(b, 1)], tiles["bc"][:, :], ALU.mult, ALU.add))
            chain(v.tensor_scalar(y, t, 0.0, None, ALU.max))

        phase_gemm(nc, k, "wc", x3, 2, [(a["L3_gnn_W_conv"], 0, DE)], DE, t4, DE, {}, 1, scaled(DE))
        phase_apply(nc, k, "c3", t4, DE, h3, {"bc": a["L3_gnn_b_conv"]}, 3, relued)
        phase_decoder(nc, k, h3, a["L3_gnn_W_lin"], a["L3_gnn_b_lin"], a["L3_gnn_W_dec1"], a["L3_gnn_b_dec1"],
                      a["L3_gnn_W_dec2"], a["L3_gnn_b_dec2"], x3, out.rearrange("(b p) n -> b p n", p=P))


_INS = ['x', 'src', 'dst', 'edge_attr_128', 'edge_weight', 'edge_weight_n2', 'L0_gnn_W1', 'L0_gnn_W2', 'L1_gnn_Wn',
        'L1_gnn_bn', 'L1_gnn_We', 'L1_gnn_be', 'L1_gnn_attn', 'L2_gnn_gamma', 'L2_gnn_beta', 'L2_gnn_W_in', 'L2_gnn_b_in',
        'L2_gnn_W_out', 'L2_gnn_b_out', 'L2_gnn_W_x2i', 'L2_gnn_b_x2i', 'L2_gnn_W_h2h', 'L3_gnn_W_conv', 'L3_gnn_b_conv',
        'L3_gnn_W_lin', 'L3_gnn_b_lin', 'L3_gnn_W_dec1', 'L3_gnn_b_dec1', 'L3_gnn_W_dec2', 'L3_gnn_b_dec2']


def kernel(**inputs):
    import numpy as _np
    import concourse.bacc as _bacc
    from concourse import mybir as _mybir
    from concourse.bass_utils import run_bass_kernel_spmd as _run

    nc = _bacc.Bacc("TRN2", target_bir_lowering=False, num_devices=1)
    arrays, args = {}, {}
    for name in _INS:
        a = _np.asarray(inputs[name])
        if name == 'L1_gnn_Wn':
            name, a = 'L1_gnn_WnT', a.T
        a = _np.ascontiguousarray(a)
        arrays[f"in_{name}_dram"] = a
        args[name] = nc.dram_tensor(f"in_{name}_dram", a.shape, _mybir.dt.from_np(a.dtype), kind="ExternalInput").ap()
    out = nc.dram_tensor("out_0_dram", (N, D), _mybir.dt.float32, kind="ExternalOutput").ap()
    build_program(nc, args, out)
    r = _run(nc, [arrays], core_ids=[0])
    return r.results[0]["out_0_dram"]
```

```python
import concourse.bass as bass
from concourse import mybir
from contextlib import ExitStack

fp32 = mybir.dt.float32
bf16 = mybir.dt.bfloat16
i32 = mybir.dt.int32
ALU = mybir.AluOpType
ACT = mybir.ActivationFunctionType
AX = mybir.AxisListType
ds = bass.ds

N = 3125
E = 100000
D = 256
DE = 128
P = 125
NB = N // P
EC = E // P
L = 128
BUCKETS = NB * NB
G = 8
RING = 4
NC = (E + BUCKETS * (L - 1)) // L + (G - 1) * NB
NC = -(-NC // G) * G
NG = NC // G
NT = -(-NG // RING)
NGA = (NT + 1) * RING
NCA = NGA * G
F = 8
SRC, DST, WIN, WOUT, EDGE = range(5)
TS = 128
BIG = 1.0e30
MAGIC = 12582912.0
EPS = 1e-5


class Steps:

    def __init__(self, sems, unroll, amount=1, i0=0):
        self.sems, self.unroll, self.amount, self.i0 = sems, unroll, amount, i0

    def from_turn(self, i0):
        return Steps(self.sems, self.unroll, self.amount, i0)

    def sem(self, j):
        return self.sems[j % len(self.sems)]

    def _count(self, i, j):
        s = len(self.sems)
        return (i + self.i0) * len(range(j % s, self.unroll, s)) + j // s

    def after(self, eng, i, j):
        eng.wait_ge(self.sem(j), (self._count(i, j) + 1) * self.amount)

    def freed(self, eng, i, j):
        eng.wait_ge(self.sem(j), self._count(i, j) * self.amount)


class Chain:

    def __init__(self, eng, sem, start=0):
        self.eng, self.sem, self.start, self.n = eng, sem, start, 0

    def __call__(self, ins):
        self.n += 1
        ins.then_inc(self.sem, 1)
        self.eng.wait_ge(self.sem, self.start + self.n)


class Scope:

    def __init__(self, nc, ctx, tag):
        self.nc, self.ctx, self.tag = nc, ctx, tag
        self.sems = []
        self.regs = {}

    def sb(self, name, shape, dt=fp32):
        return self.ctx.enter_context(self.nc.sbuf_tensor(f"{self.tag}_{name}", shape, dt))

    def ps(self, name, shape, dt=fp32):
        return self.ctx.enter_context(self.nc.psum_tensor(f"{self.tag}_{name}", shape, dt))

    def sem(self, name):
        self.sems.append(self.ctx.enter_context(self.nc.semaphore(f"{self.tag}_{name}")))
        return self.sems[-1]

    def registers(self, eng, name):
        if (eng, name) not in self.regs:
            self.regs[eng, name] = [self.ctx.enter_context(eng.register(f"{self.tag}_{name}{n}")) for n in range(G)]
        return self.regs[eng, name]

    def steps(self, name, slots=2, unroll=5, amount=1):
        return Steps([self.sem(f"{name}{s}") for s in range(slots)], unroll, amount)


def clear_semaphores(nc, scope):
    with nc.Block() as block:

        @block.gpsimd
        def _(pool):
            for sem in scope.sems:
                pool.sem_clear(sem)


def phase_order(nc, k, src, dst, w_in, w_out, edge_attr, we, be, attn):
    ctx = ExitStack()
    with ctx:
        s = Scope(nc, ctx, "ord")
        sblk, dblk = s.sb("sblk", [P, EC]), s.sb("dblk", [P, EC])
        key = s.sb("key", [P, EC])
        pay = s.sb("pay", [P, EC, 4])
        base = s.sb("base", [NB, NB])
        attnc = s.sb("attnc", [128, 2])
        attnb = s.sb("attnb", [128, 2, P])
        we_sb = s.sb("we_sb", [128, 2, DE])
        bec = s.sb("bec", [128, 2])
        vrow = s.sb("vrow", [P, DE])
        becol = s.sb("becol", [P, 1])
        tri = s.sb("tri", [P, P])
        ptri = s.sb("ptri", [NB, 32])
        iop = s.sb("iop", [128, 1])
        io25 = s.sb("io25", [P, NB])

        with ExitStack() as inner:
            a = Scope(nc, inner, "cnt")
            raws, rawd = a.sb("raws", [P, EC], i32), a.sb("rawd", [P, EC], i32)
            win, wout = a.sb("win", [P, EC]), a.sb("wout", [P, EC])
            node = a.sb("node", [P, EC])
            tmp = a.sb("tmp", [P, EC])
            ohs, ohd = a.sb("ohs", [P, EC, NB], bf16), a.sb("ohd", [P, EC, NB], bf16)
            empty = a.sb("empty", [128, NCA // 12, F])
            keyt = a.sb("keyt", [100, 2, 8, P])
            m4 = a.sb("m4", [4 * NB, 4 * NB])
            tot = a.sb("tot", [NB, NB])
            nch = a.sb("nch", [NB, NB])
            inc = a.sb("inc", [NB, NB])
            one25 = a.sb("one25", [NB, NB])
            grp = a.sb("grp", [NB, 1])
            g0 = a.sb("g0", [NB, 1])
            turns = a.sb("turns", [1, 1])
            first = a.sb("first", [NB, NB])
            ioc = a.sb("ioc", [NB, NCA])
            acc = a.sb("acc", [NB, NCA])
            row = a.sb("row", [1, NCA])
            rq = a.sb("rq", [1, NCA])
            pT = a.ps("pT", [128, 16, 128])
            pM = a.ps("pM", [128, 512])
            pK = a.ps("pK", [128, 512])
            pR = a.ps("pR", [128, 1024])
            loaded, consts, filled = a.sem("loaded"), a.sem("consts"), a.sem("filled")
            dve_chain, keyed, hot, turned = a.sem("dve_chain"), a.sem("keyed"), a.sem("hot"), a.sem("turned")
            copied, stored, counted, summed, m4ed = (a.sem(n) for n in ("copied", "stored", "counted", "summed", "m4ed"))
            grouped, prefixed, listed, rowed, packed = (a.sem(n) for n in ("grouped", "prefixed", "listed", "rowed", "packed"))
            spread, vdone = a.sem("spread"), a.sem("vdone")
            pool_chain = a.sem("pool_chain")
            with nc.Block() as block:

                @block.sync
                def _(sp):
                    sp.dma_start(raws[:, :], src.rearrange("(p c) -> p c", p=P)).then_inc(loaded, 16)
                    sp.dma_start(rawd[:, :], dst.rearrange("(p c) -> p c", p=P)).then_inc(loaded, 16)
                    sp.dma_start(win[:, :], w_in.rearrange("(p c) -> p c", p=P)).then_inc(loaded, 16)
                    sp.dma_start(wout[:, :], w_out.rearrange("(p c) -> p c", p=P)).then_inc(loaded, 16)
                    sp.dma_start(attnc[:, :], attn.rearrange("o h (t c) -> c (o h t)", t=2),
                                 allow_slow_non_contiguous=True).then_inc(loaded, 16)
                    sp.dma_start(bec[:, :], be.rearrange("(t c) -> c t", t=2),
                                 allow_slow_non_contiguous=True).then_inc(loaded, 16)
                    sp.dma_start(we_sb[:, :, :], we.rearrange("(t c) k -> c t k", t=2)).then_inc(loaded, 16)
                    sp.wait_ge(filled, 1)
                    for q in range(12):
                        w = NCA // 12
                        sp.dma_start(k["slots"][:, q * w:(q + 1) * w, :], empty[:, :, :]).then_inc(stored, 16)
                    sp.wait_ge(copied, 2)
                    for t, name in enumerate(("key_rows", "dblk_rows")):
                        sp.dma_start(k[name].rearrange("(q c) p -> c q p", q=8),
                                     keyt[:, t, :, :]).then_inc(stored, 16)
                    sp.wait_ge(stored, 14 * 16)

                @block.gpsimd
                def _(pool):
                    def made(ins):
                        ins.then_inc(consts, 1)

                    made(nc.gpsimd.iota(k["iota"][:, :], [[1, P]], 0, 0, allow_small_or_imprecise_dtypes=True))
                    made(nc.gpsimd.iota(k["iota_bf"][:, :], [[1, P]], 0, 0, allow_small_or_imprecise_dtypes=True))
                    made(nc.gpsimd.iota(iop[:, :], [[0, 1]], 0, 1, allow_small_or_imprecise_dtypes=True))
                    made(nc.gpsimd.iota(io25[:, :], [[1, NB]], 0, 0, allow_small_or_imprecise_dtypes=True))
                    made(nc.gpsimd.iota(ioc[:, :], [[1, NCA]], 0, 0, allow_small_or_imprecise_dtypes=True))
                    made(nc.gpsimd.memset(k["ones"][:, :], 1.0))
                    made(nc.gpsimd.memset(one25[:, :], 1.0))
                    made(nc.gpsimd.memset(k["zeros_bf"][:, :], 0.0))
                    made(nc.gpsimd.memset(acc[:, :], 0.0))
                    nc.gpsimd.memset(empty[:, :, :], -1.0).then_inc(filled, 1)
                    nc.gpsimd.memset(k["ident"][:, :], 0.0).then_inc(pool_chain, 1)
                    nc.gpsimd.memset(tri[:, :], 1.0).then_inc(pool_chain, 1)
                    nc.gpsimd.memset(ptri[:, :], 1.0).then_inc(pool_chain, 1)
                    pool.wait_ge(pool_chain, 3)
                    made(nc.gpsimd.affine_select(out=k["ident"][:, :], in_=k["ident"][:, :], compare_op=ALU.not_equal,
                                                 fill=1.0, base=0, pattern=[[-1, 128]], channel_multiplier=1))
                    made(nc.gpsimd.affine_select(out=tri[:, :], in_=tri[:, :], compare_op=ALU.is_gt,
                                                 fill=0.0, base=0, pattern=[[-1, P]], channel_multiplier=1))
                    made(nc.gpsimd.affine_select(out=ptri[:, :], in_=ptri[:, :], compare_op=ALU.is_gt,
                                                 fill=0.0, base=0, pattern=[[1, 32]], channel_multiplier=-1))

                @block.vector
                def _(dve):
                    chain = Chain(dve, dve_chain)
                    v = nc.vector
                    dve.wait_ge(loaded, 7 * 16)
                    dve.wait_ge(consts, 12)
                    for t in range(2):
                        ins = v.tensor_scalar(attnb[:, t, :], k["ones"][:, :], attnc[:, t:t + 1], None, ALU.mult)
                    ins.then_inc(spread, 1)
                    for raw, blk, f in ((raws, sblk, SRC), (rawd, dblk, DST)):
                        chain(v.tensor_copy(node[:, :], raw[:, :]))
                        chain(v.tensor_scalar(tmp[:, :], node[:, :], -float(P // 2), 1.0 / P, ALU.add, ALU.mult))
                        chain(v.tensor_scalar(tmp[:, :], tmp[:, :], MAGIC, None, ALU.add))
                        chain(v.tensor_scalar(blk[:, :], tmp[:, :], -MAGIC, None, ALU.add))
                        chain(v.scalar_tensor_tensor(pay[:, :, f], blk[:, :], -float(P), node[:, :], ALU.mult, ALU.add))
                    v.scalar_tensor_tensor(key[:, :], dblk[:, :], float(NB), sblk[:, :], ALU.mult, ALU.add).then_inc(keyed, 1)
                    for blk, oh in ((sblk, ohs), (dblk, ohd)):
                        v.tensor_tensor(oh[:, :, :], blk[:, :].unsqueeze(2).to_broadcast([P, EC, NB]),
                                        io25[:, :].unsqueeze(1).to_broadcast([P, EC, NB]), ALU.is_equal).then_inc(hot, 1)
                    dve.wait_ge(counted, 1)
                    v.tensor_copy(m4[:, :], pM[0:4 * NB, 0:4 * NB]).then_inc(m4ed, 1)
                    dve.wait_ge(summed, 1)
                    chain(v.tensor_copy(tot[:, :], pK[0:NB, 0:NB]))
                    chain(v.tensor_scalar(nch[:, :], tot[:, :], (L - 1) / 2.0, 1.0 / L, ALU.add, ALU.mult))
                    chain(v.tensor_scalar(nch[:, :], nch[:, :], MAGIC, None, ALU.add))
                    chain(v.tensor_scalar(nch[:, :], nch[:, :], -MAGIC, None, ALU.add))
                    chain(v.tensor_tensor_scan(inc[:, :], one25[:, :], nch[:, :], 0.0, ALU.mult, ALU.add))
                    chain(v.tensor_scalar(grp[:, :], inc[:, NB - 1:NB], (G - 1) / 2.0, 1.0 / G, ALU.add, ALU.mult))
                    chain(v.tensor_scalar(grp[:, :], grp[:, :], MAGIC, None, ALU.add))
                    chain(v.tensor_scalar(grp[:, :], grp[:, :], -MAGIC, None, ALU.add))
                    v.tensor_scalar(grp[:, :], grp[:, :], 1.0, None, ALU.max).then_inc(grouped, 1)
                    dve.wait_ge(prefixed, 1)
                    chain(v.tensor_copy(k["group_start"][0:1, 0:NB + 1], pK[0:1, 128:128 + NB + 1]))
                    chain(v.tensor_scalar(turns[:, :], pK[0:1, 128 + NB:129 + NB], (RING - 1) / 2.0, 1.0 / RING, ALU.add, ALU.mult))
                    chain(v.tensor_scalar(turns[:, :], turns[:, :], MAGIC, None, ALU.add))
                    chain(v.tensor_scalar(k["group_start"][0:1, 30:31], turns[:, :], -MAGIC, None, ALU.add))
                    chain(v.tensor_copy(g0[:, :], pK[0:NB, 256:257]))
                    chain(v.tensor_tensor(first[:, :], inc[:, :], nch[:, :], ALU.subtract))
                    chain(v.scalar_tensor_tensor(first[:, :], g0[:, :].to_broadcast([NB, NB]), float(G), first[:, :], ALU.mult, ALU.add))
                    chain(v.tensor_scalar(base[:, :], first[:, :], float(L), None, ALU.mult))
                    for q in range(NB):
                        chain(v.scalar_tensor_tensor(acc[:, :], ioc[:, :], first[:, q:q + 1], acc[:, :], ALU.is_ge, ALU.add))
                    dve.sem_inc(listed, 1)
                    dve.wait_ge(vdone, 1)
                    chain(v.tensor_copy(vrow[:, :], pK[0:P, 384:512]))
                    chain(v.tensor_copy(becol[:, :], pM[0:P, 256:257]))
                    for h in range(4):
                        w = NCA // 4
                        dve.wait_ge(rowed, h + 1)
                        chain(v.tensor_copy(row[:, h * w:(h + 1) * w], pR[0:1, (h % 2) * 512:(h % 2) * 512 + w]))
                        dve.sem_inc(packed, 1)
                    chain(v.tensor_scalar(row[:, :], row[:, :], -1.0, None, ALU.add))
                    chain(v.tensor_scalar(rq[:, :], row[:, :], -float(NB // 2), 1.0 / NB, ALU.add, ALU.mult))
                    chain(v.tensor_scalar(rq[:, :], rq[:, :], MAGIC, None, ALU.add))
                    chain(v.tensor_scalar(rq[:, :], rq[:, :], -MAGIC, None, ALU.add))
                    chain(v.scalar_tensor_tensor(row[:, :], rq[:, :], -float(NB), row[:, :], ALU.mult, ALU.add))
                    chain(v.tensor_scalar(k["tile_at"][:, :], row[:, :], float(TS), None, ALU.mult))
                    chain(v.tensor_scalar(k["parts_at"][SRC][:, :], row[:, :], 3.0, None, ALU.mult))
                    chain(v.tensor_scalar(k["parts_at"][DST][:, :], rq[:, :], 3.0, None, ALU.mult))

                @block.scalar
                def _(act):
                    act.wait_ge(loaded, 7 * 16)
                    nc.scalar.copy(pay[:, :, WIN], win[:, :])
                    nc.scalar.copy(pay[:, :, WOUT], wout[:, :])
                    for t in range(2):
                        act.wait_ge(turned, t + 1)
                        nc.scalar.copy(keyt[:, t, :, :], pT[0:100, 8 * t:8 * t + 8, 0:P]).then_inc(copied, 1)

                @block.tensor
                def _(pe):
                    t_ = nc.tensor
                    pe.wait_ge(spread, 1)
                    for t in range(2):
                        t_.matmul(pK[0:P, 384:512], attnb[:, t, :], we_sb[:, t, :], start=(t == 0), stop=(t == 1))
                    for t in range(2):
                        ins = t_.matmul(pM[0:P, 256:257], attnb[:, t, :], bec[:, t:t + 1], start=(t == 0), stop=(t == 1))
                    ins.then_inc(vdone, 1)
                    pe.wait_ge(keyed, 1)
                    for t, what in enumerate((key, dblk)):
                        for q in range(8):
                            ins = t_.transpose(pT[0:100, 8 * t + q, 0:P], what[:, 100 * q:100 * q + 100], k["ident"][0:P, 0:P])
                        ins.then_inc(turned, 1)
                    pe.wait_ge(hot, 2)
                    t_.matmul(pM[0:4 * NB, 0:4 * NB], k["zeros_bf"][0:P, 0:4 * NB], k["zeros_bf"][0:P, 0:4 * NB],
                              start=True, stop=False, skip_group_check=True)
                    with pe.Fori(0, EC // 8) as i:
                        for j in range(2):
                            c = 8 * i + 4 * j
                            t_.matmul(pM[0:4 * NB, 0:4 * NB], ohd[:, ds(c, 4), :].rearrange("p a b -> p (a b)"),
                                      ohs[:, ds(c, 4), :].rearrange("p a b -> p (a b)"),
                                      start=False, stop=False, skip_group_check=True)
                    t_.matmul(pM[0:4 * NB, 0:4 * NB], k["zeros_bf"][0:P, 0:4 * NB], k["zeros_bf"][0:P, 0:4 * NB],
                              start=False, stop=True, skip_group_check=True).then_inc(counted, 1)
                    pe.wait_ge(m4ed, 1)
                    for j in range(4):
                        ins = t_.matmul(pK[0:NB, 0:NB], k["ident"][0:4 * NB, NB * j:NB * j + NB],
                                        m4[:, NB * j:NB * j + NB], start=(j == 0), stop=(j == 3))
                    ins.then_inc(summed, 1)
                    pe.wait_ge(grouped, 1)
                    t_.matmul(pK[0:1, 128:128 + NB + 1], grp[:, :], ptri[:, 0:NB + 1], start=True, stop=True)
                    t_.matmul(pK[0:NB, 256:257], ptri[:, 0:NB], grp[:, :], start=True, stop=True).then_inc(prefixed, 1)
                    pe.wait_ge(listed, 1)
                    for h in range(4):
                        w = NCA // 4
                        if h >= 2:
                            pe.wait_ge(packed, h - 1)
                        t_.matmul(pR[0:1, (h % 2) * 512:(h % 2) * 512 + w], k["ones"][0:NB, 0:1],
                                  acc[:, h * w:(h + 1) * w], start=True, stop=True).then_inc(rowed, 1)
            clear_semaphores(nc, a)

        with ExitStack() as inner:
            b = Scope(nc, inner, "put")
            C = k["columns"]
            rows = b.sb("rows", [P, 2, C * P])
            drow = b.sb("drow", [NB, 2, C * P])
            ohdT = b.sb("ohdT", [NB, 2, C * P])
            ohd, ohs = b.sb("ohd", [P, 2, C, NB], bf16), b.sb("ohs", [P, 2, C, NB], bf16)
            ea = b.sb("ea", [P, 2, C, DE])
            prod = b.sb("prod", [P, 2, C, DE])
            junk = b.sb("junk", [P, C, P], bf16)
            pre = b.sb("pre", [NB, 2, C, NB])
            rank = b.sb("rank", [P, 2, C])
            hit = b.sb("hit", [P, 2, C, NB])
            col = b.sb("col", [P, 2, C])
            pos = b.sb("pos", [P, 2, C])
            chk = b.sb("chk", [P, 2, C])
            index = b.sb("index", [P, 2, C], i32)
            stage = [b.sb(f"stage{h}", [P, C, F]) for h in range(2)]
            pK = b.ps("pK", [128, 512])
            pL = b.ps("pL", [128, 2, 512])
            loaded = b.steps("loaded", 2, 2, 16)
            hot = b.steps("hot", 2, 2)
            ranked = b.steps("ranked", 2, 2)
            looked = b.steps("looked", 2, 2)
            placed = b.steps("placed", 2, 2)
            staged = b.steps("staged", 2, 2)
            sent = k["sent"]
            counted, copied, cleared = b.sem("counted"), b.sem("copied"), b.sem("cleared")
            dve_chain, passed = b.sem("dve_chain"), b.sem("passed")
            slots = k["slots"].rearrange("l c f -> (l c) f")
            PER = 13
            with nc.Block() as block:

                @block.sync
                def _(sp):
                    keys_v = k["key_rows"].rearrange("(g c) p -> g (c p)", c=C)
                    dblk_v = k["dblk_rows"].rearrange("(g c) p -> g (c p)", c=C)
                    ea_v = edge_attr.rearrange("(p c) k -> p c k", p=P)
                    with sp.Fori(0, EC // C // 2) as i:
                        for h in range(2):
                            ranked.freed(sp, i, h)
                            hot.freed(sp, i, h)
                            g = 2 * i + h
                            sp.dma_start(rows[:, h, :], keys_v[ds(g, 1), :].to_broadcast([P, C * P])).then_inc(loaded.sem(h), 16)
                            sp.dma_start(drow[:, h, :], dblk_v[ds(g, 1), :].to_broadcast([NB, C * P])).then_inc(loaded.sem(h), 16)
                            sp.dma_start(ea[:, h, :, :], ea_v[:, ds(g * C, C), :]).then_inc(loaded.sem(h), 16)

                @block.vector
                def _(dve):
                    v = nc.vector
                    for h in range(2):
                        v.memset(stage[h][:, :, :], 0.0).then_inc(cleared, 1)
                    dve.wait_ge(cleared, 2)
                    with dve.Fori(0, EC // C // 2) as i:
                        for h in range(2):
                            g = 2 * i + h
                            chain = Chain(dve, dve_chain, g * PER)
                            dve.wait_ge(loaded.sem(h), 48 * i + 48)
                            looked.freed(dve, i, h)
                            v.tensor_scalar(ohdT[:, h, :], drow[:, h, :], iop[0:NB, :], None, ALU.is_equal)
                            v.tensor_tensor(ohd[:, h, :, :], dblk[:, ds(g * C, C)].unsqueeze(2).to_broadcast([P, C, NB]),
                                            io25[:, :].unsqueeze(1).to_broadcast([P, C, NB]), ALU.is_equal)
                            chain(v.tensor_tensor(ohs[:, h, :, :], sblk[:, ds(g * C, C)].unsqueeze(2).to_broadcast([P, C, NB]),
                                                  io25[:, :].unsqueeze(1).to_broadcast([P, C, NB]), ALU.is_equal))
                            dve.sem_inc(hot.sem(h), 1)
                            for j in range(C):
                                ins = v.scalar_tensor_tensor(junk[:, j, :], rows[:, h, j * P:(j + 1) * P], key[:, ds(g * C + j, 1)],
                                                             tri[:, :], ALU.is_equal, ALU.mult, accum_out=rank[:, h, j:j + 1])
                                chain(ins) if j == C - 1 else None
                            chain(v.tensor_tensor(prod[:, h, :, :], ea[:, h, :, :], vrow[:, :].unsqueeze(1).to_broadcast([P, C, DE]), ALU.mult))
                            chain(v.tensor_reduce(col[:, h, :], prod[:, h, :, :], AX.X, ALU.add))
                            dve.sem_inc(ranked.sem(h), 1)
                            sent.freed(dve, i, h)
                            chain(v.tensor_scalar(stage[h][:, :, EDGE], col[:, h, :], becol[:, :], None, ALU.add))
                            looked.after(dve, i, h)
                            chain(v.tensor_tensor(hit[:, h, :, :], pL[0:P, h, 0:C * NB].rearrange("p (c s) -> p c s", s=NB),
                                                  ohs[:, h, :, :], ALU.mult))
                            chain(v.tensor_reduce(pos[:, h, :], hit[:, h, :, :], AX.X, ALU.add))
                            chain(v.tensor_tensor(pos[:, h, :], pos[:, h, :], rank[:, h, :], ALU.add))
                            chain(v.tensor_scalar(chk[:, h, :], pos[:, h, :], -(L - 1) / 2.0, 1.0 / L, ALU.add, ALU.mult))
                            chain(v.tensor_scalar(chk[:, h, :], chk[:, h, :], MAGIC, None, ALU.add))
                            chain(v.tensor_scalar(chk[:, h, :], chk[:, h, :], -MAGIC, None, ALU.add))
                            chain(v.scalar_tensor_tensor(pos[:, h, :], chk[:, h, :], -float(L), pos[:, h, :], ALU.mult, ALU.add))
                            chain(v.scalar_tensor_tensor(index[:, h, :], pos[:, h, :], float(NCA), chk[:, h, :], ALU.mult, ALU.add))
                            assert chain.n == PER, chain.n
                            dve.sem_inc(placed.sem(h), 1)

                @block.scalar
                def _(act):
                    act.wait_ge(cleared, 2)
                    with act.Fori(0, EC // C // 2) as i:
                        for h in range(2):
                            g = 2 * i + h
                            looked.freed(act, i, h)
                            for j in range(C):
                                act.wait_ge(counted, g * C + j + 1)
                                nc.scalar.copy(pre[:, h, j, :], pK[0:NB, 0:NB]).then_inc(copied, 1)
                            sent.freed(act, i, h)
                            nc.scalar.copy(stage[h][:, :, 0:4], pay[:, ds(g * C, C), :]).then_inc(staged.sem(h), 1)

                @block.tensor
                def _(pe):
                    t_ = nc.tensor
                    t_.matmul(pK[0:NB, 0:NB], k["ident"][0:NB, 0:NB], base[:, :], start=True, stop=False,
                              skip_group_check=True).then_inc(counted, 1)
                    with pe.Fori(0, EC // C // 2) as i:
                        for h in range(2):
                            g = 2 * i + h
                            hot.after(pe, i, h)
                            placed.freed(pe, i, h)
                            for j in range(C):
                                pe.wait_ge(copied, g * C + j + 1)
                                t_.matmul(pK[0:NB, 0:NB], ohd[:, h, j, :], ohs[:, h, j, :], start=False, stop=False,
                                          skip_group_check=True).then_inc(counted, 1)
                                ins = t_.matmul(pL[0:P, h, NB * j:NB * j + NB], ohdT[:, h, j * P:(j + 1) * P], pre[:, h, j, :],
                                                start=True, stop=True)
                            ins.then_inc(looked.sem(h), 1)

                @block.gpsimd
                def _(pool):
                    with pool.Fori(0, EC // C // 2) as i:
                        for h in range(2):
                            placed.after(pool, i, h)
                            staged.after(pool, i, h)
                            pool.sem_inc(passed, 1)
                            for j in range(C):
                                nc.gpsimd.indirect_dma_start(
                                    slots, bass.IndirectOffsetOnAxis(index[:, h, j:j + 1], 0),
                                    stage[h][:, j, :], None).then_inc(sent.sem(h), 16)
                    for h in range(2):
                        pool.wait_ge(sent.sem(h), 16 * C * (EC // C // 2))
            clear_semaphores(nc, b)


class Norm:

    CHAINED = 5

    def __init__(self, s):
        self.stats, self.mv = s.sb("stats", [P, 2, 6]), s.sb("mv", [P, 2, 2])
        self.ve, self.sd, self.rs = s.sb("ve", [P, 2]), s.sb("sd", [P, 2]), s.sb("rs", [P, 2])
        self.shifted = s.steps("shifted")
        self.rooted = s.steps("rooted")
        self.passed = s.sem("passed")

    def on_dve(self, nc, dve, chain, i, j, r, y):
        h, v = j % 2, nc.vector
        chain(v.bn_stats(self.stats[:, h, :], r))
        dve.sem_inc(self.passed, 1)
        chain(v.bn_aggr(self.mv[:, h, :], self.stats[:, h, :]))
        chain(v.tensor_scalar(self.ve[:, h:h + 1], self.mv[:, h, 1:2], EPS, None, ALU.add))
        dve.sem_inc(self.shifted.sem(j), 1)
        self.rooted.after(dve, i, j)
        chain(v.reciprocal(self.rs[:, h:h + 1], self.sd[:, h:h + 1]))
        chain(v.tensor_scalar(y, r, self.mv[:, h, 0:1], self.rs[:, h:h + 1], ALU.subtract, ALU.mult))

    def on_act(self, nc, act, i, j):
        h = j % 2
        self.shifted.after(act, i, j)
        nc.scalar.activation(self.sd[:, h:h + 1], self.ve[:, h:h + 1], ACT.Sqrt).then_inc(self.rooted.sem(j), 1)


def load_rows(sp, rows, sem):
    for tile, vector in rows:
        sp.dma_start(tile[:, :], vector.partition_broadcast(P)).then_inc(sem, 16)


def group_range(eng, k, d):
    g0 = eng.value_load(k["group_start"][0:1, ds(d, 1)], min_val=0, max_val=NG - 1)
    g1 = eng.value_load(k["group_start"][0:1, ds(d + 1, 1)], min_val=1, max_val=NG)
    return g0, g1


def tiles_of(ps):
    return ps[0:P, 0:NB * TS].rearrange("p (s q) -> p s q", q=TS)


HALF = 12


def word(k, c, f):
    return k["edges"][:, ds(c, 1), f:f + 1].rearrange("p a b -> p (a b)")


def turns_of(eng, k):
    return eng.value_load(k["group_start"][0:1, 30:31], min_val=1, max_val=NT)


def load_offsets(eng, s, name, table, c, most):
    regs = s.registers(eng, name)
    for q in range(0, G, 4):
        eng.load(regs[q:q + 4], table[0:1, ds(c + q, 4)])
    return [eng.snap(r, min_val=0, max_val=most) for r in regs]


def zero_tiles(nc, k, ps):
    for q in range(7):
        nc.tensor.matmul(ps[:, 512 * q:512 * q + 512], k["zeros_bf"][:, 0:128], k["zeros_bf"][:, :], start=True, stop=False,
                         skip_group_check=True)


class Ring:

    def __init__(self, s, parts):
        self.parts = parts
        self.buf = s.sb("ring", [L, RING, len(parts), G * P], bf16)
        self.landed = [s.sem(f"landed{r}") for r in range(RING)]
        self.arrived, self.passed = s.sem("arrived"), s.sem("ring_passed")

    def on_sp(self, sp, k, read):
        hot = k["hot"]

        def load(g, j):
            for n, part in enumerate(self.parts):
                sp.dma_start(self.buf[:, j % RING, n, :], hot[ds(g, 1), :, part, :].rearrange("o p n -> (o p) n")
                             ).then_inc(self.landed[j % RING], 16)

        n = 16 * len(self.parts)
        for j in range(RING - 1):
            load(j, j)
        with sp.Fori(0, turns_of(sp, k)) as i:
            for j in range(RING):
                g = RING * i + j
                for sem in read:
                    sp.wait_ge(sem, g)
                load(g + RING - 1, j + RING - 1)
                sp.wait_ge(self.landed[j], n * i + n)
                sp.sem_inc(self.arrived, 1)
        turns = turns_of(sp, k)
        for j in range(RING - 1):
            sp.wait_ge(self.landed[j], n * turns + n)
        sp.sem_inc(self.passed, 1)

    def part(self, g, n, c0=0, c1=G):
        return self.buf[:, ds(g % RING, 1), n, c0 * P:c1 * P].rearrange("p a n -> p (a n)")


def phase_adjacency(nc, k):
    ctx = ExitStack()
    with ctx:
        s = Scope(nc, ctx, "adj")
        T = s.sb("T", [P, 2, NB, P])
        ring = s.sb("ring", [L, RING, 2, G * P], bf16)
        deg, root = s.sb("deg", [P, NB]), s.sb("root", [P, NB])
        ps = s.ps("ps", [128, 4096])
        loaded, hot, used, moved, summed, ended, rooted, shifted, passed = (
            s.sem(n) for n in ("loaded", "hot", "used", "moved", "summed", "ended", "rooted", "shifted", "passed"))
        saved = [s.sem(f"saved{r}") for r in range(RING)]
        stored = [s.sem(f"stored{r}") for r in range(2)]
        with nc.Block() as block:

            @block.sync
            def _(sp):
                sp.dma_start(k["edges"][:, :, :], k["slots"]).then_inc(loaded, 16)
                turns = turns_of(sp, k)
                with sp.Fori(0, turns + 1) as i:
                    for j in range(RING):
                        g = RING * i + j
                        sp.wait_ge(hot, g + 1)
                        sp.dma_start(k["hot"][ds(g, 1)].rearrange("o p t n -> (o p) (t n)"),
                                     ring[:, j, :, :].rearrange("p t n -> p (t n)")).then_inc(saved[j], 16)
                turns = turns_of(sp, k)
                for j in range(RING):
                    sp.wait_ge(saved[j], 16 * turns + 16)
                sp.sem_inc(passed, 1)

            @block.vector
            def _(dve):
                dve.wait_ge(loaded, 16)
                with dve.Fori(0, turns_of(dve, k) + 1) as i:
                    for j in range(RING):
                        g = RING * i + j
                        dve.wait_ge(used, g + 1)
                        dve.wait_ge(saved[j], 16 * i)
                        for c in range(G):
                            for f in (SRC, DST):
                                ins = nc.vector.tensor_scalar(ring[:, j, f, c * P:(c + 1) * P], k["iota_bf"][:, :],
                                                              word(k, G * g + c, f), None, ALU.is_equal)
                        ins.then_inc(hot, 1)
                dve.wait_ge(summed, NB)
                nc.vector.tensor_scalar(deg[:, :], ps[0:P, 3584:3584 + NB], 1.0, None, ALU.add).then_inc(shifted, 1)
                dve.wait_ge(rooted, 1)
                nc.vector.reciprocal(k["dinv"][:, :], root[:, :]).then_inc(ended, 1)
                dve.wait_ge(ended, 1)

            @block.scalar
            def _(act):
                with act.Fori(0, NB // 5) as i:
                    for j in range(5):
                        d = 5 * i + j
                        act.wait_ge(summed, d)
                        g1 = act.value_load(k["group_start"][0:1, ds(d + 1, 1)], min_val=1, max_val=NG)
                        act.wait_ge(used, g1 + RING)
                        act.wait_ge(stored[j % 2], 16 * (i * len(range(j % 2, 5, 2)) + j // 2))
                        nc.scalar.copy(T[:, j % 2, :, :], tiles_of(ps)[:, :, 0:P]).then_inc(moved, 1)
                        act.wait_ge(moved, d + 1)
                        act.dma_start(k["counts"][ds(d, 1)].rearrange("o p n -> (o p) n"),
                                      T[:, j % 2, :, :].rearrange("p s q -> p (s q)")).then_inc(stored[j % 2], 16)
                act.wait_ge(shifted, 1)
                nc.scalar.activation(root[:, :], deg[:, :], ACT.Sqrt).then_inc(rooted, 1)
                act.wait_ge(stored[0], 16 * 15)
                act.wait_ge(stored[1], 16 * 10)

            @block.tensor
            def _(pe):
                t_ = nc.tensor
                pe.sem_inc(used, RING)
                with pe.Fori(0, NB // 5) as i:
                    for j in range(5):
                        d = 5 * i + j
                        g0, g1 = group_range(pe, k, d)
                        zero_tiles(nc, k, ps)
                        with pe.Fori(g0, g1) as g:
                            at = load_offsets(pe, s, "at", k["tile_at"], G * g, (NB - 1) * TS)
                            pe.wait_ge(hot, g + 1)
                            for c in range(G):
                                left, right = (ring[:, ds(g % RING, 1), f, c * P:(c + 1) * P].rearrange("p a n -> p (a n)")
                                               for f in (SRC, DST))
                                ins = t_.matmul(ps[0:P, ds(at[c], P)], left, right, start=False, stop=False,
                                                skip_group_check=True)
                            ins.then_inc(used, 1)
                        pe.wait_ge(moved, d + 1)
                        for q in range(NB):
                            ins = t_.matmul(ps[0:P, ds(d + 3584, 1)], T[:, j % 2, q, :], k["ones"][0:P, 0:1],
                                            start=(q == 0), stop=(q == NB - 1), skip_group_check=True)
                        ins.then_inc(summed, 1)
                pe.drain().then_inc(used, 2 * RING)
        clear_semaphores(nc, s)


def phase_lookup(nc, k, tag, part, values, per_turn, finish, prepare=None):
    ctx = ExitStack()
    with ctx:
        s = Scope(nc, ctx, tag)
        ring = Ring(s, (part,))
        v3 = s.sb("v3", [P, NB, 3], bf16)
        rest = s.sb("rest", [P, NB])
        ident_bf = s.sb("ident_bf", [L, L], bf16)
        turned = s.sb("turned", [P, 2, G * L], bf16)
        pt = s.ps("pt", [128, 2, G * L])
        pz = s.ps("pz", [128, 2, 512])
        z = s.sb("z", [L, 2, 2 * G])
        split, chain_sem = s.sem("split"), s.sem("chain")
        flipped, copied = s.sem("flipped"), s.sem("copied")
        looked = s.steps("looked", 2, 2)
        finished = s.steps("finished", 2, 2)
        ended = s.sem("ended")
        with nc.Block() as block:

            @block.sync
            def _(sp):
                ring.on_sp(sp, k, [flipped])

            @block.tensor
            def _(pe):
                t_ = nc.tensor

                def turn(g, j):
                    pe.wait_ge(ring.arrived, g + 1)
                    pe.wait_ge(copied, g + 1)
                    for c in range(G):
                        ins = t_.matmul(pt[0:P, j % 2, L * c:L * c + L], ring.buf[:, j, 0, c * P:(c + 1) * P], ident_bf[:, :],
                                        start=True, stop=True)
                    ins.then_inc(flipped, 1)

                def look(i, g, j):
                    at = load_offsets(pe, s, "at", k["parts_at"][part], G * g, (NB - 1) * 3)
                    pe.wait_ge(copied, g + 3)
                    if j % 2 == 0:
                        finished.freed(pe, i, j // 2)
                    v3f = v3[:, :, :].rearrange("p b n -> p (b n)")
                    for c in range(G):
                        o = (j % 2) * 3 * G + 3 * c
                        ins = t_.matmul(pz[0:L, j // 2, o:o + 3], turned[:, j % 2, L * c:L * c + L], v3f[:, ds(at[c], 3)],
                                        start=True, stop=True)
                    if j % 2 == 1:
                        ins.then_inc(looked.sem(j // 2), 1)

                pe.wait_ge(split, 1)
                pe.sem_inc(copied, 2)
                with pe.Fori(0, turns_of(pe, k)) as i:
                    for j in range(RING):
                        turn(RING * i + j, j)
                        if j > 0:
                            look(i, RING * i + j - 1, j - 1)
                    look(i, RING * i + RING - 1, RING - 1)

            @block.scalar
            def _(act):
                with act.Fori(0, turns_of(act, k)) as i:
                    for j in range(RING):
                        g = RING * i + j
                        act.wait_ge(flipped, g + 1)
                        if j < 2:
                            looked.freed(act, i, 1)
                        else:
                            looked.after(act, i, 0)
                        nc.scalar.copy(turned[:, j % 2, :], pt[0:P, j % 2, :]).then_inc(copied, 1)

            @block.vector
            def _(dve):
                v = nc.vector
                chain = Chain(dve, chain_sem)
                chain(v.tensor_copy(ident_bf[:, :], k["ident"][:, :]))
                if prepare:
                    prepare(dve, chain)
                chain(v.tensor_copy(v3[:, :, 0], values))
                chain(v.tensor_tensor(rest[:, :], values, v3[:, :, 0], ALU.subtract))
                chain(v.tensor_copy(v3[:, :, 1], rest[:, :]))
                chain(v.tensor_tensor(rest[:, :], rest[:, :], v3[:, :, 1], ALU.subtract))
                chain(v.tensor_copy(v3[:, :, 2], rest[:, :]))
                dve.sem_inc(split, 1)
                n = chain.n
                with dve.Fori(0, turns_of(dve, k)) as i:
                    for h in range(2):
                        g = RING * i + 2 * h
                        chain = Chain(dve, chain_sem, n + (2 * i + h) * per_turn)
                        looked.after(dve, i, h)
                        chain(v.tensor_reduce(z[:, h, :], pz[0:L, h, 0:6 * G].rearrange("p (c t) -> p c t", t=3), AX.X, ALU.add))
                        dve.sem_inc(finished.sem(h), 1)
                        finish(dve, chain, z[:, h, :], g)
                        assert chain.n == per_turn
        clear_semaphores(nc, s)


def phase_greatest(nc, k, logit, greatest):
    ctx = ExitStack()
    with ctx:
        s = Scope(nc, ctx, "max")
        ring = Ring(s, (DST,))
        far = s.sb("far", [L, 2, 4 * P], bf16)
        top8 = s.sb("top8", [L, G, P])
        tops = s.sb("tops", [L, NB, P])
        ps = s.ps("ps", [128, 4096])
        read, chain_a, chain_d, topped, turned, passed = (
            s.sem(n) for n in ("read", "chain_a", "chain_d", "topped", "turned", "passed"))
        with nc.Block() as block:

            @block.sync
            def _(sp):
                ring.on_sp(sp, k, [read])

            @block.vector
            def _(dve):
                v = nc.vector
                with dve.Fori(0, NB) as d:
                    g0, g1 = group_range(dve, k, d)
                    chain = Chain(dve, chain_d, 2 * d)
                    chain(v.memset(top8[:, :, :], -BIG))
                    dve.sem_inc(passed, 1)
                    with dve.Fori(g0, g1) as g:
                        c1 = Chain(dve, chain_a, g * 3)
                        dve.wait_ge(ring.arrived, g + 1)
                        for h in range(2):
                            ins = v.tensor_scalar(far[:, h, :], ring.part(g, 0, 4 * h, 4 * h + 4), -1.0, BIG, ALU.add, ALU.mult)
                            c1(ins) if h == 1 else None
                        dve.sem_inc(read, 1)
                        for c in range(G):
                            ins = v.scalar_tensor_tensor(top8[:, c, :], far[:, c // 4, (c % 4) * P:(c % 4 + 1) * P],
                                                         logit[:, ds(G * g + c, 1)], top8[:, c, :], ALU.add, ALU.max)
                        c1(ins)
                        c1(v.tensor_copy(far[0:1, 0, 0:1], far[0:1, 0, 0:1]))
                    chain(v.tensor_reduce(tops[:, ds(d, 1), :].rearrange("p a n -> p (a n)"),
                                          top8[:, :, :].rearrange("p j q -> p q j"), AX.X, ALU.max))
                dve.sem_inc(topped, 1)
                dve.sem_inc(read, RING)
                dve.wait_ge(turned, 1)
                v.tensor_reduce(greatest, ps[0:P, 0:NB * L].rearrange("p (b l) -> p b l", l=L), AX.X, ALU.max).then_inc(topped, 1)
                dve.wait_ge(topped, 2)

            @block.tensor
            def _(pe):
                pe.wait_ge(topped, 1)
                for b in range(NB):
                    ins = nc.tensor.transpose(ps[0:P, L * b:L * b + L], tops[:, b, :], k["ident"][:, :])
                ins.then_inc(turned, 1)
        clear_semaphores(nc, s)


def phase_weighted(nc, k, tag, by_dst, table, width, weight, dve_per_d, epilogue, make):
    ctx = ExitStack()
    with ctx:
        s = Scope(nc, ctx, tag)
        ring = Ring(s, (SRC, DST))
        lf, rf = (SRC, DST) if by_dst else (DST, SRC)
        left, right = s.sb("left", [L, 2, 4, P]), s.sb("right", [L, 2, 4, P])
        H = s.sb("H", [P, NB, width])
        T = s.sb("T", [P, NB, P])
        ps = s.ps("ps", [128, 4096])
        loaded, moved, summed = s.sem("loaded"), s.sem("moved"), s.sem("summed")
        left_ready, right_ready, used = s.steps("left", 2, 2), s.steps("right", 2, 2), s.steps("used", 2, 2)
        multiplied, added = (s.steps("multiplied", 2, NB), s.steps("added", 2, NB)) if not by_dst else (None, None)
        slot = (lambda h: ps[0:P, 3584 - 512 * (h % 2):3584 - 512 * (h % 2) + width])
        hooks = make(s)

        def complete(eng, g1):
            for h in range(2):
                used.freed(eng, g1, h)

        def tiles_free(eng, d):
            if by_dst:
                eng.wait_ge(summed, d)
            else:
                for h in range(2):
                    multiplied.freed(eng, d, h)

        with nc.Block() as block:

            @block.sync
            def _(sp):
                sp.dma_start(H[:, :, :], table.rearrange("b p n -> p b n")).then_inc(loaded, 16)
                ring.on_sp(sp, k, [left_ready.sem(1), right_ready.sem(1)])

            @block.tensor
            def _(pe):
                t_ = nc.tensor
                pe.wait_ge(loaded, 16)
                with pe.Fori(0, NB) as d:
                    g0, g1 = group_range(pe, k, d)
                    if not by_dst:
                        for h in range(2):
                            added.freed(pe, d, h)
                    zero_tiles(nc, k, ps)
                    with pe.Fori(g0, g1) as g:
                        at = load_offsets(pe, s, "at", k["tile_at"], G * g, (NB - 1) * TS)
                        for h in range(2):
                            left_ready.after(pe, g, h)
                            right_ready.after(pe, g, h)
                            for c in range(4):
                                ins = t_.matmul(ps[0:P, ds(at[4 * h + c], P)], left[:, h, c, :], right[:, h, c, :],
                                                start=False, stop=False, skip_group_check=True)
                            ins.then_inc(used.sem(h), 1)
                    pe.wait_ge(moved, 2 * d + 2)
                    if by_dst:
                        hooks["pe"](pe, d)
                        for q in range(NB):
                            ins = t_.matmul(slot(0), T[:, q, :], H[:, q, :], start=(q == 0), stop=(q == NB - 1))
                        ins.then_inc(summed, 1)
                    else:
                        for q in range(NB):
                            added.freed(pe, d, q)
                            t_.matmul(slot(q), T[:, q, :], H[:, ds(d, 1), :].rearrange("p a n -> p (a n)"),
                                      start=True, stop=True).then_inc(multiplied.sem(q), 1)

            @block.scalar
            def _(act):
                with act.Fori(0, NB) as d:
                    g0, g1 = group_range(act, k, d)
                    with act.Fori(g0, g1) as g:
                        act.wait_ge(ring.arrived, g + 1)
                        for h in range(2):
                            used.freed(act, g, h)
                            nc.scalar.copy(left[:, h, :, :].rearrange("p c n -> p (c n)"), ring.part(g, lf, 4 * h, 4 * h + 4)
                                           ).then_inc(left_ready.sem(h), 1)
                    complete(act, g1)
                    tiles_free(act, d)
                    nc.scalar.copy(T[:, 0:HALF, :], tiles_of(ps)[:, 0:HALF, 0:P]).then_inc(moved, 1)
                    hooks["act"](act, d)
                act.drain().then_inc(left_ready.sem(1), RING)

            @block.vector
            def _(dve):
                v = nc.vector
                hooks["dve"](dve)
                with dve.Fori(0, NB) as d:
                    g0, g1 = group_range(dve, k, d)
                    with dve.Fori(g0, g1) as g:
                        dve.wait_ge(ring.arrived, g + 1)
                        for h in range(2):
                            used.freed(dve, g, h)
                            v.tensor_tensor(right[:, h, :, :], ring.part(g, rf, 4 * h, 4 * h + 4).rearrange("p (c n) -> p c n", n=P),
                                            weight(G * g + 4 * h).unsqueeze(2).to_broadcast([L, 4, P]), ALU.mult
                                            ).then_inc(right_ready.sem(h), 1)
                    complete(dve, g1)
                    tiles_free(dve, d)
                    v.tensor_copy(T[:, HALF:NB, :], tiles_of(ps)[:, HALF:NB, 0:P]).then_inc(moved, 1)
                    if by_dst:
                        dve.wait_ge(summed, d + 1)
                        epilogue(dve, d, slot(0), hooks)
                    else:
                        out = hooks["sum"]
                        for h in range(2):
                            added.freed(dve, d, h)
                        for q in range(NB):
                            multiplied.after(dve, d, q)
                            v.tensor_tensor(out[:, q, :], out[:, q, :], slot(q), ALU.add).then_inc(added.sem(q), 1)
                dve.drain().then_inc(right_ready.sem(1), RING)
                if not by_dst:
                    hooks["done"](dve)

            @block.gpsimd
            def _(pool):
                hooks["pool"](pool)
        clear_semaphores(nc, s)


def phase_attended(nc, k, x1, x2):
    PER = 9

    def make(s):
        b = {n: s.sb(n, [P, w]) for n, w in (("den", 1), ("stats", 6), ("mv", 2), ("ve", 1), ("sd", 1), ("rs", 1), ("r", D), ("y", D))}
        X = s.sb("X", [P, NB, D])
        xin, varied, rooted, read, finished, stored, chain, passed = (
            s.sem(n) for n in ("xin", "varied", "rooted", "read", "finished", "stored", "chain", "passed"))

        def pool(pool):
            pool.dma_start(X[:, :, :], x1.rearrange("b p n -> p b n")).then_inc(xin, 16)
            with pool.Fori(0, NB) as d:
                pool.wait_ge(finished, d + 1)
                pool.dma_start(x2[ds(d, 1)].rearrange("o p n -> (o p) n"), b["y"][:, :]).then_inc(stored, 16)
            pool.wait_ge(stored, 16 * NB)

        def act(act, d):
            act.wait_ge(varied, d + 1)
            nc.scalar.activation(b["sd"][:, :], b["ve"][:, :], ACT.Sqrt).then_inc(rooted, 1)

        return {"pool": pool, "act": act, "dve": lambda dve: dve.wait_ge(xin, 16), "pe": lambda pe, d: pe.wait_ge(read, d),
                "b": b, "X": X, "varied": varied, "rooted": rooted, "read": read, "finished": finished, "stored": stored,
                "chain": chain, "passed": passed}

    def epilogue(dve, d, po, h):
        v, b = nc.vector, h["b"]
        den, stats, mv, ve, sd, rs, r, y = (b[n][:, :] for n in ("den", "stats", "mv", "ve", "sd", "rs", "r", "y"))
        chain = Chain(dve, h["chain"], d * PER)
        chain(v.tensor_scalar(den, po[:, D:D + 1], 1e-16, None, ALU.add))
        chain(v.reciprocal(den, den))
        chain(v.tensor_scalar(r, po[:, 0:D], den, 0.0, ALU.mult, ALU.max))
        dve.sem_inc(h["read"], 1)
        chain(v.tensor_tensor(r, r, h["X"][:, ds(d, 1), :].rearrange("p a n -> p (a n)"), ALU.add))
        chain(v.bn_stats(stats, r))
        dve.sem_inc(h["passed"], 1)
        chain(v.bn_aggr(mv, stats))
        chain(v.tensor_scalar(ve, mv[:, 1:2], EPS, None, ALU.add))
        dve.sem_inc(h["varied"], 1)
        dve.wait_ge(h["rooted"], d + 1)
        chain(v.reciprocal(rs, sd))
        dve.wait_ge(h["stored"], 16 * d)
        chain(v.tensor_scalar(y, r, mv[:, 0:1], rs, ALU.subtract, ALU.mult))
        assert chain.n == PER, chain.n
        dve.sem_inc(h["finished"], 1)

    phase_weighted(nc, k, "att", True, k["t3"], D + 1, lambda c: k["prob"][:, ds(c, 4)], PER, epilogue, make)


def phase_gated_in(nc, k, table):
    def make(s):
        y = s.sb("y", [P, D])
        read, stored = s.sem("read"), s.sem("stored")

        def pool(pool):
            with pool.Fori(0, NB) as d:
                pool.wait_ge(read, d + 1)
                pool.dma_start(k["cat"][ds(d, 1), :, 0:D].rearrange("o p n -> (o p) n"), y[:, :]).then_inc(stored, 16)
            pool.wait_ge(stored, 16 * NB)

        return {"pool": pool, "act": lambda act, d: None, "dve": lambda dve: None, "pe": lambda pe, d: pe.wait_ge(read, d),
                "y": y, "read": read, "stored": stored}

    def epilogue(dve, d, po, h):
        dve.wait_ge(h["stored"], 16 * d)
        nc.vector.tensor_copy(h["y"][:, :], po).then_inc(h["read"], 1)

    phase_weighted(nc, k, "gin", True, table, D, lambda c: k["edges"][:, ds(c, 4), WIN], 0, epilogue, make)


def phase_gated_out(nc, k, table):
    def make(s):
        out = s.sb("out", [P, NB, D])
        cleared, done, stored = s.sem("cleared"), s.sem("done"), s.sem("stored")

        def start(dve):
            nc.vector.memset(out[:, :, :], 0.0).then_inc(cleared, 1)
            dve.wait_ge(cleared, 1)

        def pool(pool):
            pool.wait_ge(done, 1)
            pool.dma_start(k["cat"][:, :, D:2 * D].rearrange("b p n -> p b n"), out[:, :, :]).then_inc(stored, 16)
            pool.wait_ge(stored, 16)

        return {"pool": pool, "act": lambda act, d: None, "dve": start, "pe": None, "sum": out,
                "done": lambda dve: dve.drain().then_inc(done, 1)}

    phase_weighted(nc, k, "gou", False, table, D, lambda c: k["edges"][:, ds(c, 4), WOUT], 0, None, make)


def phase_gemm(nc, k, tag, src, kc, weights, width, out, out_width, rows, chained, epilogue, prepare=None):
    ctx = ExitStack()
    i0 = 5 * k["gemm_turn"]
    k["gemm_turn"] += 1
    st = k["gemm_steps"]
    with ctx:
        s = Scope(nc, ctx, tag)
        x = s.sb("x", [P, 2, kc * 128])
        xt = s.sb("xt", [128, 2, kc, P])
        w = s.sb("w", [128, kc, width])
        y = s.sb("y", [P, 2, out_width])
        tiles = {name: s.sb(name, [P, vec.shape[-1]]) for name, vec in rows.items()}
        pt = s.ps("pt", [128, 2, 512])
        po = s.ps("po", [128, 2, 512])
        ready, chain_sem, prepared = s.sem("ready"), s.sem("chain"), s.sem("prepared")
        n_ready = 16 * (len(weights) + len(rows))
        with nc.Block() as block:

            @block.sync
            def _(sp):
                for wd, c0, n in weights:
                    sp.dma_start(w[:, :, c0:c0 + n], wd.rearrange("(t c) n -> c t n", c=128)).then_inc(ready, 16)
                load_rows(sp, [(tiles[name], vec) for name, vec in rows.items()], ready)
                with sp.Fori(0, 5) as i:
                    for j in range(5):
                        st["turned"].freed(sp, i + i0, j)
                        sp.dma_start(x[:, j % 2, :], src[ds(5 * i + j, 1)].rearrange("o p n -> (o p) n")).then_inc(st["loaded"].sem(j), 16)

            @block.gpsimd
            def _(pool):
                with pool.Fori(0, 5) as i:
                    for j in range(5):
                        st["finished"].after(pool, i + i0, j)
                        pool.dma_start(out[ds(5 * i + j, 1)].rearrange("o p n -> (o p) n"), y[:, j % 2, :]).then_inc(st["stored"].sem(j), 16)
                for j in range(2):
                    st["stored"].freed(pool, i0 + 5, j)

            @block.scalar
            def _(act):
                with act.Fori(0, 5) as i:
                    for j in range(5):
                        st["turned"].after(act, i + i0, j)
                        st["multiplied"].freed(act, i + i0, j)
                        nc.scalar.copy(xt[:, j % 2, :, :], pt[:, j % 2, 0:kc * 128].rearrange("p (t q) -> p t q", q=128)[:, :, 0:P]
                                       ).then_inc(st["copied"].sem(j), 1)

            @block.tensor
            def _(pe):
                t_ = nc.tensor

                def turn(i, j):
                    st["loaded"].after(pe, i + i0, j)
                    st["copied"].freed(pe, i + i0, j)
                    for t in range(kc):
                        ins = t_.transpose(pt[:, j % 2, 128 * t:128 * t + P], x[:, j % 2, 128 * t:128 * t + 128], k["ident"][0:P, 0:P])
                    ins.then_inc(st["turned"].sem(j), 1)

                def multiply(i, j):
                    st["copied"].after(pe, i + i0, j)
                    st["finished"].freed(pe, i + i0, j)
                    for t in range(kc):
                        ins = t_.matmul(po[0:P, j % 2, 0:width], xt[:, j % 2, t, :], w[:, t, :], start=(t == 0), stop=(t == kc - 1))
                    ins.then_inc(st["multiplied"].sem(j), 1)

                pe.wait_ge(ready, n_ready)
                with pe.Fori(0, 5) as i:
                    turn(i, 0)
                    for j in range(5):
                        if j < 4:
                            turn(i, j + 1)
                        multiply(i, j)

            @block.vector
            def _(dve):
                dve.wait_ge(ready, n_ready)
                if prepare:
                    prepare(dve, y, prepared)
                with dve.Fori(0, 5) as i:
                    for j in range(5):
                        b = 5 * i + j
                        chain = Chain(dve, chain_sem, b * chained)
                        st["multiplied"].after(dve, i + i0, j)
                        st["stored"].freed(dve, i + i0, j)
                        epilogue(dve, chain, b, po[0:P, j % 2, :], y[:, j % 2, :], tiles)
                        assert chain.n == chained, (tag, chain.n)
                        dve.sem_inc(st["finished"].sem(j), 1)
        clear_semaphores(nc, s)


def phase_apply(nc, k, tag, table, width, out, rows, chained, epilogue, resid=None, norm=False):
    ctx = ExitStack()
    i0 = 5 * k["apply_turn"]
    k["apply_turn"] += 1
    st = k["apply_steps"]
    with ctx:
        s = Scope(nc, ctx, tag)
        H = s.sb("H", [P, NB, width])
        T = [s.sb(f"T{h}", [P, NB, P]) for h in range(2)]
        X = s.sb("X", [P, NB, D]) if resid is not None else None
        y = s.sb("y", [P, 2, width])
        tmp = s.sb("tmp", [P, 2, width])
        tiles = {name: s.sb(name, [P, vec.shape[-1]]) for name, vec in rows.items()}
        po = s.ps("po", [128, 2, 512])
        nm = Norm(s) if norm else None
        ready, chain_sem = s.sem("ready"), s.sem("chain")
        n_ready = 16 * (1 + len(rows) + (resid is not None))
        with nc.Block() as block:

            @block.sync
            def _(sp):
                sp.dma_start(H[:, :, :], table.rearrange("b p n -> p b n")).then_inc(ready, 16)
                if resid is not None:
                    sp.dma_start(X[:, :, :], resid.rearrange("b p n -> p b n")).then_inc(ready, 16)
                load_rows(sp, [(tiles[name], vec) for name, vec in rows.items()], ready)
                with sp.Fori(0, 5) as i:
                    for j in range(5):
                        st["summed"].freed(sp, i + i0, j)
                        sp.dma_start(T[j % 2][:, :, :].rearrange("p s q -> p (s q)"),
                                     k["counts"][ds(5 * i + j, 1)].rearrange("o p n -> (o p) n")).then_inc(st["loaded"].sem(j), 16)

            @block.gpsimd
            def _(pool):
                with pool.Fori(0, 5) as i:
                    for j in range(5):
                        st["finished"].after(pool, i + i0, j)
                        pool.dma_start(out[ds(5 * i + j, 1)].rearrange("o p n -> (o p) n"), y[:, j % 2, :]).then_inc(st["stored"].sem(j), 16)
                for j in range(2):
                    st["stored"].freed(pool, i0 + 5, j)

            @block.tensor
            def _(pe):
                pe.wait_ge(ready, n_ready)
                with pe.Fori(0, 5) as i:
                    for j in range(5):
                        st["loaded"].after(pe, i + i0, j)
                        st["finished"].freed(pe, i + i0, j)
                        for q in range(NB):
                            ins = nc.tensor.matmul(po[0:P, j % 2, 0:width], T[j % 2][:, q, :], H[:, q, :],
                                                   start=(q == 0), stop=(q == NB - 1))
                        ins.then_inc(st["summed"].sem(j), 1)

            if norm:
                @block.scalar
                def _(act):
                    with act.Fori(0, 5) as i:
                        for j in range(5):
                            nm.on_act(nc, act, i, j)

            @block.vector
            def _(dve):
                dve.wait_ge(ready, n_ready)
                with dve.Fori(0, 5) as i:
                    for j in range(5):
                        b = 5 * i + j
                        chain = Chain(dve, chain_sem, b * chained)
                        st["summed"].after(dve, i + i0, j)
                        st["stored"].freed(dve, i + i0, j)
                        at = (lambda A: A[:, ds(b, 1), :].rearrange("p a n -> p (a n)"))
                        t = tmp[:, j % 2, :]
                        chain(nc.vector.tensor_tensor(t, po[0:P, j % 2, 0:width], at(H), ALU.add))
                        epilogue(dve, chain, i, j, b, t, y[:, j % 2, :], tiles, at(X) if X is not None else None, nm)
                        assert chain.n == chained, (tag, chain.n)
                        dve.sem_inc(st["finished"].sem(j), 1)
        clear_semaphores(nc, s)


def phase_attention(nc, k, x1, x2):
    with ExitStack() as ctx:
        s = Scope(nc, ctx, "soft")
        k["prob"] = logit = s.sb("prob", [L, NCA])
        greatest = s.sb("greatest", [P, NB])
        diff = s.sb("diff", [L, 2, 2 * G])
        v = nc.vector

        def to_logits(dve, chain, z, g):
            c = G * g
            chain(v.tensor_tensor(z, z, k["edges"][:, ds(c, 2 * G), EDGE], ALU.add))
            chain(v.scalar_tensor_tensor(logit[:, ds(c, 2 * G)], z, 0.01, z, ALU.mult, ALU.max))

        def to_differences(dve, chain, z, g):
            chain(v.tensor_tensor(logit[:, ds(G * g, 2 * G)], logit[:, ds(G * g, 2 * G)], z, ALU.subtract))

        phase_lookup(nc, k, "lhs", SRC, k["hs"][:, :], 3, to_logits)
        phase_greatest(nc, k, logit, greatest[:, :])
        phase_lookup(nc, k, "lmx", DST, greatest[:, :], 2, to_differences)
        done = s.sem("done")
        with nc.Block() as block:

            @block.scalar
            def _(act):
                with act.Fori(0, turns_of(act, k)) as i:
                    n = RING * G
                    nc.scalar.activation(k["prob"][:, ds(n * i, n)], logit[:, ds(n * i, n)], ACT.Exp).then_inc(done, 1)
        clear_semaphores(nc, s)
        phase_attended(nc, k, x1, x2)


def phase_batch_norm(nc, k, x2, gamma, beta):
    ctx = ExitStack()
    with ctx:
        s = Scope(nc, ctx, "bn")
        X, Q = s.sb("X", [P, NB, D]), s.sb("Q", [P, NB, D])
        mean, scale, root = s.sb("mean", [P, D]), s.sb("scale", [P, D]), s.sb("root", [P, D])
        gm, bt = s.sb("gm", [P, D]), s.sb("bt", [P, D])
        pm, pv = s.ps("pm", [P, D]), s.ps("pv", [P, D])
        loaded, meaned, centred, squared, varied, shifted, rooted, chain_sem, done, stored = (
            s.sem(n) for n in ("loaded", "meaned", "centred", "squared", "varied", "shifted", "rooted", "chain", "done", "stored"))
        with nc.Block() as block:

            @block.sync
            def _(sp):
                sp.dma_start(X[:, :, :], x2.rearrange("b p n -> p b n")).then_inc(loaded, 16)
                load_rows(sp, [(gm, gamma), (bt, beta)], loaded)
                sp.wait_ge(done, 1)
                sp.dma_start(k["cat"][:, :, 2 * D:3 * D].rearrange("b p n -> p b n"), Q[:, :, :]).then_inc(stored, 16)
                sp.wait_ge(stored, 16)

            @block.tensor
            def _(pe):
                pe.wait_ge(loaded, 48)
                for q in range(NB):
                    ins = nc.tensor.matmul(pm[:, :], k["ones"][0:P, :], X[:, q, :], start=(q == 0), stop=(q == NB - 1))
                ins.then_inc(meaned, 1)
                pe.wait_ge(squared, 1)
                for q in range(NB):
                    ins = nc.tensor.matmul(pv[:, :], k["ones"][0:P, :], Q[:, q, :], start=(q == 0), stop=(q == NB - 1))
                ins.then_inc(varied, 1)

            @block.scalar
            def _(act):
                act.wait_ge(centred, 1)
                nc.scalar.activation(Q[:, :, :], X[:, :, :], ACT.Square).then_inc(squared, 1)
                act.wait_ge(shifted, 1)
                nc.scalar.activation(root[:, :], scale[:, :], ACT.Sqrt).then_inc(rooted, 1)

            @block.vector
            def _(dve):
                v = nc.vector
                chain = Chain(dve, chain_sem)
                wide = (lambda t: t[:, :].unsqueeze(1).to_broadcast([P, NB, D]))
                dve.wait_ge(loaded, 48)
                dve.wait_ge(meaned, 1)
                chain(v.tensor_scalar(mean[:, :], pm[:, :], 1.0 / N, None, ALU.mult))
                v.tensor_tensor(X[:, :, :], X[:, :, :], wide(mean), ALU.subtract).then_inc(centred, 1)
                dve.wait_ge(varied, 1)
                v.tensor_scalar(scale[:, :], pv[:, :], 1.0 / N, EPS, ALU.mult, ALU.add).then_inc(shifted, 1)
                dve.wait_ge(rooted, 1)
                chain(v.reciprocal(scale[:, :], root[:, :]))
                chain(v.tensor_tensor(scale[:, :], scale[:, :], gm[:, :], ALU.mult))
                chain(v.tensor_tensor(Q[:, :, :], X[:, :, :], wide(scale), ALU.mult))
                v.tensor_tensor(Q[:, :, :], Q[:, :, :], wide(bt), ALU.add).then_inc(done, 1)
        clear_semaphores(nc, s)


def phase_gates(nc, k, x2, w_x2i, b_x2i, w_h2h, x3):
    ctx = ExitStack()
    KC = 3 * D // 128
    with ctx:
        s = Scope(nc, ctx, "upd")
        x = s.sb("x", [P, 2, 3 * D])
        xt = s.sb("xt", [128, 2, KC, P])
        w = s.sb("w", [128, KC, 2 * D])
        X, Hn = s.sb("X", [P, NB, D]), s.sb("Hn", [P, NB, D])
        bias = s.sb("bias", [P, 2 * D])
        pre, gate = s.sb("pre", [P, 2, 2 * D]), s.sb("gate", [P, 2, 2 * D])
        r, y = s.sb("r", [P, 2, D]), s.sb("y", [P, 2, D])
        pt, po = s.ps("pt", [128, 2, 1024]), s.ps("po", [128, 2, 512])
        nm = Norm(s)
        ready, chain_sem = s.sem("ready"), s.sem("chain")
        i0 = 5 * k["gemm_turn"]
        k["gemm_turn"] += 1
        loaded, turned, copied, multiplied, finished, stored = (
            k["gemm_steps"][n].from_turn(i0) for n in ("loaded", "turned", "copied", "multiplied", "finished", "stored"))
        biased, gated = s.steps("biased"), s.steps("gated")
        PER = 5 + Norm.CHAINED
        with nc.Block() as block:

            @block.sync
            def _(sp):
                sp.dma_start(w[:, 0:4, :], w_x2i.rearrange("(t c) n -> c t n", c=128)).then_inc(ready, 16)
                sp.dma_start(w[:, 4:6, :], w_h2h.rearrange("(t c) n -> c t n", c=128)).then_inc(ready, 16)
                load_rows(sp, [(bias, b_x2i)], ready)
                sp.dma_start(X[:, :, :], x2.rearrange("b p n -> p b n")).then_inc(ready, 16)
                sp.dma_start(Hn[:, :, :], k["cat"][:, :, 2 * D:3 * D].rearrange("b p n -> p b n")).then_inc(ready, 16)
                with sp.Fori(0, 5) as i:
                    for j in range(5):
                        turned.freed(sp, i, j)
                        sp.dma_start(x[:, j % 2, :], k["cat"][ds(5 * i + j, 1)].rearrange("o p n -> (o p) n")).then_inc(loaded.sem(j), 16)

            @block.gpsimd
            def _(pool):
                with pool.Fori(0, 5) as i:
                    for j in range(5):
                        finished.after(pool, i, j)
                        pool.dma_start(x3[ds(5 * i + j, 1)].rearrange("o p n -> (o p) n"), y[:, j % 2, :]).then_inc(stored.sem(j), 16)
                for j in range(2):
                    stored.freed(pool, 5, j)

            @block.tensor
            def _(pe):
                t_ = nc.tensor

                def turn(i, j):
                    loaded.after(pe, i, j)
                    copied.freed(pe, i, j)
                    for t in range(KC):
                        ins = t_.transpose(pt[:, j % 2, 128 * t:128 * t + P], x[:, j % 2, 128 * t:128 * t + 128], k["ident"][0:P, 0:P])
                    ins.then_inc(turned.sem(j), 1)

                pe.wait_ge(ready, 80)
                with pe.Fori(0, 5) as i:
                    turn(i, 0)
                    for j in range(5):
                        if j < 4:
                            turn(i, j + 1)
                        copied.after(pe, i, j)
                        biased.freed(pe, i, j)
                        for t in range(KC):
                            ins = t_.matmul(po[0:P, j % 2, :], xt[:, j % 2, t, :], w[:, t, :], start=(t == 0), stop=(t == KC - 1))
                        ins.then_inc(multiplied.sem(j), 1)

            @block.scalar
            def _(act):
                def copy(i, j):
                    turned.after(act, i, j)
                    multiplied.freed(act, i, j)
                    nc.scalar.copy(xt[:, j % 2, :, :], pt[:, j % 2, 0:KC * 128].rearrange("p (t q) -> p t q", q=128)[:, :, 0:P]
                                   ).then_inc(copied.sem(j), 1)

                with act.Fori(0, 5) as i:
                    copy(i, 0)
                    for j in range(5):
                        if j < 4:
                            copy(i, j + 1)
                        biased.after(act, i, j)
                        finished.freed(act, i, j)
                        nc.scalar.activation(gate[:, j % 2, 0:D], pre[:, j % 2, 0:D], ACT.Sigmoid)
                        nc.scalar.activation(gate[:, j % 2, D:2 * D], pre[:, j % 2, D:2 * D], ACT.Tanh).then_inc(gated.sem(j), 1)
                        nm.on_act(nc, act, i, j)

            @block.vector
            def _(dve):
                v = nc.vector
                dve.wait_ge(ready, 80)
                with dve.Fori(0, 5) as i:
                    for j in range(5):
                        b, h = 5 * i + j, j % 2
                        chain = Chain(dve, chain_sem, b * PER)
                        at = (lambda A: A[:, ds(b, 1), :].rearrange("p a n -> p (a n)"))
                        multiplied.after(dve, i, j)
                        gated.freed(dve, i, j)
                        chain(v.tensor_tensor(pre[:, h, :], po[0:P, h, :], bias[:, :], ALU.add))
                        dve.sem_inc(biased.sem(j), 1)
                        gated.after(dve, i, j)
                        new = gate[:, h, D:2 * D]
                        chain(v.tensor_tensor(r[:, h, :], at(Hn), new, ALU.subtract))
                        chain(v.tensor_tensor(r[:, h, :], r[:, h, :], gate[:, h, 0:D], ALU.mult))
                        chain(v.tensor_tensor(r[:, h, :], r[:, h, :], new, ALU.add))
                        chain(v.tensor_tensor(r[:, h, :], r[:, h, :], at(X), ALU.add))
                        stored.freed(dve, i, j)
                        nm.on_dve(nc, dve, chain, i, j, r[:, h, :], y[:, h, :])
                        assert chain.n == PER
                        dve.sem_inc(finished.sem(j), 1)
        clear_semaphores(nc, s)


def phase_decoder(nc, k, h3, w_lin, b_lin, w_dec1, b_dec1, w_dec2, b_dec2, x3, out):
    ctx = ExitStack()
    HID0, HID1 = w_lin.shape
    with ctx:
        s = Scope(nc, ctx, "dec")
        x = s.sb("x", [P, 2, HID0])
        ht, zt, dt = s.sb("ht", [HID0, 2, P]), s.sb("zt", [HID1, 2, P]), s.sb("dt", [HID0, 2, P])
        wl, w1, w2 = s.sb("wl", [HID0, HID1]), s.sb("w1", [HID1, HID0]), s.sb("w2", [HID0, D])
        bl, b1, b2 = s.sb("bl", [HID1, 1]), s.sb("b1", [HID0, 1]), s.sb("b2", [P, D])
        X = s.sb("X", [P, NB, D])
        r, y = s.sb("r", [P, 2, D]), s.sb("y", [P, 2, D])
        pt, pz, pd, po = (s.ps(n, [128, 2, 512]) for n in ("pt", "pz", "pd", "po"))
        nm = Norm(s)
        ready, chain_sem = s.sem("ready"), s.sem("chain")
        i0 = 5 * k["gemm_turn"]
        k["gemm_turn"] += 1
        loaded, turned, copied, multiplied, finished, stored = (
            k["gemm_steps"][n].from_turn(i0) for n in ("loaded", "turned", "copied", "multiplied", "finished", "stored"))
        lined, z_ready, decoded, d_ready = (s.steps(n) for n in ("lined", "z_ready", "decoded", "d_ready"))
        PER = 2 + Norm.CHAINED
        with nc.Block() as block:

            @block.sync
            def _(sp):
                sp.dma_start(wl[:, :], w_lin).then_inc(ready, 16)
                sp.dma_start(w1[:, :], w_dec1).then_inc(ready, 16)
                sp.dma_start(w2[:, :], w_dec2).then_inc(ready, 16)
                sp.dma_start(bl[:, :], b_lin.unsqueeze(1)).then_inc(ready, 16)
                sp.dma_start(b1[:, :], b_dec1.unsqueeze(1)).then_inc(ready, 16)
                load_rows(sp, [(b2, b_dec2)], ready)
                sp.dma_start(X[:, :, :], x3.rearrange("b p n -> p b n")).then_inc(ready, 16)
                with sp.Fori(0, 5) as i:
                    for j in range(5):
                        turned.freed(sp, i, j)
                        sp.dma_start(x[:, j % 2, :], h3[ds(5 * i + j, 1)].rearrange("o p n -> (o p) n")).then_inc(loaded.sem(j), 16)

            @block.gpsimd
            def _(pool):
                with pool.Fori(0, 5) as i:
                    for j in range(5):
                        finished.after(pool, i, j)
                        pool.dma_start(out[ds(5 * i + j, 1)].rearrange("o p n -> (o p) n"), y[:, j % 2, :]).then_inc(stored.sem(j), 16)
                for j in range(2):
                    stored.freed(pool, 5, j)

            @block.tensor
            def _(pe):
                t_ = nc.tensor

                def turn(i, j):
                    loaded.after(pe, i, j)
                    copied.freed(pe, i, j)
                    t_.transpose(pt[:, j % 2, 0:P], x[:, j % 2, :], k["ident"][0:P, 0:P]).then_inc(turned.sem(j), 1)

                pe.wait_ge(ready, 16 * 7)
                with pe.Fori(0, 5) as i:
                    turn(i, 0)
                    for j in range(5):
                        h = j % 2
                        if j < 4:
                            turn(i, j + 1)
                        copied.after(pe, i, j)
                        z_ready.freed(pe, i, j)
                        t_.matmul(pz[0:HID1, h, 0:P], wl[:, :], ht[:, h, :], start=True, stop=True).then_inc(lined.sem(j), 1)
                        z_ready.after(pe, i, j)
                        d_ready.freed(pe, i, j)
                        t_.matmul(pd[0:HID0, h, 0:P], w1[:, :], zt[:, h, :], start=True, stop=True).then_inc(decoded.sem(j), 1)
                        d_ready.after(pe, i, j)
                        finished.freed(pe, i, j)
                        t_.matmul(po[0:P, h, 0:D], dt[:, h, :], w2[:, :], start=True, stop=True).then_inc(multiplied.sem(j), 1)

            @block.scalar
            def _(act):
                act.wait_ge(ready, 16 * 7)
                with act.Fori(0, 5) as i:
                    for j in range(5):
                        h = j % 2
                        turned.after(act, i, j)
                        lined.freed(act, i, j)
                        nc.scalar.copy(ht[:, h, :], pt[:, h, 0:P]).then_inc(copied.sem(j), 1)
                        lined.after(act, i, j)
                        decoded.freed(act, i, j)
                        nc.scalar.activation(zt[:, h, :], pz[0:HID1, h, 0:P], ACT.Identity, bias=bl[:, :]).then_inc(z_ready.sem(j), 1)
                        decoded.after(act, i, j)
                        multiplied.freed(act, i, j)
                        nc.scalar.activation(dt[:, h, :], pd[0:HID0, h, 0:P], ACT.Relu, bias=b1[:, :]).then_inc(d_ready.sem(j), 1)
                        nm.on_act(nc, act, i, j)

            @block.vector
            def _(dve):
                v = nc.vector
                dve.wait_ge(ready, 16 * 7)
                with dve.Fori(0, 5) as i:
                    for j in range(5):
                        b, h = 5 * i + j, j % 2
                        chain = Chain(dve, chain_sem, b * PER)
                        multiplied.after(dve, i, j)
                        chain(v.tensor_tensor(r[:, h, :], po[0:P, h, 0:D], b2[:, :], ALU.add))
                        chain(v.tensor_tensor(r[:, h, :], r[:, h, :], X[:, ds(b, 1), :].rearrange("p a n -> p (a n)"), ALU.add))
                        stored.freed(dve, i, j)
                        nm.on_dve(nc, dve, chain, i, j, r[:, h, :], y[:, h, :])
                        assert chain.n == PER
                        dve.sem_inc(finished.sem(j), 1)
        clear_semaphores(nc, s)


def build_program(nc, a, out):
    ctx = ExitStack()
    with ctx:
        s = Scope(nc, ctx, "all")

        def dram(name, shape):
            return nc.dram_tensor(name, shape, fp32).ap()

        k = {
            "iota": s.sb("iota", [128, P]), "iota_bf": s.sb("iota_bf", [128, P], bf16),
            "ones": s.sb("ones", [128, P]), "zeros_bf": s.sb("zeros_bf", [128, 512], bf16),
            "ident": s.sb("ident", [128, 128]),
            "group_start": s.sb("group_start", [1, 32], i32), "tile_at": s.sb("tile_at", [1, NCA], i32),
            "parts_at": [s.sb(f"parts_at{f}", [1, NCA], i32) for f in (SRC, DST)],
            "dinv": s.sb("dinv", [P, NB]), "hs": s.sb("hs", [P, NB]),
            "hot": nc.dram_tensor("hot", [NGA, L, 2, G * P], bf16).ap(), "slots": dram("slots", [L, NCA, F]), "key_rows": dram("key_rows", [EC, P]), "dblk_rows": dram("dblk_rows", [EC, P]),
            "counts": dram("counts", [NB, P, NB * P]), "hs_row": dram("hs_row", [NB, P]),
            "table": dram("table", [NB, P, 2 * D]), "cat": dram("cat", [NB, P, 3 * D]),
            "columns": 8, "sent": s.steps("sent", 2, 2, 16 * 8), "gemm_turn": 0, "apply_turn": 0,
        }
        k["gemm_steps"] = {n: s.steps(f"gemm_{n}", amount=16 if n in ("loaded", "stored") else 1)
                           for n in ("loaded", "turned", "copied", "multiplied", "finished", "stored")}
        k["apply_steps"] = {n: s.steps(f"apply_{n}", amount=16 if n in ("loaded", "stored") else 1)
                            for n in ("loaded", "summed", "finished", "stored")}
        x0 = a["x"].rearrange("(b p) n -> b p n", p=P)
        t1, t2, t3 = dram("t1", [NB, P, D]), dram("t2", [NB, P, D]), dram("t3", [NB, P, D + 1])
        h1, x1, x2, x3 = (dram(n, [NB, P, D]) for n in ("h1", "x1", "x2", "x3"))
        k["t3"] = t3
        t4, h3 = dram("t4", [NB, P, DE]), dram("h3", [NB, P, DE])
        v = nc.vector

        phase_order(nc, k, a["src"], a["dst"], a["edge_weight"], a["edge_weight_n2"], a["edge_attr_128"],
                    a["L1_gnn_We"], a["L1_gnn_be"], a["L1_gnn_attn"])
        with ExitStack() as inner:
            k["edges"] = inner.enter_context(nc.sbuf_tensor("edges", [L, NCA, F], fp32))
            phase_adjacency(nc, k)

            def scaled(width):
                def epilogue(dve, chain, b, po, y, tiles):
                    chain(v.tensor_scalar(y, po[:, 0:width], k["dinv"][:, ds(b, 1)], None, ALU.mult))
                return epilogue

            def hidden(dve, chain, i, j, b, t, y, tiles, x, nm):
                chain(v.tensor_scalar(y, t, k["dinv"][:, ds(b, 1)], 0.0, ALU.mult, ALU.max))

            def normed(dve, chain, i, j, b, t, y, tiles, x, nm):
                chain(v.scalar_tensor_tensor(t, t, k["dinv"][:, ds(b, 1)], x, ALU.mult, ALU.add))
                nm.on_dve(nc, dve, chain, i, j, t, y)

            phase_gemm(nc, k, "w1", x0, 2, [(a["L0_gnn_W1"], 0, D)], D, t1, D, {}, 1, scaled(D))
            phase_apply(nc, k, "c1", t1, D, h1, {}, 2, hidden)
            phase_gemm(nc, k, "w2", h1, 2, [(a["L0_gnn_W2"], 0, D)], D, t2, D, {}, 1, scaled(D))
            phase_apply(nc, k, "c2", t2, D, x1, {}, 2 + Norm.CHAINED, normed, resid=x0, norm=True)

            def with_logit(dve, chain, b, po, y, tiles):
                chain(v.tensor_tensor(y[:, 0:D], po[:, 0:D], tiles["bn"][:, :], ALU.add))
                chain(v.scalar_tensor_tensor(po[:, 0:D], y[:, 0:D], 1.0, tiles["attn"][:, :], ALU.mult, ALU.mult,
                                             accum_out=k["hs"][:, ds(b, 1)]))

            def ones_column(dve, y, sem):
                for h in range(2):
                    v.memset(y[:, h, D:D + 1], 1.0).then_inc(sem, 1)
                dve.wait_ge(sem, 2)

            phase_gemm(nc, k, "wn", x1, 2, [(a["L1_gnn_WnT"], 0, D)], D, t3, D + 1,
                       {"bn": a["L1_gnn_bn"], "attn": a["L1_gnn_attn"].rearrange("o h n -> (o h n)")}, 2, with_logit, ones_column)
            wide = k["table"]
            phase_attention(nc, k, x1, x2)

            phase_batch_norm(nc, k, x2, a["L2_gnn_gamma"], a["L2_gnn_beta"])

            def biased(dve, chain, b, po, y, tiles):
                chain(v.tensor_tensor(y[:, 0:D], po[:, 0:D], tiles["bi"][:, :], ALU.add))
                chain(v.tensor_tensor(y[:, D:2 * D], po[:, D:2 * D], tiles["bo"][:, :], ALU.add))

            phase_gemm(nc, k, "wio", k["cat"][:, :, 2 * D:3 * D], 2, [(a["L2_gnn_W_in"], 0, D), (a["L2_gnn_W_out"], D, D)], 2 * D,
                       wide, 2 * D, {"bi": a["L2_gnn_b_in"], "bo": a["L2_gnn_b_out"]}, 2, biased)
            phase_gated_in(nc, k, wide[:, :, 0:D])
            phase_gated_out(nc, k, wide[:, :, D:2 * D])
        phase_gates(nc, k, x2, a["L2_gnn_W_x2i"], a["L2_gnn_b_x2i"], a["L2_gnn_W_h2h"], x3)

        def relued(dve, chain, i, j, b, t, y, tiles, x, nm):
            chain(v.scalar_tensor_tensor(t, t, k["dinv"][:, ds(b, 1)], tiles["bc"][:, :], ALU.mult, ALU.add))
            chain(v.tensor_scalar(y, t, 0.0, None, ALU.max))

        phase_gemm(nc, k, "wc", x3, 2, [(a["L3_gnn_W_conv"], 0, DE)], DE, t4, DE, {}, 1, scaled(DE))
        phase_apply(nc, k, "c3", t4, DE, h3, {"bc": a["L3_gnn_b_conv"]}, 3, relued)
        phase_decoder(nc, k, h3, a["L3_gnn_W_lin"], a["L3_gnn_b_lin"], a["L3_gnn_W_dec1"], a["L3_gnn_b_dec1"],
                      a["L3_gnn_W_dec2"], a["L3_gnn_b_dec2"], x3, out.rearrange("(b p) n -> b p n", p=P))


_INS = ['x', 'src', 'dst', 'edge_attr_128', 'edge_weight', 'edge_weight_n2', 'L0_gnn_W1', 'L0_gnn_W2', 'L1_gnn_Wn',
        'L1_gnn_bn', 'L1_gnn_We', 'L1_gnn_be', 'L1_gnn_attn', 'L2_gnn_gamma', 'L2_gnn_beta', 'L2_gnn_W_in', 'L2_gnn_b_in',
        'L2_gnn_W_out', 'L2_gnn_b_out', 'L2_gnn_W_x2i', 'L2_gnn_b_x2i', 'L2_gnn_W_h2h', 'L3_gnn_W_conv', 'L3_gnn_b_conv',
        'L3_gnn_W_lin', 'L3_gnn_b_lin', 'L3_gnn_W_dec1', 'L3_gnn_b_dec1', 'L3_gnn_W_dec2', 'L3_gnn_b_dec2']


def kernel(**inputs):
    import numpy as _np
    import concourse.bacc as _bacc
    from concourse import mybir as _mybir
    from concourse.bass_utils import run_bass_kernel_spmd as _run

    nc = _bacc.Bacc("TRN2", target_bir_lowering=False, num_devices=1)
    arrays, args = {}, {}
    for name in _INS:
        a = _np.asarray(inputs[name])
        if name == 'L1_gnn_Wn':
            name, a = 'L1_gnn_WnT', a.T
        a = _np.ascontiguousarray(a)
        arrays[f"in_{name}_dram"] = a
        args[name] = nc.dram_tensor(f"in_{name}_dram", a.shape, _mybir.dt.from_np(a.dtype), kind="ExternalInput").ap()
    out = nc.dram_tensor("out_0_dram", (N, D), _mybir.dt.float32, kind="ExternalOutput").ap()
    build_program(nc, args, out)
    r = _run(nc, [arrays], core_ids=[0])
    return r.results[0]["out_0_dram"]
```

```python
import concourse.bass as bass
from concourse import mybir
from contextlib import ExitStack

fp32 = mybir.dt.float32
bf16 = mybir.dt.bfloat16
i32 = mybir.dt.int32
ALU = mybir.AluOpType
ACT = mybir.ActivationFunctionType
AX = mybir.AxisListType
ds = bass.ds

N = 3125
E = 100000
D = 256
DE = 128
P = 125
NB = N // P
EC = E // P
L = 128
BUCKETS = NB * NB
G = 8
RING = 4
PARTS = 4
W = G // PARTS
NC = (E + BUCKETS * (L - 1)) // L + (G - 1) * NB
NC = -(-NC // G) * G
NG = NC // G
NT = -(-NG // RING)
NGA = (NT + 1) * RING
NCA = NGA * G
F = 8
SRC, DST, WIN, WOUT, EDGE = range(5)
TS = 128
BIG = 1.0e30
MAGIC = 12582912.0
EPS = 1e-5


class Steps:

    def __init__(self, sems, unroll, amount=1, i0=0, head=0):
        self.sems, self.unroll, self.amount, self.i0, self.head = sems, unroll, amount, i0, head

    def begin(self, eng):
        if self.i0 == 0:
            for sem in self.sems:
                eng.sem_inc(sem, self.head)

    def begin_with_dma(self, pool, k):
        if self.i0 == 0:
            for sem in self.sems:
                pool.dma_start(k["spare"][k["spare_rows"]:k["spare_rows"] + 1, :], k["ones"][0:1, :]).then_inc(sem, self.head)
                k["spare_rows"] += 1

    def from_turn(self, i0):
        return Steps(self.sems, self.unroll, self.amount, i0, self.head)

    def sem(self, j):
        return self.sems[j % len(self.sems)]

    def _count(self, i, j):
        s = len(self.sems)
        return (i + self.i0) * len(range(j % s, self.unroll, s)) + j // s

    def after(self, eng, i, j):
        eng.wait_ge(self.sem(j), (self._count(i, j) + 1) * self.amount + self.head)

    def freed(self, eng, i, j):
        eng.wait_ge(self.sem(j), self._count(i, j) * self.amount + self.head)


class Chain:

    def __init__(self, eng, sem, start=0):
        self.eng, self.sem, self.start, self.n = eng, sem, start, 0

    def __call__(self, ins):
        self.n += 1
        ins.then_inc(self.sem, 1)
        self.eng.wait_ge(self.sem, self.start + self.n)


class Scope:

    def __init__(self, nc, ctx, tag):
        self.nc, self.ctx, self.tag = nc, ctx, tag
        self.sems = []
        self.regs = {}

    def sb(self, name, shape, dt=fp32):
        return self.ctx.enter_context(self.nc.sbuf_tensor(f"{self.tag}_{name}", shape, dt))

    def ps(self, name, shape, dt=fp32):
        return self.ctx.enter_context(self.nc.psum_tensor(f"{self.tag}_{name}", shape, dt))

    def sem(self, name):
        self.sems.append(self.ctx.enter_context(self.nc.semaphore(f"{self.tag}_{name}")))
        return self.sems[-1]

    def registers(self, eng, name):
        if (eng, name) not in self.regs:
            self.regs[eng, name] = [self.ctx.enter_context(eng.register(f"{self.tag}_{name}{n}")) for n in range(G)]
        return self.regs[eng, name]

    def steps(self, name, slots=2, unroll=5, amount=1, head=0):
        return Steps([self.sem(f"{name}{s}") for s in range(slots)], unroll, amount, head=head)


def clear_semaphores(nc, scope):
    with nc.Block() as block:

        @block.gpsimd
        def _(pool):
            for sem in scope.sems:
                pool.sem_clear(sem)


def phase_order(nc, k, src, dst, w_in, w_out, edge_attr, we, be, attn):
    ctx = ExitStack()
    with ctx:
        s = Scope(nc, ctx, "ord")
        sblk, dblk = s.sb("sblk", [P, EC]), s.sb("dblk", [P, EC])
        key = s.sb("key", [P, EC])
        pay = s.sb("pay", [P, EC, 4])
        base = s.sb("base", [NB, NB])
        attnc = s.sb("attnc", [128, 2])
        attnb = s.sb("attnb", [128, 2, P])
        we_sb = s.sb("we_sb", [128, 2, DE])
        bec = s.sb("bec", [128, 2])
        vrow = s.sb("vrow", [P, DE])
        becol = s.sb("becol", [P, 1])
        tri = s.sb("tri", [P, P])
        ptri = s.sb("ptri", [NB, 32])
        iop = s.sb("iop", [128, 1])
        io25 = s.sb("io25", [P, NB])

        with ExitStack() as inner:
            a = Scope(nc, inner, "cnt")
            raws, rawd = a.sb("raws", [P, EC], i32), a.sb("rawd", [P, EC], i32)
            win, wout = a.sb("win", [P, EC]), a.sb("wout", [P, EC])
            node = a.sb("node", [P, EC])
            tmp = a.sb("tmp", [P, EC])
            ohs, ohd = a.sb("ohs", [P, EC, NB], bf16), a.sb("ohd", [P, EC, NB], bf16)
            empty = a.sb("empty", [128, NCA // 12, F])
            keyt = a.sb("keyt", [100, 2, 8, P])
            m4 = a.sb("m4", [4 * NB, 4 * NB])
            tot = a.sb("tot", [NB, NB])
            nch = a.sb("nch", [NB, NB])
            inc = a.sb("inc", [NB, NB])
            one25 = a.sb("one25", [NB, NB])
            grp = a.sb("grp", [NB, 1])
            g0 = a.sb("g0", [NB, 1])
            turns = a.sb("turns", [1, 1])
            first = a.sb("first", [NB, NB])
            ioc = a.sb("ioc", [NB, NCA])
            acc = a.sb("acc", [NB, NCA])
            row = a.sb("row", [1, NCA])
            rq = a.sb("rq", [1, NCA])
            pT = a.ps("pT", [128, 16, 128])
            pM = a.ps("pM", [128, 512])
            pK = a.ps("pK", [128, 512])
            pR = a.ps("pR", [128, 1024])
            loaded, consts, filled = a.sem("loaded"), a.sem("consts"), a.sem("filled")
            dve_chain, keyed, hot, turned = a.sem("dve_chain"), a.sem("keyed"), a.sem("hot"), a.sem("turned")
            copied, stored, counted, summed, m4ed = (a.sem(n) for n in ("copied", "stored", "counted", "summed", "m4ed"))
            grouped, prefixed, listed, rowed, packed = (a.sem(n) for n in ("grouped", "prefixed", "listed", "rowed", "packed"))
            spread, vdone = a.sem("spread"), a.sem("vdone")
            pool_chain = a.sem("pool_chain")
            with nc.Block() as block:

                @block.sync
                def _(sp):
                    sp.dma_start(raws[:, :], src.rearrange("(p c) -> p c", p=P)).then_inc(loaded, 16)
                    sp.dma_start(rawd[:, :], dst.rearrange("(p c) -> p c", p=P)).then_inc(loaded, 16)
                    sp.dma_start(win[:, :], w_in.rearrange("(p c) -> p c", p=P)).then_inc(loaded, 16)
                    sp.dma_start(wout[:, :], w_out.rearrange("(p c) -> p c", p=P)).then_inc(loaded, 16)
                    sp.dma_start(attnc[:, :], attn.rearrange("o h (t c) -> c (o h t)", t=2),
                                 allow_slow_non_contiguous=True).then_inc(loaded, 16)
                    sp.dma_start(bec[:, :], be.rearrange("(t c) -> c t", t=2),
                                 allow_slow_non_contiguous=True).then_inc(loaded, 16)
                    sp.dma_start(we_sb[:, :, :], we.rearrange("(t c) k -> c t k", t=2)).then_inc(loaded, 16)
                    sp.wait_ge(filled, 1)
                    for q in range(12):
                        w = NCA // 12
                        sp.dma_start(k["slots"][:, q * w:(q + 1) * w, :], empty[:, :, :]).then_inc(stored, 16)
                    sp.wait_ge(copied, 2)
                    for t, name in enumerate(("key_rows", "dblk_rows")):
                        sp.dma_start(k[name].rearrange("(q c) p -> c q p", q=8),
                                     keyt[:, t, :, :]).then_inc(stored, 16)
                    sp.wait_ge(stored, 14 * 16)

                @block.gpsimd
                def _(pool):
                    def made(ins):
                        ins.then_inc(consts, 1)

                    made(nc.gpsimd.iota(k["iota"][:, :], [[1, P]], 0, 0, allow_small_or_imprecise_dtypes=True))
                    made(nc.gpsimd.iota(k["iota_bf"][:, :], [[1, P]], 0, 0, allow_small_or_imprecise_dtypes=True))
                    made(nc.gpsimd.iota(iop[:, :], [[0, 1]], 0, 1, allow_small_or_imprecise_dtypes=True))
                    made(nc.gpsimd.iota(io25[:, :], [[1, NB]], 0, 0, allow_small_or_imprecise_dtypes=True))
                    made(nc.gpsimd.iota(ioc[:, :], [[1, NCA]], 0, 0, allow_small_or_imprecise_dtypes=True))
                    made(nc.gpsimd.memset(k["ones"][:, :], 1.0))
                    made(nc.gpsimd.memset(one25[:, :], 1.0))
                    made(nc.gpsimd.memset(k["zeros_bf"][:, :], 0.0))
                    made(nc.gpsimd.memset(acc[:, :], 0.0))
                    nc.gpsimd.memset(empty[:, :, :], -1.0).then_inc(filled, 1)
                    nc.gpsimd.memset(k["ident"][:, :], 0.0).then_inc(pool_chain, 1)
                    nc.gpsimd.memset(tri[:, :], 1.0).then_inc(pool_chain, 1)
                    nc.gpsimd.memset(ptri[:, :], 1.0).then_inc(pool_chain, 1)
                    pool.wait_ge(pool_chain, 3)
                    made(nc.gpsimd.affine_select(out=k["ident"][:, :], in_=k["ident"][:, :], compare_op=ALU.not_equal,
                                                 fill=1.0, base=0, pattern=[[-1, 128]], channel_multiplier=1))
                    made(nc.gpsimd.affine_select(out=tri[:, :], in_=tri[:, :], compare_op=ALU.is_gt,
                                                 fill=0.0, base=0, pattern=[[-1, P]], channel_multiplier=1))
                    made(nc.gpsimd.affine_select(out=ptri[:, :], in_=ptri[:, :], compare_op=ALU.is_gt,
                                                 fill=0.0, base=0, pattern=[[1, 32]], channel_multiplier=-1))

                @block.vector
                def _(dve):
                    chain = Chain(dve, dve_chain)
                    v = nc.vector
                    dve.wait_ge(loaded, 7 * 16)
                    dve.wait_ge(consts, 12)
                    for t in range(2):
                        ins = v.tensor_scalar(attnb[:, t, :], k["ones"][:, :], attnc[:, t:t + 1], None, ALU.mult)
                    ins.then_inc(spread, 1)
                    for raw, blk, f in ((raws, sblk, SRC), (rawd, dblk, DST)):
                        chain(v.tensor_copy(node[:, :], raw[:, :]))
                        chain(v.tensor_scalar(tmp[:, :], node[:, :], -float(P // 2), 1.0 / P, ALU.add, ALU.mult))
                        chain(v.tensor_scalar(tmp[:, :], tmp[:, :], MAGIC, None, ALU.add))
                        chain(v.tensor_scalar(blk[:, :], tmp[:, :], -MAGIC, None, ALU.add))
                        chain(v.scalar_tensor_tensor(pay[:, :, f], blk[:, :], -float(P), node[:, :], ALU.mult, ALU.add))
                    v.scalar_tensor_tensor(key[:, :], dblk[:, :], float(NB), sblk[:, :], ALU.mult, ALU.add).then_inc(keyed, 1)
                    for blk, oh in ((sblk, ohs), (dblk, ohd)):
                        v.tensor_tensor(oh[:, :, :], blk[:, :].unsqueeze(2).to_broadcast([P, EC, NB]),
                                        io25[:, :].unsqueeze(1).to_broadcast([P, EC, NB]), ALU.is_equal).then_inc(hot, 1)
                    dve.wait_ge(counted, 1)
                    v.tensor_copy(m4[:, :], pM[0:4 * NB, 0:4 * NB]).then_inc(m4ed, 1)
                    dve.wait_ge(summed, 1)
                    chain(v.tensor_copy(tot[:, :], pK[0:NB, 0:NB]))
                    chain(v.tensor_scalar(nch[:, :], tot[:, :], (L - 1) / 2.0, 1.0 / L, ALU.add, ALU.mult))
                    chain(v.tensor_scalar(nch[:, :], nch[:, :], MAGIC, None, ALU.add))
                    chain(v.tensor_scalar(nch[:, :], nch[:, :], -MAGIC, None, ALU.add))
                    chain(v.tensor_tensor_scan(inc[:, :], one25[:, :], nch[:, :], 0.0, ALU.mult, ALU.add))
                    chain(v.tensor_scalar(grp[:, :], inc[:, NB - 1:NB], (G - 1) / 2.0, 1.0 / G, ALU.add, ALU.mult))
                    chain(v.tensor_scalar(grp[:, :], grp[:, :], MAGIC, None, ALU.add))
                    chain(v.tensor_scalar(grp[:, :], grp[:, :], -MAGIC, None, ALU.add))
                    v.tensor_scalar(grp[:, :], grp[:, :], 2.0, None, ALU.max).then_inc(grouped, 1)
                    dve.wait_ge(prefixed, 1)
                    chain(v.tensor_copy(k["group_start"][0:1, 0:NB + 1], pK[0:1, 128:128 + NB + 1]))
                    chain(v.tensor_scalar(turns[:, :], pK[0:1, 128 + NB:129 + NB], (RING - 1) / 2.0, 1.0 / RING, ALU.add, ALU.mult))
                    chain(v.tensor_scalar(turns[:, :], turns[:, :], MAGIC, None, ALU.add))
                    chain(v.tensor_scalar(k["group_start"][0:1, 30:31], turns[:, :], -MAGIC, None, ALU.add))
                    chain(v.tensor_copy(g0[:, :], pK[0:NB, 256:257]))
                    chain(v.tensor_tensor(first[:, :], inc[:, :], nch[:, :], ALU.subtract))
                    chain(v.scalar_tensor_tensor(first[:, :], g0[:, :].to_broadcast([NB, NB]), float(G), first[:, :], ALU.mult, ALU.add))
                    chain(v.tensor_scalar(base[:, :], first[:, :], float(L), None, ALU.mult))
                    for q in range(NB):
                        chain(v.scalar_tensor_tensor(acc[:, :], ioc[:, :], first[:, q:q + 1], acc[:, :], ALU.is_ge, ALU.add))
                    dve.sem_inc(listed, 1)
                    dve.wait_ge(vdone, 1)
                    chain(v.tensor_copy(vrow[:, :], pK[0:P, 384:512]))
                    chain(v.tensor_copy(becol[:, :], pM[0:P, 256:257]))
                    for h in range(4):
                        w = NCA // 4
                        dve.wait_ge(rowed, h + 1)
                        chain(v.tensor_copy(row[:, h * w:(h + 1) * w], pR[0:1, (h % 2) * 512:(h % 2) * 512 + w]))
                        dve.sem_inc(packed, 1)
                    chain(v.tensor_scalar(row[:, :], row[:, :], -1.0, None, ALU.add))
                    chain(v.tensor_scalar(rq[:, :], row[:, :], -float(NB // 2), 1.0 / NB, ALU.add, ALU.mult))
                    chain(v.tensor_scalar(rq[:, :], rq[:, :], MAGIC, None, ALU.add))
                    chain(v.tensor_scalar(rq[:, :], rq[:, :], -MAGIC, None, ALU.add))
                    chain(v.scalar_tensor_tensor(row[:, :], rq[:, :], -float(NB), row[:, :], ALU.mult, ALU.add))
                    chain(v.tensor_scalar(k["tile_at"][:, :], row[:, :], float(TS), None, ALU.mult))
                    chain(v.tensor_scalar(k["parts_at"][SRC][:, :], row[:, :], 3.0, None, ALU.mult))
                    chain(v.tensor_scalar(k["parts_at"][DST][:, :], rq[:, :], 3.0, None, ALU.mult))

                @block.scalar
                def _(act):
                    act.wait_ge(loaded, 7 * 16)
                    nc.scalar.copy(pay[:, :, WIN], win[:, :])
                    nc.scalar.copy(pay[:, :, WOUT], wout[:, :])
                    for t in range(2):
                        act.wait_ge(turned, t + 1)
                        nc.scalar.copy(keyt[:, t, :, :], pT[0:100, 8 * t:8 * t + 8, 0:P]).then_inc(copied, 1)

                @block.tensor
                def _(pe):
                    t_ = nc.tensor
                    pe.wait_ge(spread, 1)
                    for t in range(2):
                        t_.matmul(pK[0:P, 384:512], attnb[:, t, :], we_sb[:, t, :], start=(t == 0), stop=(t == 1))
                    for t in range(2):
                        ins = t_.matmul(pM[0:P, 256:257], attnb[:, t, :], bec[:, t:t + 1], start=(t == 0), stop=(t == 1))
                    ins.then_inc(vdone, 1)
                    pe.wait_ge(keyed, 1)
                    for t, what in enumerate((key, dblk)):
                        for q in range(8):
                            ins = t_.transpose(pT[0:100, 8 * t + q, 0:P], what[:, 100 * q:100 * q + 100], k["ident"][0:P, 0:P])
                        ins.then_inc(turned, 1)
                    pe.wait_ge(hot, 2)
                    t_.matmul(pM[0:4 * NB, 0:4 * NB], k["zeros_bf"][0:P, 0:4 * NB], k["zeros_bf"][0:P, 0:4 * NB],
                              start=True, stop=False, skip_group_check=True)
                    with pe.Fori(0, EC // 8) as i:
                        for j in range(2):
                            c = 8 * i + 4 * j
                            t_.matmul(pM[0:4 * NB, 0:4 * NB], ohd[:, ds(c, 4), :].rearrange("p a b -> p (a b)"),
                                      ohs[:, ds(c, 4), :].rearrange("p a b -> p (a b)"),
                                      start=False, stop=False, skip_group_check=True)
                    t_.matmul(pM[0:4 * NB, 0:4 * NB], k["zeros_bf"][0:P, 0:4 * NB], k["zeros_bf"][0:P, 0:4 * NB],
                              start=False, stop=True, skip_group_check=True).then_inc(counted, 1)
                    pe.wait_ge(m4ed, 1)
                    for j in range(4):
                        ins = t_.matmul(pK[0:NB, 0:NB], k["ident"][0:4 * NB, NB * j:NB * j + NB],
                                        m4[:, NB * j:NB * j + NB], start=(j == 0), stop=(j == 3))
                    ins.then_inc(summed, 1)
                    pe.wait_ge(grouped, 1)
                    t_.matmul(pK[0:1, 128:128 + NB + 1], grp[:, :], ptri[:, 0:NB + 1], start=True, stop=True)
                    t_.matmul(pK[0:NB, 256:257], ptri[:, 0:NB], grp[:, :], start=True, stop=True).then_inc(prefixed, 1)
                    pe.wait_ge(listed, 1)
                    for h in range(4):
                        w = NCA // 4
                        if h >= 2:
                            pe.wait_ge(packed, h - 1)
                        t_.matmul(pR[0:1, (h % 2) * 512:(h % 2) * 512 + w], k["ones"][0:NB, 0:1],
                                  acc[:, h * w:(h + 1) * w], start=True, stop=True).then_inc(rowed, 1)
            clear_semaphores(nc, a)

        with ExitStack() as inner:
            b = Scope(nc, inner, "put")
            C = k["columns"]
            rows = b.sb("rows", [P, 2, C * P])
            drow = b.sb("drow", [NB, 2, C * P])
            ohdT = b.sb("ohdT", [NB, 2, C * P])
            ohd, ohs = b.sb("ohd", [P, 2, C, NB], bf16), b.sb("ohs", [P, 2, C, NB], bf16)
            ea = b.sb("ea", [P, 2, C, DE])
            prod = b.sb("prod", [P, 2, C, DE])
            junk, copy = b.sb("junk", [P, C, P], bf16), b.sb("copy", [P, C, DE], bf16)
            pre = b.sb("pre", [NB, 2, C, NB])
            rank = b.sb("rank", [P, 2, C])
            hit = b.sb("hit", [P, 2, C, NB])
            col = b.sb("col", [P, 2, C])
            pos = b.sb("pos", [P, 2, C])
            chk = b.sb("chk", [P, 2, C])
            index = b.sb("index", [P, 2, C], i32)
            stage = [b.sb(f"stage{h}", [P, C, F]) for h in range(2)]
            pK = b.ps("pK", [128, 512])
            pL = b.ps("pL", [128, 2, 512])
            loaded = b.steps("loaded", 2, 2, 16)
            hot = b.steps("hot", 2, 2, head=1)
            ranked = b.steps("ranked", 2, 2, head=1)
            looked = b.steps("looked", 2, 2, head=1)
            placed = b.steps("placed", 2, 2, head=1)
            staged = b.steps("staged", 2, 2, head=1)
            sent = k["sent"]
            counted, copied, cleared = b.sem("counted"), b.sem("copied"), b.sem("cleared")
            dve_chain, passed = b.sem("dve_chain"), b.sem("passed")
            slots = k["slots"].rearrange("l c f -> (l c) f")
            added = b.sem("added")
            PER = 11
            with nc.Block() as block:

                @block.sync
                def _(sp):
                    keys_v = k["key_rows"].rearrange("(g c) p -> g (c p)", c=C)
                    dblk_v = k["dblk_rows"].rearrange("(g c) p -> g (c p)", c=C)
                    ea_v = edge_attr.rearrange("(p c) k -> p c k", p=P)
                    with sp.Fori(0, EC // C // 2) as i:
                        for h in range(2):
                            ranked.freed(sp, i, h)
                            hot.freed(sp, i, h)
                            g = 2 * i + h
                            sp.dma_start(rows[:, h, :], keys_v[ds(g, 1), :].to_broadcast([P, C * P])).then_inc(loaded.sem(h), 16)
                            sp.dma_start(drow[:, h, :], dblk_v[ds(g, 1), :].to_broadcast([NB, C * P])).then_inc(loaded.sem(h), 16)
                            sp.dma_start(ea[:, h, :, :], ea_v[:, ds(g * C, C), :]).then_inc(loaded.sem(h), 16)

                @block.vector
                def _(dve):
                    v = nc.vector
                    for h in range(2):
                        v.memset(stage[h][:, :, :], 0.0).then_inc(cleared, 1)
                    dve.wait_ge(cleared, 2)
                    for step in (hot, ranked, placed):
                        step.begin(dve)
                    with dve.Fori(0, EC // C // 2) as i:
                        for h in range(2):
                            g = 2 * i + h
                            chain = Chain(dve, dve_chain, g * PER)
                            dve.wait_ge(loaded.sem(h), 48 * i + 48)
                            looked.freed(dve, i, h)
                            v.tensor_scalar(ohdT[:, h, :], drow[:, h, :], iop[0:NB, :], None, ALU.is_equal)
                            v.tensor_tensor(ohd[:, h, :, :], dblk[:, ds(g * C, C)].unsqueeze(2).to_broadcast([P, C, NB]),
                                            io25[:, :].unsqueeze(1).to_broadcast([P, C, NB]), ALU.is_equal)
                            chain(v.tensor_tensor(ohs[:, h, :, :], sblk[:, ds(g * C, C)].unsqueeze(2).to_broadcast([P, C, NB]),
                                                  io25[:, :].unsqueeze(1).to_broadcast([P, C, NB]), ALU.is_equal))
                            dve.sem_inc(hot.sem(h), 1)
                            for j in range(C):
                                ins = v.scalar_tensor_tensor(junk[:, j, :], rows[:, h, j * P:(j + 1) * P], key[:, ds(g * C + j, 1)],
                                                             tri[:, :], ALU.is_equal, ALU.mult, accum_out=rank[:, h, j:j + 1])
                                chain(ins) if j == C - 1 else None
                            staged.freed(dve, i, h)
                            chain(v.tensor_tensor(prod[:, h, :, :], ea[:, h, :, :], vrow[:, :].unsqueeze(1).to_broadcast([P, C, DE]), ALU.mult))
                            dve.sem_inc(ranked.sem(h), 1)
                            looked.after(dve, i, h)
                            chain(v.tensor_tensor(hit[:, h, :, :], pL[0:P, h, 0:C * NB].rearrange("p (c s) -> p c s", s=NB),
                                                  ohs[:, h, :, :], ALU.mult))
                            chain(v.tensor_reduce(pos[:, h, :], hit[:, h, :, :], AX.X, ALU.add))
                            chain(v.tensor_tensor(pos[:, h, :], pos[:, h, :], rank[:, h, :], ALU.add))
                            chain(v.tensor_scalar(chk[:, h, :], pos[:, h, :], -(L - 1) / 2.0, 1.0 / L, ALU.add, ALU.mult))
                            chain(v.tensor_scalar(chk[:, h, :], chk[:, h, :], MAGIC, None, ALU.add))
                            chain(v.tensor_scalar(chk[:, h, :], chk[:, h, :], -MAGIC, None, ALU.add))
                            chain(v.scalar_tensor_tensor(pos[:, h, :], chk[:, h, :], -float(L), pos[:, h, :], ALU.mult, ALU.add))
                            sent.freed(dve, i, h)
                            chain(v.scalar_tensor_tensor(index[:, h, :], pos[:, h, :], float(NCA), chk[:, h, :], ALU.mult, ALU.add))
                            assert chain.n == PER, chain.n
                            dve.sem_inc(placed.sem(h), 1)

                @block.scalar
                def _(act):
                    act.wait_ge(cleared, 2)
                    staged.begin(act)
                    with act.Fori(0, EC // C // 2) as i:
                        for h in range(2):
                            g = 2 * i + h
                            looked.freed(act, i, h)
                            for j in range(C):
                                act.wait_ge(counted, g * C + j + 1)
                                nc.scalar.copy(pre[:, h, j, :], pK[0:NB, 0:NB]).then_inc(copied, 1)
                            sent.freed(act, i, h)
                            nc.scalar.copy(stage[h][:, :, 0:4], pay[:, ds(g * C, C), :])
                            ranked.after(act, i, h)
                            for j in range(C):
                                ins = nc.scalar.activation(copy[:, j, :], prod[:, h, j, :], ACT.Copy, accum_out=col[:, h, j:j + 1])
                            ins.then_inc(added, 1)
                            act.wait_ge(added, g + 1)
                            nc.scalar.activation(stage[h][:, :, EDGE], col[:, h, :], ACT.Identity, bias=becol[:, :]
                                                 ).then_inc(staged.sem(h), 1)

                @block.tensor
                def _(pe):
                    t_ = nc.tensor
                    looked.begin(pe)
                    t_.matmul(pK[0:NB, 0:NB], k["ident"][0:NB, 0:NB], base[:, :], start=True, stop=False,
                              skip_group_check=True).then_inc(counted, 1)
                    with pe.Fori(0, EC // C // 2) as i:
                        for h in range(2):
                            g = 2 * i + h
                            hot.after(pe, i, h)
                            placed.freed(pe, i, h)
                            for j in range(C):
                                pe.wait_ge(copied, g * C + j + 1)
                                t_.matmul(pK[0:NB, 0:NB], ohd[:, h, j, :], ohs[:, h, j, :], start=False, stop=False,
                                          skip_group_check=True).then_inc(counted, 1)
                                ins = t_.matmul(pL[0:P, h, NB * j:NB * j + NB], ohdT[:, h, j * P:(j + 1) * P], pre[:, h, j, :],
                                                start=True, stop=True)
                            ins.then_inc(looked.sem(h), 1)

                @block.gpsimd
                def _(pool):
                    sent.begin_with_dma(pool, k)
                    with pool.Fori(0, EC // C // 2) as i:
                        for h in range(2):
                            placed.after(pool, i, h)
                            staged.after(pool, i, h)
                            pool.sem_inc(passed, 1)
                            for j in range(C):
                                nc.gpsimd.indirect_dma_start(
                                    slots, bass.IndirectOffsetOnAxis(index[:, h, j:j + 1], 0),
                                    stage[h][:, j, :], None).then_inc(sent.sem(h), 16)
                    for h in range(2):
                        sent.freed(pool, EC // C // 2, h)
            clear_semaphores(nc, b)


class Norm:

    CHAINED = 5

    def __init__(self, s):
        self.stats, self.mv = s.sb("stats", [P, 2, 6]), s.sb("mv", [P, 2, 2])
        self.ve, self.sd, self.rs = s.sb("ve", [P, 2]), s.sb("sd", [P, 2]), s.sb("rs", [P, 2])
        self.shifted = s.steps("shifted")
        self.rooted = s.steps("rooted")
        self.passed = s.sem("passed")

    def on_dve(self, nc, dve, chain, i, j, r, y):
        h, v = j % 2, nc.vector
        chain(v.bn_stats(self.stats[:, h, :], r))
        dve.sem_inc(self.passed, 1)
        chain(v.bn_aggr(self.mv[:, h, :], self.stats[:, h, :]))
        chain(v.tensor_scalar(self.ve[:, h:h + 1], self.mv[:, h, 1:2], EPS, None, ALU.add))
        dve.sem_inc(self.shifted.sem(j), 1)
        self.rooted.after(dve, i, j)
        chain(v.reciprocal(self.rs[:, h:h + 1], self.sd[:, h:h + 1]))
        chain(v.tensor_scalar(y, r, self.mv[:, h, 0:1], self.rs[:, h:h + 1], ALU.subtract, ALU.mult))

    def on_act(self, nc, act, i, j):
        h = j % 2
        self.shifted.after(act, i, j)
        nc.scalar.activation(self.sd[:, h:h + 1], self.ve[:, h:h + 1], ACT.Sqrt).then_inc(self.rooted.sem(j), 1)


def load_rows(sp, rows, sem):
    for tile, vector in rows:
        sp.dma_start(tile[:, :], vector.partition_broadcast(P)).then_inc(sem, 16)


def group_range(eng, k, d):
    g0 = eng.value_load(k["group_start"][0:1, ds(d, 1)], min_val=0, max_val=NG - 1)
    g1 = eng.value_load(k["group_start"][0:1, ds(d + 1, 1)], min_val=1, max_val=NG)
    return g0, g1


def tiles_of(ps):
    return ps[0:P, 0:NB * TS].rearrange("p (s q) -> p s q", q=TS)



def word(k, c, f):
    return k["edges"][:, ds(c, 1), f:f + 1].rearrange("p a b -> p (a b)")


def turns_of(eng, k):
    return eng.value_load(k["group_start"][0:1, 30:31], min_val=1, max_val=NT)


class Offsets:

    def __init__(self, eng, s, name, table, most):
        self.eng, self.table, self.most = eng, table, most
        self.regs = s.registers(eng, name)

    def load(self, g):
        self.eng.load(self.regs, self.table[0:1, ds(G * g, G)])

    def some(self, a, b):
        return [self.eng.snap(r, min_val=0, max_val=self.most) for r in self.regs[a:b]]


def zero_tiles(nc, k, ps, a=0, b=7):
    for q in range(a, b):
        nc.tensor.matmul(ps[:, 512 * q:512 * q + 512], k["zeros_bf"][:, 0:128], k["zeros_bf"][:, :], start=True, stop=False,
                         skip_group_check=True)


class Ring:

    def __init__(self, s, parts):
        self.parts = parts
        self.buf = s.sb("ring", [L, RING, len(parts), G * P], bf16)
        self.landed = [s.sem(f"landed{r}") for r in range(RING)]
        self.arrived = s.sem("arrived")

    def on_sp(self, sp, k, read):
        hot = k["hot"]

        def load(g, j):
            for n, part in enumerate(self.parts):
                sp.dma_start(self.buf[:, j % RING, n, :], hot[ds(g, 1), :, part, :].rearrange("o p n -> (o p) n")
                             ).then_inc(self.landed[j % RING], 16)

        n = 16 * len(self.parts)
        for j in range(RING - 1):
            load(j, j)
        sp.wait_ge(self.landed[0], n)
        sp.sem_inc(self.arrived, 1)
        with sp.Fori(0, turns_of(sp, k)) as i:
            for j in range(RING):
                g = RING * i + j
                sp.wait_ge(self.landed[(j + 1) % RING], n * (i + (j + 1) // RING) + n)
                sp.sem_inc(self.arrived, 1)
                for sem in read:
                    sp.wait_ge(sem, g + 1)
                load(g + RING - 1, j + RING - 1)
        turns = turns_of(sp, k)
        for j in range(RING - 1):
            sp.wait_ge(self.landed[j], n * turns + n)
        sp.sem_inc(self.arrived, 1)

    def part(self, g, n, c0=0, c1=G):
        return self.slot(g % RING, n, c0, c1)

    def slot(self, r, n, c0, c1):
        return self.buf[:, ds(r, 1), n, c0 * P:c1 * P].rearrange("p a n -> p (a n)")


def phase_adjacency(nc, k):
    ctx = ExitStack()
    with ctx:
        s = Scope(nc, ctx, "adj")
        T = s.sb("T", [P, 2, NB, P])
        ring = s.sb("ring", [L, RING, 2, G * P], bf16)
        deg, root = s.sb("deg", [P, NB]), s.sb("root", [P, NB])
        U = s.sb("U", [P, 12, P])
        totals = s.sb("totals", [P, NB, P])
        ps = s.ps("ps", [128, 4096])
        pool_chain, pool_passed = s.sem("pool_chain"), s.sem("pool_passed")
        totalled, loaded, hot, used, moved, summed, ended, rooted, shifted, passed = (
            s.sem(n) for n in ("totalled", "loaded", "hot", "used", "moved", "summed", "ended", "rooted", "shifted", "passed"))
        saved = [s.sem(f"saved{r}") for r in range(RING)]
        stored = [s.sem(f"stored{r}") for r in range(2)]
        with nc.Block() as block:

            @block.sync
            def _(sp):
                sp.dma_start(k["edges"][:, :, :], k["slots"]).then_inc(loaded, 16)
                for sem in saved:
                    sp.sem_inc(sem, 16)
                turns = turns_of(sp, k)
                with sp.Fori(0, turns + 1) as i:
                    for j in range(RING):
                        g = RING * i + j
                        sp.wait_ge(hot, g + 1)
                        sp.dma_start(k["hot"][ds(g, 1)].rearrange("o p t n -> (o p) (t n)"),
                                     ring[:, j, :, :].rearrange("p t n -> p (t n)")).then_inc(saved[j], 16)
                turns = turns_of(sp, k)
                for j in range(RING):
                    sp.wait_ge(saved[j], 16 * turns + 32)
                sp.sem_inc(passed, 1)

            @block.vector
            def _(dve):
                dve.wait_ge(loaded, 16)
                with dve.Fori(0, turns_of(dve, k) + 1) as i:
                    for j in range(RING):
                        g = RING * i + j
                        dve.wait_ge(used, g + 1)
                        dve.wait_ge(saved[j], 16 * i + 16)
                        for c in range(G):
                            for f in (SRC, DST):
                                ins = nc.vector.tensor_scalar(ring[:, j, f, c * P:(c + 1) * P], k["iota_bf"][:, :],
                                                              word(k, G * g + c, f), None, ALU.is_equal)
                        ins.then_inc(hot, 1)
                dve.wait_ge(summed, 1)
                nc.vector.tensor_scalar(deg[:, :], ps[0:P, 3584:3584 + NB], 1.0, None, ALU.add).then_inc(shifted, 1)
                dve.wait_ge(rooted, 1)
                nc.vector.reciprocal(k["dinv"][:, :], root[:, :]).then_inc(ended, 1)
                dve.wait_ge(ended, 1)

            @block.scalar
            def _(act):
                for sem in stored:
                    act.sem_inc(sem, 16)
                with act.Fori(0, NB // 5) as i:
                    for j in range(5):
                        d = 5 * i + j
                        g1 = act.value_load(k["group_start"][0:1, ds(d + 1, 1)], min_val=1, max_val=NG)
                        act.wait_ge(used, g1 + RING)
                        act.wait_ge(stored[j % 2], 16 * (i * len(range(j % 2, 5, 2)) + j // 2) + 16)
                        act.wait_ge(totalled, d + 1)
                        for a, b in ((0, 16), (16, NB)):
                            nc.scalar.copy(T[:, j % 2, a:b, :], tiles_of(ps)[:, a:b, 0:P]).then_inc(moved, 1)
                        act.wait_ge(moved, 2 * d + 2)
                        act.dma_start(k["counts"][ds(d, 1)].rearrange("o p n -> (o p) n"),
                                      T[:, j % 2, :, :].rearrange("p s q -> p (s q)")).then_inc(stored[j % 2], 16)
                act.wait_ge(shifted, 1)
                nc.scalar.activation(root[:, :], deg[:, :], ACT.Sqrt).then_inc(rooted, 1)
                act.wait_ge(stored[0], 16 + 16 * 15)
                act.wait_ge(stored[1], 16 + 16 * 10)

            @block.gpsimd
            def _(pool):
                pool.sem_inc(totalled, 1)
                with pool.Fori(0, NB // 5) as i:
                    for j in range(5):
                        d = 5 * i + j
                        pool.wait_ge(moved, 2 * d + 2)
                        total = totals[:, ds(d, 1), :].rearrange("p a n -> p (a n)")
                        chain = Chain(pool, pool_chain, 5 * d)
                        g = nc.gpsimd
                        chain(g.tensor_tensor(U[:, :, :], T[:, j % 2, 0:12, :], T[:, j % 2, 12:24, :], ALU.add))
                        chain(g.tensor_tensor(U[:, 0, :], U[:, 0, :], T[:, j % 2, 24, :], ALU.add))
                        chain(g.tensor_tensor(U[:, 0:6, :], U[:, 0:6, :], U[:, 6:12, :], ALU.add))
                        chain(g.tensor_tensor(U[:, 0:3, :], U[:, 0:3, :], U[:, 3:6, :], ALU.add))
                        chain(g.tensor_tensor(U[:, 0, :], U[:, 0, :], U[:, 1, :], ALU.add))
                        pool.sem_inc(pool_passed, 1)
                        g.tensor_tensor(total, U[:, 0, :], U[:, 2, :], ALU.add).then_inc(totalled, 1)
                        pool.wait_ge(totalled, d + 2)

            @block.tensor
            def _(pe):
                t_ = nc.tensor
                pe.sem_inc(used, RING)
                at = Offsets(pe, s, "at", k["tile_at"], (NB - 1) * TS)
                zero_tiles(nc, k, ps, 0, 7)
                with pe.Fori(0, NB // 5) as i:
                    for j in range(5):
                        d = 5 * i + j
                        g0, g1 = group_range(pe, k, d)
                        with pe.Fori(g0, g1) as g:
                            at.load(g)
                            pe.wait_ge(hot, g + 1)
                            for c in range(G):
                                if c % 4 == 0:
                                    four = at.some(c, c + 4)
                                left, right = (ring[:, ds(g % RING, 1), f, c * P:(c + 1) * P].rearrange("p a n -> p (a n)")
                                               for f in (SRC, DST))
                                ins = t_.matmul(ps[0:P, ds(four[c % 4], P)], left, right, start=False, stop=False,
                                                skip_group_check=True)
                            ins.then_inc(used, 1)
                        pe.wait_ge(moved, 2 * d + 1)
                        zero_tiles(nc, k, ps, 0, 4)
                        pe.wait_ge(moved, 2 * d + 2)
                        zero_tiles(nc, k, ps, 4, 7)
                pe.drain().then_inc(used, 2 * RING)
                pe.wait_ge(totalled, NB + 1)
                for d in range(NB):
                    ins = t_.matmul(ps[0:P, 3584 + d:3585 + d], totals[:, d, :], k["ones"][0:P, 0:1], start=True, stop=True)
                ins.then_inc(summed, 1)
        clear_semaphores(nc, s)


def phase_lookup(nc, k, tag, part, values, per_turn, finish, prepare=None):
    ctx = ExitStack()
    with ctx:
        s = Scope(nc, ctx, tag)
        ring = Ring(s, (part,))
        v3 = s.sb("v3", [P, NB, 3], bf16)
        rest = s.sb("rest", [P, NB])
        ident_bf = s.sb("ident_bf", [L, L], bf16)
        turned = s.sb("turned", [P, 2, G * L], bf16)
        pt = s.ps("pt", [128, 2, G * L])
        pz = s.ps("pz", [128, 2, 512])
        z = s.sb("z", [L, 2, 2 * G])
        split, chain_sem = s.sem("split"), s.sem("chain")
        flipped, copied = s.sem("flipped"), s.sem("copied")
        looked = s.steps("looked", 2, 2, head=1)
        finished = s.steps("finished", 2, 2, head=1)
        ended = s.sem("ended")
        with nc.Block() as block:

            @block.sync
            def _(sp):
                ring.on_sp(sp, k, [flipped])

            @block.tensor
            def _(pe):
                t_ = nc.tensor

                def turn(g, j):
                    pe.wait_ge(ring.arrived, g + 1)
                    pe.wait_ge(copied, g + 1)
                    for c in range(G):
                        ins = t_.matmul(pt[0:P, j % 2, L * c:L * c + L], ring.buf[:, j, 0, c * P:(c + 1) * P], ident_bf[:, :],
                                        start=True, stop=True)
                    ins.then_inc(flipped, 1)

                def look(i, g, j):
                    at.load(g)
                    pe.wait_ge(copied, g + 3)
                    if j % 2 == 0:
                        finished.freed(pe, i, j // 2)
                    v3f = v3[:, :, :].rearrange("p b n -> p (b n)")
                    for c in range(G):
                        o = (j % 2) * 3 * G + 3 * c
                        if c % 4 == 0:
                            four = at.some(c, c + 4)
                        ins = t_.matmul(pz[0:L, j // 2, o:o + 3], turned[:, j % 2, L * c:L * c + L], v3f[:, ds(four[c % 4], 3)],
                                        start=True, stop=True)
                    if j % 2 == 1:
                        ins.then_inc(looked.sem(j // 2), 1)

                at = Offsets(pe, s, "at", k["parts_at"][part], (NB - 1) * 3)
                pe.wait_ge(split, 1)
                pe.sem_inc(copied, 2)
                pe.sem_inc(flipped, 1)
                looked.begin(pe)
                with pe.Fori(0, turns_of(pe, k)) as i:
                    for j in range(RING):
                        turn(RING * i + j, j)
                        if j > 0:
                            look(i, RING * i + j - 1, j - 1)
                    look(i, RING * i + RING - 1, RING - 1)

            @block.scalar
            def _(act):
                with act.Fori(0, turns_of(act, k)) as i:
                    for j in range(RING):
                        g = RING * i + j
                        act.wait_ge(flipped, g + 2)
                        if j < 2:
                            looked.freed(act, i, 1)
                        else:
                            looked.after(act, i, 0)
                        nc.scalar.copy(turned[:, j % 2, :], pt[0:P, j % 2, :]).then_inc(copied, 1)

            @block.vector
            def _(dve):
                v = nc.vector
                chain = Chain(dve, chain_sem)
                chain(v.tensor_copy(ident_bf[:, :], k["ident"][:, :]))
                if prepare:
                    prepare(dve, chain)
                chain(v.tensor_copy(v3[:, :, 0], values))
                chain(v.tensor_tensor(rest[:, :], values, v3[:, :, 0], ALU.subtract))
                chain(v.tensor_copy(v3[:, :, 1], rest[:, :]))
                chain(v.tensor_tensor(rest[:, :], rest[:, :], v3[:, :, 1], ALU.subtract))
                chain(v.tensor_copy(v3[:, :, 2], rest[:, :]))
                dve.sem_inc(split, 1)
                finished.begin(dve)
                n = chain.n
                with dve.Fori(0, turns_of(dve, k)) as i:
                    for h in range(2):
                        g = RING * i + 2 * h
                        chain = Chain(dve, chain_sem, n + (2 * i + h) * per_turn)
                        looked.after(dve, i, h)
                        chain(v.tensor_reduce(z[:, h, :], pz[0:L, h, 0:6 * G].rearrange("p (c t) -> p c t", t=3), AX.X, ALU.add))
                        dve.sem_inc(finished.sem(h), 1)
                        finish(dve, chain, z[:, h, :], g)
                        assert chain.n == per_turn
        clear_semaphores(nc, s)


def phase_greatest(nc, k, logit, negated):
    ctx = ExitStack()
    with ctx:
        s = Scope(nc, ctx, "max")
        ring = Ring(s, (DST,))
        far = s.sb("far", [L, 2, G * P], bf16)
        floor = s.sb("floor", [L, G * P])
        top8 = s.sb("top8", [L, 2, G * P])
        tops = s.sb("tops", [L, NB, P])
        ps = s.ps("ps", [128, 4096])
        greatest, diag, ones = s.sb("greatest", [P, NB]), s.sb("diag", [P, NB, P]), s.sb("ones", [P, L])
        read, grouped, floored, lowered, joined = (s.sem(n) for n in ("read", "grouped", "floored", "lowered", "joined"))
        passed, turned, ended = (s.sem(n) for n in ("passed", "turned", "ended"))

        def top(d):
            return top8[:, ds(d % 2, 1), :].rearrange("p a n -> p (a n)")

        with nc.Block() as block:

            @block.sync
            def _(sp):
                ring.on_sp(sp, k, [read])

            @block.vector
            def _(dve):
                v = nc.vector

                def measure(g):
                    dve.wait_ge(ring.arrived, g + 1)
                    v.tensor_scalar(far[:, ds(g % 2, 1), :].rearrange("p a n -> p (a n)"), ring.part(g, 0), -1.0, BIG,
                                    ALU.add, ALU.mult).then_inc(read, 1)

                dve.sem_inc(grouped, 1)
                dve.sem_inc(read, 1)
                measure(0)
                with dve.Fori(0, NB) as d:
                    g0, g1 = group_range(dve, k, d)
                    dve.wait_ge(lowered, d + 1)
                    dve.sem_inc(passed, 1)
                    with dve.Fori(g0, g1) as g:
                        dve.wait_ge(grouped, g + 1)
                        measure(g + 1)
                        dve.wait_ge(read, g + 2)
                        for c in range(G):
                            ins = v.scalar_tensor_tensor(top(d)[:, c * P:(c + 1) * P],
                                                         far[:, ds(g % 2, 1), c * P:(c + 1) * P].rearrange("p a n -> p (a n)"),
                                                         logit[:, ds(G * g + c, 1)], top(d)[:, c * P:(c + 1) * P], ALU.add, ALU.max)
                        ins.then_inc(grouped, 1)
                    dve.wait_ge(grouped, g1 + 1)
                    v.tensor_reduce(tops[:, ds(d, 1), :].rearrange("p a n -> p (a n)"),
                                    top(d).rearrange("p (c n) -> p n c", n=P), AX.X, ALU.max).then_inc(joined, 1)
                dve.sem_inc(read, RING)
                dve.wait_ge(turned, 1)
                v.tensor_reduce(greatest[:, :], ps[0:P, 0:NB * L].rearrange("p (b l) -> p b l", l=L), AX.X, ALU.max).then_inc(ended, 1)
                dve.wait_ge(ended, 1)
                for b in range(NB):
                    ins = v.tensor_scalar(diag[:, b, :], k["ident"][0:P, 0:P], greatest[:, b:b + 1], -1.0, ALU.mult, ALU.mult)
                ins.then_inc(ended, 1)
                dve.wait_ge(turned, 2)
                v.tensor_copy(negated, ps[:, 0:NB * L].rearrange("p (b l) -> p b l", l=L)[:, :, 0:P]).then_inc(ended, 1)
                dve.wait_ge(ended, 3)

            @block.scalar
            def _(act):
                def lower(d):
                    nc.scalar.copy(top(d), floor[:, :]).then_inc(lowered, 1)

                act.wait_ge(floored, 1)
                for d in range(2):
                    lower(d)
                with act.Fori(2, NB) as d:
                    act.wait_ge(joined, d - 1)
                    lower(d)

            @block.gpsimd
            def _(pool):
                nc.gpsimd.memset(ones[:, :], 1.0)
                nc.gpsimd.memset(floor[:, :], -BIG).then_inc(floored, 1)

            @block.tensor
            def _(pe):
                pe.wait_ge(joined, NB)
                for b in range(NB):
                    ins = nc.tensor.transpose(ps[0:P, L * b:L * b + L], tops[:, b, :], k["ident"][:, :])
                ins.then_inc(turned, 1)
                pe.wait_ge(floored, 1)
                pe.wait_ge(ended, 2)
                for b in range(NB):
                    ins = nc.tensor.matmul(ps[:, L * b:L * b + P], ones[:, :], diag[:, b, :], start=True, stop=True)
                ins.then_inc(turned, 1)
        clear_semaphores(nc, s)


def phase_weighted(nc, k, tag, by_dst, table, width, weight, make, attention=None):
    ctx = ExitStack()
    with ctx:
        s = Scope(nc, ctx, tag)
        ring = Ring(s, (SRC, DST))
        lf, rf = (SRC, DST) if by_dst else (DST, SRC)
        left, right = s.sb("left", [L, PARTS, W, P]), s.sb("right", [L, PARTS, W, P])
        H = s.sb("H", [P, NB, width])
        T = [s.sb(f"T{h}", [P, NB, P]) for h in range(2)]
        ps = s.ps("ps", [128, 4096])
        loaded, moved, last_moved = s.sem("loaded"), s.sem("moved"), s.sem("last_moved")
        left_ready, right_ready, used = (s.steps(n, PARTS, PARTS, head=1) for n in ("left", "right", "used"))
        half = 12 if by_dst else 16
        summed, read = (s.sem("summed"), s.sem("read")) if by_dst else (None, None)
        pairs = -(-NB // 2)
        multiplied, added = (None, None) if by_dst else (s.steps("multiplied", 2, pairs), s.steps("added", 2, pairs))
        product = (lambda h, n=width: ps[0:P, 3584 - 512 * (h % 2):3584 - 512 * (h % 2) + n])
        s.read = read
        hooks = make(s)
        if attention:
            logit, negated = attention
            far, power = s.sb("far", [L, 2, G * P], bf16), s.sb("power", [L, PARTS, W, P])
            measured, powered = s.sem("measured"), s.steps("powered", PARTS, PARTS, head=1)
        rights_read = measured if attention else right_ready.sem(PARTS - 1)

        def blocks(eng, step):
            for d in range(3):
                step(d, d % 2, min(d, 2))
            with eng.Fori(0, (NB - 3) // 2) as i:
                for j in range(2):
                    step(2 * i + 3 + j, (j + 1) % 2, 2)

        def tiles_full(eng, g1):
            for f in range(PARTS):
                used.freed(eng, g1, f)

        def tiles_free(eng, d, n):
            if n == 2 and by_dst:
                eng.wait_ge(summed, d - 1)
            elif n == 2:
                for h in range(2):
                    multiplied.freed(eng, d - 1, h)

        with nc.Block() as block:

            @block.sync
            def _(sp):
                sp.dma_start(H[:, :, :], table.rearrange("b p n -> p b n")).then_inc(loaded, 16)
                ring.on_sp(sp, k, [left_ready.sem(PARTS - 1), rights_read])

            @block.tensor
            def _(pe):
                t_ = nc.tensor

                def multiply(d, h, after_last):
                    if by_dst:
                        pe.wait_ge(moved, 2 * d + 2)
                        if not isinstance(d, int) or d > 0:
                            pe.wait_ge(read, d)
                        for q in range(NB):
                            ins = t_.matmul(product(0), T[h][:, q, :], H[:, q, :], start=(q == 0), stop=(q == NB - 1))
                        ins.then_inc(summed, 1)
                        return
                    pe.wait_ge(moved, 2 * d + 2)
                    for r in range(pairs):
                        if r == 1:
                            pe.wait_ge(last_moved, after_last)
                        if not isinstance(d, int) or d + r // 2 > 0:
                            added.freed(pe, d, r)
                        for q in range(2 * r, min(2 * r + 2, NB)):
                            ins = t_.matmul(product(r, 2 * D)[:, q % 2 * D:q % 2 * D + D], T[h][:, q, :],
                                            H[:, ds(d, 1), :].rearrange("p a n -> p (a n)"), start=True, stop=True)
                        ins.then_inc(multiplied.sem(r), 1)

                def step(d, h, n):
                    g0, g1 = group_range(pe, k, d)
                    if n > 0:
                        pe.wait_ge(moved, 2 * d)
                    if n == 2 and not by_dst:
                        added.freed(pe, d - 1, 1)
                    zero_tiles(nc, k, ps)
                    with pe.Fori(g0, g1) as g:
                        at.load(g)
                        for f in range(PARTS):
                            if W * f % 4 == 0:
                                four = at.some(W * f, W * f + 4)
                            left_ready.after(pe, g, f)
                            right_ready.after(pe, g, f)
                            for c in range(W):
                                ins = t_.matmul(ps[0:P, ds(four[(W * f + c) % 4], P)], left[:, f, c, :], right[:, f, c, :],
                                                start=False, stop=False, skip_group_check=True)
                            ins.then_inc(used.sem(f), 1)
                    if n > 0:
                        multiply(d - 1, 1 - h, d + 1)

                at = Offsets(pe, s, "at", k["tile_at"], (NB - 1) * TS)
                pe.wait_ge(loaded, 16)
                used.begin(pe)
                blocks(pe, step)
                multiply(NB - 1, (NB - 1) % 2, NB)

            @block.scalar
            def _(act):
                def widen(g):
                    r = act.snap(g % RING, min_val=0, max_val=RING - 1)
                    act.wait_ge(ring.arrived, g + 1)
                    for f in range(PARTS):
                        used.freed(act, g, f)
                        nc.scalar.copy(left[:, f, :, :].rearrange("p c n -> p (c n)"), ring.slot(r, lf, W * f, W * f + W)
                                       ).then_inc(left_ready.sem(f), 1)
                        if attention:
                            powered.after(act, g, f)
                            nc.scalar.activation(right[:, f, :, :], power[:, f, :, :], ACT.Exp).then_inc(right_ready.sem(f), 1)

                def take(d):
                    act.wait_ge(summed, d + 1)
                    nc.scalar.copy(hooks["rows"](act, d), product(0)).then_inc(read, 1)

                def step(d, h, n):
                    g0, g1 = group_range(act, k, d)
                    widen(g0)
                    if n == 2 and by_dst:
                        take(d - 2)
                    with act.Fori(g0 + 1, g1) as g:
                        widen(g)
                    tiles_full(act, g1)
                    tiles_free(act, d, n)
                    nc.scalar.copy(T[h][:, 0:half, :], tiles_of(ps)[:, 0:half, 0:P]).then_inc(moved, 1)
                    if n == 2 and by_dst:
                        hooks["act"](act, d - 2)

                left_ready.begin(act)
                if attention:
                    right_ready.begin(act)
                blocks(act, step)
                act.drain().then_inc(left_ready.sem(PARTS - 1), RING)
                if by_dst:
                    for d in (NB - 2, NB - 1):
                        take(d)
                        hooks["act"](act, d)

            @block.vector
            def _(dve):
                v = nc.vector

                def add(d):
                    for r in range(pairs):
                        out = hooks["sum"][:, 2 * r:min(2 * r + 2, NB), :].rearrange("p b n -> p (b n)")
                        multiplied.after(dve, d, r)
                        v.tensor_tensor(out, out, product(r, out.shape[-1]), ALU.add).then_inc(added.sem(r), 1)

                def measure(g):
                    dve.wait_ge(ring.arrived, g + 1)
                    v.tensor_scalar(far[:, ds(g % 2, 1), :].rearrange("p a n -> p (a n)"), ring.part(g, rf), -1.0, BIG,
                                    ALU.add, ALU.mult).then_inc(measured, 1)

                def attend(d, g):
                    powered.freed(dve, g, PARTS - 1)
                    measure(g + 1)
                    dve.wait_ge(measured, g + 2)
                    for f in range(PARTS):
                        right_ready.freed(dve, g, f)
                        for c in range(W):
                            q = W * f + c
                            ins = v.scalar_tensor_tensor(power[:, f, c, :], negated[:, ds(d, 1), :].rearrange("p a n -> p (a n)"),
                                                         logit[:, ds(G * g + q, 1)],
                                                         far[:, ds(g % 2, 1), q * P:(q + 1) * P].rearrange("p a n -> p (a n)"),
                                                         ALU.add, ALU.min)
                        ins.then_inc(powered.sem(f), 1)

                def weigh(g):
                    r = dve.snap(g % RING, min_val=0, max_val=RING - 1)
                    dve.wait_ge(ring.arrived, g + 1)
                    for f in range(PARTS):
                        used.freed(dve, g, f)
                        v.tensor_tensor(right[:, f, :, :], ring.slot(r, rf, W * f, W * f + W).rearrange("p (c n) -> p c n", n=P),
                                        weight(G * g + W * f, W).unsqueeze(2).to_broadcast([L, W, P]), ALU.mult
                                        ).then_inc(right_ready.sem(f), 1)

                def step(d, h, n):
                    g0, g1 = group_range(dve, k, d)
                    with dve.Fori(g0, g1) as g:
                        attend(d, g) if attention else weigh(g)
                    tiles_full(dve, g1)
                    tiles_free(dve, d, n)
                    if by_dst:
                        v.tensor_copy(T[h][:, half:NB, :], tiles_of(ps)[:, half:NB, 0:P]).then_inc(moved, 1)
                        if n == 2:
                            hooks["dve"](dve, d - 2)
                        return
                    v.tensor_copy(T[h][:, NB - 1, :], tiles_of(ps)[:, NB - 1, 0:P]).then_inc(last_moved, 1)
                    v.tensor_copy(T[h][:, half:NB - 1, :], tiles_of(ps)[:, half:NB - 1, 0:P]).then_inc(moved, 1)
                    if n > 0:
                        if n == 2:
                            for f in range(2):
                                added.freed(dve, d - 1, f)
                        add(d - 1)

                hooks["start"](dve)
                if attention:
                    powered.begin(dve)
                    dve.sem_inc(measured, 1)
                    measure(0)
                else:
                    right_ready.begin(dve)
                blocks(dve, step)
                dve.drain().then_inc(rights_read, RING)
                if by_dst:
                    for d in (NB - 2, NB - 1):
                        hooks["dve"](dve, d)
                else:
                    for f in range(2):
                        added.freed(dve, NB - 1, f)
                    add(NB - 1)
                    hooks["done"](dve)

            @block.gpsimd
            def _(pool):
                hooks["pool"](pool)
        clear_semaphores(nc, s)


def phase_attended(nc, k, x1, x2, attention):
    PER = 9

    def make(s):
        b = {n: s.sb(n, [P, w]) for n, w in (("den", 1), ("stats", 6), ("mv", 2), ("ve", 1), ("sd", 1), ("rs", 1), ("r", D), ("y", D))}
        x = s.sb("x", [P, D])
        sums = s.sb("sums", [P, D + 1])
        xin, varied, rooted, finished, stored, chain_sem, passed, pool_passed = (
            s.sem(n) for n in ("xin", "varied", "rooted", "finished", "stored", "chain", "passed", "pool_passed"))

        def pool(pool):
            with pool.Fori(0, NB) as d:
                pool.dma_start(x[:, :], x1[ds(d, 1)].rearrange("o p n -> (o p) n")).then_inc(xin, 16)
                pool.wait_ge(finished, d + 1)
                pool.sem_inc(pool_passed, 1)
                pool.dma_start(x2[ds(d, 1)].rearrange("o p n -> (o p) n"), b["y"][:, :]).then_inc(stored, 16)
            pool.wait_ge(stored, 16 * NB)

        def rows(act, d):
            return sums[:, :]

        def act(act, d):
            act.wait_ge(varied, d + 1)
            nc.scalar.activation(b["sd"][:, :], b["ve"][:, :], ACT.Sqrt).then_inc(rooted, 1)

        def dve(dve, d):
            v = nc.vector
            den, stats, mv, ve, sd, rs, r, y = (b[n][:, :] for n in ("den", "stats", "mv", "ve", "sd", "rs", "r", "y"))
            chain = Chain(dve, chain_sem, d * PER)
            dve.wait_ge(s.read, d + 1)
            chain(v.tensor_scalar(den, sums[:, D:D + 1], 1e-16, None, ALU.add))
            chain(v.reciprocal(den, den))
            chain(v.tensor_scalar(r, sums[:, 0:D], den, 0.0, ALU.mult, ALU.max))
            dve.wait_ge(xin, 16 * d + 16)
            chain(v.tensor_tensor(r, r, x[:, :], ALU.add))
            chain(v.bn_stats(stats, r))
            dve.sem_inc(passed, 1)
            chain(v.bn_aggr(mv, stats))
            chain(v.tensor_scalar(ve, mv[:, 1:2], EPS, None, ALU.add))
            dve.sem_inc(varied, 1)
            dve.wait_ge(rooted, d + 1)
            chain(v.reciprocal(rs, sd))
            if not isinstance(d, int) or d > 0:
                dve.wait_ge(stored, 16 * d)
            chain(v.tensor_scalar(y, r, mv[:, 0:1], rs, ALU.subtract, ALU.mult))
            assert chain.n == PER, chain.n
            dve.sem_inc(finished, 1)

        return {"pool": pool, "rows": rows, "act": act, "dve": dve, "start": lambda dve: None}

    phase_weighted(nc, k, "att", True, k["t3"], D + 1, None, make, attention)


def phase_gated_in(nc, k, table):
    def make(s):
        y = s.sb("y", [P, D])
        stored = s.sem("stored")

        def pool(pool):
            with pool.Fori(0, NB) as d:
                pool.wait_ge(s.read, d + 1)
                pool.dma_start(k["cat"][ds(d, 1), :, 0:D].rearrange("o p n -> (o p) n"), y[:, :]).then_inc(stored, 16)
            pool.wait_ge(stored, 16 * NB)

        def rows(act, d):
            if not isinstance(d, int) or d > 0:
                act.wait_ge(stored, 16 * d)
            return y[:, :]

        return {"pool": pool, "rows": rows, "act": lambda act, d: None, "dve": lambda dve, d: None, "start": lambda dve: None}

    phase_weighted(nc, k, "gin", True, table, D, lambda c, n: k["edges"][:, ds(c, n), WIN], make)


def phase_gated_out(nc, k, table):
    def make(s):
        out = s.sb("out", [P, NB, D])
        cleared, done, stored = s.sem("cleared"), s.sem("done"), s.sem("stored")

        def start(dve):
            nc.vector.memset(out[:, :, :], 0.0).then_inc(cleared, 1)
            dve.wait_ge(cleared, 1)

        def pool(pool):
            pool.wait_ge(done, 1)
            pool.dma_start(k["cat"][:, :, D:2 * D].rearrange("b p n -> p b n"), out[:, :, :]).then_inc(stored, 16)
            pool.wait_ge(stored, 16)

        return {"pool": pool, "start": start, "sum": out, "done": lambda dve: dve.drain().then_inc(done, 1)}

    phase_weighted(nc, k, "gou", False, table, D, lambda c, n: k["edges"][:, ds(c, n), WOUT], make)


def phase_gemm(nc, k, tag, src, kc, weights, width, out, out_width, rows, chained, epilogue, prepare=None):
    ctx = ExitStack()
    i0 = 5 * k["gemm_turn"]
    k["gemm_turn"] += 1
    st = {n: steps.from_turn(i0) for n, steps in k["gemm_steps"].items()}
    with ctx:
        s = Scope(nc, ctx, tag)
        x = s.sb("x", [P, 2, kc * 128])
        xt = s.sb("xt", [128, 2, kc, P])
        w = s.sb("w", [128, kc, width])
        y = s.sb("y", [P, 2, out_width])
        tiles = {name: s.sb(name, [P, vec.shape[-1]]) for name, vec in rows.items()}
        pt = s.ps("pt", [128, 2, 512])
        po = s.ps("po", [128, 2, 512])
        ready, chain_sem, prepared = s.sem("ready"), s.sem("chain"), s.sem("prepared")
        n_ready = 16 * (len(weights) + len(rows))
        with nc.Block() as block:

            @block.sync
            def _(sp):
                for wd, c0, n in weights:
                    sp.dma_start(w[:, :, c0:c0 + n], wd.rearrange("(t c) n -> c t n", c=128)).then_inc(ready, 16)
                load_rows(sp, [(tiles[name], vec) for name, vec in rows.items()], ready)
                with sp.Fori(0, 5) as i:
                    for j in range(5):
                        st["turned"].freed(sp, i, j)
                        sp.dma_start(x[:, j % 2, :], src[ds(5 * i + j, 1)].rearrange("o p n -> (o p) n")).then_inc(st["loaded"].sem(j), 16)

            @block.gpsimd
            def _(pool):
                st["stored"].begin_with_dma(pool, k)
                with pool.Fori(0, 5) as i:
                    for j in range(5):
                        st["finished"].after(pool, i, j)
                        pool.dma_start(out[ds(5 * i + j, 1)].rearrange("o p n -> (o p) n"), y[:, j % 2, :]).then_inc(st["stored"].sem(j), 16)
                for j in range(2):
                    st["stored"].freed(pool, 5, j)

            @block.scalar
            def _(act):
                st["copied"].begin(act)
                with act.Fori(0, 5) as i:
                    for j in range(5):
                        st["turned"].after(act, i, j)
                        st["multiplied"].freed(act, i, j)
                        nc.scalar.copy(xt[:, j % 2, :, :], pt[:, j % 2, 0:kc * 128].rearrange("p (t q) -> p t q", q=128)[:, :, 0:P]
                                       ).then_inc(st["copied"].sem(j), 1)

            @block.tensor
            def _(pe):
                t_ = nc.tensor

                def turn(i, j):
                    st["loaded"].after(pe, i, j)
                    st["copied"].freed(pe, i, j)
                    for t in range(kc):
                        ins = t_.transpose(pt[:, j % 2, 128 * t:128 * t + P], x[:, j % 2, 128 * t:128 * t + 128], k["ident"][0:P, 0:P])
                    ins.then_inc(st["turned"].sem(j), 1)

                def multiply(i, j):
                    st["copied"].after(pe, i, j)
                    st["finished"].freed(pe, i, j)
                    for t in range(kc):
                        ins = t_.matmul(po[0:P, j % 2, 0:width], xt[:, j % 2, t, :], w[:, t, :], start=(t == 0), stop=(t == kc - 1))
                    ins.then_inc(st["multiplied"].sem(j), 1)

                pe.wait_ge(ready, n_ready)
                for n in ("turned", "multiplied"):
                    st[n].begin(pe)
                with pe.Fori(0, 5) as i:
                    turn(i, 0)
                    for j in range(5):
                        if j < 4:
                            turn(i, j + 1)
                        multiply(i, j)

            @block.vector
            def _(dve):
                dve.wait_ge(ready, n_ready)
                st["finished"].begin(dve)
                if prepare:
                    prepare(dve, y, prepared)
                with dve.Fori(0, 5) as i:
                    for j in range(5):
                        b = 5 * i + j
                        chain = Chain(dve, chain_sem, b * chained)
                        st["multiplied"].after(dve, i, j)
                        st["stored"].freed(dve, i, j)
                        epilogue(dve, chain, b, po[0:P, j % 2, :], y[:, j % 2, :], tiles)
                        assert chain.n == chained, (tag, chain.n)
                        dve.sem_inc(st["finished"].sem(j), 1)
        clear_semaphores(nc, s)


def phase_apply(nc, k, tag, table, width, out, rows, chained, epilogue, resid=None, norm=False):
    ctx = ExitStack()
    i0 = 5 * k["apply_turn"]
    k["apply_turn"] += 1
    st = {n: steps.from_turn(i0) for n, steps in k["apply_steps"].items()}
    with ctx:
        s = Scope(nc, ctx, tag)
        H = s.sb("H", [P, NB, width])
        T = [s.sb(f"T{h}", [P, NB, P]) for h in range(2)]
        X = s.sb("X", [P, NB, D]) if resid is not None else None
        y = s.sb("y", [P, 2, width])
        tmp = s.sb("tmp", [P, 2, width])
        tiles = {name: s.sb(name, [P, vec.shape[-1]]) for name, vec in rows.items()}
        po = s.ps("po", [128, 2, 512])
        nm = Norm(s) if norm else None
        ready, chain_sem = s.sem("ready"), s.sem("chain")
        n_ready = 16 * (1 + len(rows) + (resid is not None))
        with nc.Block() as block:

            @block.sync
            def _(sp):
                sp.dma_start(H[:, :, :], table.rearrange("b p n -> p b n")).then_inc(ready, 16)
                if resid is not None:
                    sp.dma_start(X[:, :, :], resid.rearrange("b p n -> p b n")).then_inc(ready, 16)
                load_rows(sp, [(tiles[name], vec) for name, vec in rows.items()], ready)
                with sp.Fori(0, 5) as i:
                    for j in range(5):
                        st["summed"].freed(sp, i, j)
                        sp.dma_start(T[j % 2][:, :, :].rearrange("p s q -> p (s q)"),
                                     k["counts"][ds(5 * i + j, 1)].rearrange("o p n -> (o p) n")).then_inc(st["loaded"].sem(j), 16)

            @block.gpsimd
            def _(pool):
                st["stored"].begin_with_dma(pool, k)
                with pool.Fori(0, 5) as i:
                    for j in range(5):
                        st["finished"].after(pool, i, j)
                        pool.dma_start(out[ds(5 * i + j, 1)].rearrange("o p n -> (o p) n"), y[:, j % 2, :]).then_inc(st["stored"].sem(j), 16)
                for j in range(2):
                    st["stored"].freed(pool, 5, j)

            @block.tensor
            def _(pe):
                pe.wait_ge(ready, n_ready)
                st["summed"].begin(pe)
                with pe.Fori(0, 5) as i:
                    for j in range(5):
                        st["loaded"].after(pe, i, j)
                        st["finished"].freed(pe, i, j)
                        for q in range(NB):
                            ins = nc.tensor.matmul(po[0:P, j % 2, 0:width], T[j % 2][:, q, :], H[:, q, :],
                                                   start=(q == 0), stop=(q == NB - 1))
                        ins.then_inc(st["summed"].sem(j), 1)

            if norm:
                @block.scalar
                def _(act):
                    with act.Fori(0, 5) as i:
                        for j in range(5):
                            nm.on_act(nc, act, i, j)

            @block.vector
            def _(dve):
                dve.wait_ge(ready, n_ready)
                st["finished"].begin(dve)
                with dve.Fori(0, 5) as i:
                    for j in range(5):
                        b = 5 * i + j
                        chain = Chain(dve, chain_sem, b * chained)
                        st["summed"].after(dve, i, j)
                        st["stored"].freed(dve, i, j)
                        at = (lambda A: A[:, ds(b, 1), :].rearrange("p a n -> p (a n)"))
                        t = tmp[:, j % 2, :]
                        chain(nc.vector.tensor_tensor(t, po[0:P, j % 2, 0:width], at(H), ALU.add))
                        epilogue(dve, chain, i, j, b, t, y[:, j % 2, :], tiles, at(X) if X is not None else None, nm)
                        assert chain.n == chained, (tag, chain.n)
                        dve.sem_inc(st["finished"].sem(j), 1)
        clear_semaphores(nc, s)


def phase_attention(nc, k, x1, x2):
    with ExitStack() as ctx:
        s = Scope(nc, ctx, "soft")
        logit = s.sb("logit", [L, NCA])
        negated = s.sb("negated", [L, NB, P])
        v = nc.vector

        def to_logits(dve, chain, z, g):
            c = G * g
            chain(v.tensor_tensor(z, z, k["edges"][:, ds(c, 2 * G), EDGE], ALU.add))
            chain(v.scalar_tensor_tensor(logit[:, ds(c, 2 * G)], z, 0.01, z, ALU.mult, ALU.max))

        def clear(dve, chain):
            chain(v.memset(logit[:, :], 0.0))

        phase_lookup(nc, k, "lhs", SRC, k["hs"][:, :], 3, to_logits, clear)
        phase_greatest(nc, k, logit, negated[:, :, :])
        phase_attended(nc, k, x1, x2, (logit, negated))


def phase_batch_norm(nc, k, x2, gamma, beta):
    ctx = ExitStack()
    with ctx:
        s = Scope(nc, ctx, "bn")
        X, Q = s.sb("X", [P, NB, D]), s.sb("Q", [P, NB, D])
        mean, scale, root = s.sb("mean", [P, D]), s.sb("scale", [P, D]), s.sb("root", [P, D])
        gm, bt = s.sb("gm", [P, D]), s.sb("bt", [P, D])
        pm, pv = s.ps("pm", [P, D]), s.ps("pv", [P, D])
        loaded, meaned, centred, squared, varied, shifted, rooted, chain_sem, done, stored = (
            s.sem(n) for n in ("loaded", "meaned", "centred", "squared", "varied", "shifted", "rooted", "chain", "done", "stored"))
        with nc.Block() as block:

            @block.sync
            def _(sp):
                sp.dma_start(X[:, :, :], x2.rearrange("b p n -> p b n")).then_inc(loaded, 16)
                load_rows(sp, [(gm, gamma), (bt, beta)], loaded)
                sp.wait_ge(done, 1)
                sp.dma_start(k["cat"][:, :, 2 * D:3 * D].rearrange("b p n -> p b n"), Q[:, :, :]).then_inc(stored, 16)
                sp.wait_ge(stored, 16)

            @block.tensor
            def _(pe):
                pe.wait_ge(loaded, 48)
                for q in range(NB):
                    ins = nc.tensor.matmul(pm[:, :], k["ones"][0:P, :], X[:, q, :], start=(q == 0), stop=(q == NB - 1))
                ins.then_inc(meaned, 1)
                pe.wait_ge(squared, 1)
                for q in range(NB):
                    ins = nc.tensor.matmul(pv[:, :], k["ones"][0:P, :], Q[:, q, :], start=(q == 0), stop=(q == NB - 1))
                ins.then_inc(varied, 1)

            @block.scalar
            def _(act):
                act.wait_ge(centred, 1)
                nc.scalar.activation(Q[:, :, :], X[:, :, :], ACT.Square).then_inc(squared, 1)
                act.wait_ge(shifted, 1)
                nc.scalar.activation(root[:, :], scale[:, :], ACT.Sqrt).then_inc(rooted, 1)

            @block.vector
            def _(dve):
                v = nc.vector
                chain = Chain(dve, chain_sem)
                wide = (lambda t: t[:, :].unsqueeze(1).to_broadcast([P, NB, D]))
                dve.wait_ge(loaded, 48)
                dve.wait_ge(meaned, 1)
                chain(v.tensor_scalar(mean[:, :], pm[:, :], 1.0 / N, None, ALU.mult))
                v.tensor_tensor(X[:, :, :], X[:, :, :], wide(mean), ALU.subtract).then_inc(centred, 1)
                dve.wait_ge(varied, 1)
                v.tensor_scalar(scale[:, :], pv[:, :], 1.0 / N, EPS, ALU.mult, ALU.add).then_inc(shifted, 1)
                dve.wait_ge(rooted, 1)
                chain(v.reciprocal(scale[:, :], root[:, :]))
                chain(v.tensor_tensor(scale[:, :], scale[:, :], gm[:, :], ALU.mult))
                chain(v.tensor_tensor(Q[:, :, :], X[:, :, :], wide(scale), ALU.mult))
                v.tensor_tensor(Q[:, :, :], Q[:, :, :], wide(bt), ALU.add).then_inc(done, 1)
        clear_semaphores(nc, s)


def phase_gates(nc, k, x2, w_x2i, b_x2i, w_h2h, x3):
    ctx = ExitStack()
    KC = 3 * D // 128
    with ctx:
        s = Scope(nc, ctx, "upd")
        x = s.sb("x", [P, 2, 3 * D])
        xt = s.sb("xt", [128, 2, KC, P])
        w = s.sb("w", [128, KC, 2 * D])
        X, Hn = s.sb("X", [P, NB, D]), s.sb("Hn", [P, NB, D])
        bias = s.sb("bias", [P, 2 * D])
        pre, gate = s.sb("pre", [P, 2, 2 * D]), s.sb("gate", [P, 2, 2 * D])
        r, y = s.sb("r", [P, 2, D]), s.sb("y", [P, 2, D])
        pt, po = s.ps("pt", [128, 2, 1024]), s.ps("po", [128, 2, 512])
        nm = Norm(s)
        ready, chain_sem = s.sem("ready"), s.sem("chain")
        i0 = 5 * k["gemm_turn"]
        k["gemm_turn"] += 1
        loaded, turned, copied, multiplied, finished, stored = (
            k["gemm_steps"][n].from_turn(i0) for n in ("loaded", "turned", "copied", "multiplied", "finished", "stored"))
        biased, gated = s.steps("biased"), s.steps("gated", head=1)
        PER = 5 + Norm.CHAINED
        with nc.Block() as block:

            @block.sync
            def _(sp):
                sp.dma_start(w[:, 0:4, :], w_x2i.rearrange("(t c) n -> c t n", c=128)).then_inc(ready, 16)
                sp.dma_start(w[:, 4:6, :], w_h2h.rearrange("(t c) n -> c t n", c=128)).then_inc(ready, 16)
                load_rows(sp, [(bias, b_x2i)], ready)
                sp.dma_start(X[:, :, :], x2.rearrange("b p n -> p b n")).then_inc(ready, 16)
                sp.dma_start(Hn[:, :, :], k["cat"][:, :, 2 * D:3 * D].rearrange("b p n -> p b n")).then_inc(ready, 16)
                with sp.Fori(0, 5) as i:
                    for j in range(5):
                        turned.freed(sp, i, j)
                        sp.dma_start(x[:, j % 2, :], k["cat"][ds(5 * i + j, 1)].rearrange("o p n -> (o p) n")).then_inc(loaded.sem(j), 16)

            @block.gpsimd
            def _(pool):
                with pool.Fori(0, 5) as i:
                    for j in range(5):
                        finished.after(pool, i, j)
                        pool.dma_start(x3[ds(5 * i + j, 1)].rearrange("o p n -> (o p) n"), y[:, j % 2, :]).then_inc(stored.sem(j), 16)
                for j in range(2):
                    stored.freed(pool, 5, j)

            @block.tensor
            def _(pe):
                t_ = nc.tensor

                def turn(i, j):
                    loaded.after(pe, i, j)
                    copied.freed(pe, i, j)
                    for t in range(KC):
                        ins = t_.transpose(pt[:, j % 2, 128 * t:128 * t + P], x[:, j % 2, 128 * t:128 * t + 128], k["ident"][0:P, 0:P])
                    ins.then_inc(turned.sem(j), 1)

                pe.wait_ge(ready, 80)
                with pe.Fori(0, 5) as i:
                    turn(i, 0)
                    for j in range(5):
                        if j < 4:
                            turn(i, j + 1)
                        copied.after(pe, i, j)
                        biased.freed(pe, i, j)
                        for t in range(KC):
                            ins = t_.matmul(po[0:P, j % 2, :], xt[:, j % 2, t, :], w[:, t, :], start=(t == 0), stop=(t == KC - 1))
                        ins.then_inc(multiplied.sem(j), 1)

            @block.scalar
            def _(act):
                def copy(i, j):
                    turned.after(act, i, j)
                    multiplied.freed(act, i, j)
                    nc.scalar.copy(xt[:, j % 2, :, :], pt[:, j % 2, 0:KC * 128].rearrange("p (t q) -> p t q", q=128)[:, :, 0:P]
                                   ).then_inc(copied.sem(j), 1)

                gated.begin(act)
                with act.Fori(0, 5) as i:
                    copy(i, 0)
                    for j in range(5):
                        if j < 4:
                            copy(i, j + 1)
                        biased.after(act, i, j)
                        finished.freed(act, i, j)
                        nc.scalar.activation(gate[:, j % 2, 0:D], pre[:, j % 2, 0:D], ACT.Sigmoid)
                        nc.scalar.activation(gate[:, j % 2, D:2 * D], pre[:, j % 2, D:2 * D], ACT.Tanh).then_inc(gated.sem(j), 1)
                        nm.on_act(nc, act, i, j)

            @block.vector
            def _(dve):
                v = nc.vector
                dve.wait_ge(ready, 80)
                with dve.Fori(0, 5) as i:
                    for j in range(5):
                        b, h = 5 * i + j, j % 2
                        chain = Chain(dve, chain_sem, b * PER)
                        at = (lambda A: A[:, ds(b, 1), :].rearrange("p a n -> p (a n)"))
                        multiplied.after(dve, i, j)
                        gated.freed(dve, i, j)
                        chain(v.tensor_tensor(pre[:, h, :], po[0:P, h, :], bias[:, :], ALU.add))
                        dve.sem_inc(biased.sem(j), 1)
                        gated.after(dve, i, j)
                        new = gate[:, h, D:2 * D]
                        chain(v.tensor_tensor(r[:, h, :], at(Hn), new, ALU.subtract))
                        chain(v.tensor_tensor(r[:, h, :], r[:, h, :], gate[:, h, 0:D], ALU.mult))
                        chain(v.tensor_tensor(r[:, h, :], r[:, h, :], new, ALU.add))
                        chain(v.tensor_tensor(r[:, h, :], r[:, h, :], at(X), ALU.add))
                        stored.freed(dve, i, j)
                        nm.on_dve(nc, dve, chain, i, j, r[:, h, :], y[:, h, :])
                        assert chain.n == PER
                        dve.sem_inc(finished.sem(j), 1)
        clear_semaphores(nc, s)


def phase_decoder(nc, k, h3, w_lin, b_lin, w_dec1, b_dec1, w_dec2, b_dec2, x3, out):
    ctx = ExitStack()
    HID0, HID1 = w_lin.shape
    with ctx:
        s = Scope(nc, ctx, "dec")
        x = s.sb("x", [P, 2, HID0])
        ht, zt, dt = s.sb("ht", [HID0, 2, P]), s.sb("zt", [HID1, 2, P]), s.sb("dt", [HID0, 2, P])
        wl, w1, w2 = s.sb("wl", [HID0, HID1]), s.sb("w1", [HID1, HID0]), s.sb("w2", [HID0, D])
        bl, b1, b2 = s.sb("bl", [HID1, 1]), s.sb("b1", [HID0, 1]), s.sb("b2", [P, D])
        X = s.sb("X", [P, NB, D])
        r, y = s.sb("r", [P, 2, D]), s.sb("y", [P, 2, D])
        pt, pz, pd, po = (s.ps(n, [128, 2, 512]) for n in ("pt", "pz", "pd", "po"))
        nm = Norm(s)
        ready, chain_sem = s.sem("ready"), s.sem("chain")
        i0 = 5 * k["gemm_turn"]
        k["gemm_turn"] += 1
        loaded, turned, copied, multiplied, finished, stored = (
            k["gemm_steps"][n].from_turn(i0) for n in ("loaded", "turned", "copied", "multiplied", "finished", "stored"))
        lined, z_ready, decoded, d_ready = (s.steps(n, head=1) for n in ("lined", "z_ready", "decoded", "d_ready"))
        PER = 2 + Norm.CHAINED
        with nc.Block() as block:

            @block.sync
            def _(sp):
                sp.dma_start(wl[:, :], w_lin).then_inc(ready, 16)
                sp.dma_start(w1[:, :], w_dec1).then_inc(ready, 16)
                sp.dma_start(w2[:, :], w_dec2).then_inc(ready, 16)
                sp.dma_start(bl[:, :], b_lin.unsqueeze(1)).then_inc(ready, 16)
                sp.dma_start(b1[:, :], b_dec1.unsqueeze(1)).then_inc(ready, 16)
                load_rows(sp, [(b2, b_dec2)], ready)
                sp.dma_start(X[:, :, :], x3.rearrange("b p n -> p b n")).then_inc(ready, 16)
                with sp.Fori(0, 5) as i:
                    for j in range(5):
                        turned.freed(sp, i, j)
                        sp.dma_start(x[:, j % 2, :], h3[ds(5 * i + j, 1)].rearrange("o p n -> (o p) n")).then_inc(loaded.sem(j), 16)

            @block.gpsimd
            def _(pool):
                with pool.Fori(0, 5) as i:
                    for j in range(5):
                        finished.after(pool, i, j)
                        pool.dma_start(out[ds(5 * i + j, 1)].rearrange("o p n -> (o p) n"), y[:, j % 2, :]).then_inc(stored.sem(j), 16)
                for j in range(2):
                    stored.freed(pool, 5, j)

            @block.tensor
            def _(pe):
                t_ = nc.tensor

                def turn(i, j):
                    loaded.after(pe, i, j)
                    copied.freed(pe, i, j)
                    t_.transpose(pt[:, j % 2, 0:P], x[:, j % 2, :], k["ident"][0:P, 0:P]).then_inc(turned.sem(j), 1)

                pe.wait_ge(ready, 16 * 7)
                lined.begin(pe)
                decoded.begin(pe)
                with pe.Fori(0, 5) as i:
                    turn(i, 0)
                    for j in range(5):
                        h = j % 2
                        if j < 4:
                            turn(i, j + 1)
                        copied.after(pe, i, j)
                        z_ready.freed(pe, i, j)
                        t_.matmul(pz[0:HID1, h, 0:P], wl[:, :], ht[:, h, :], start=True, stop=True).then_inc(lined.sem(j), 1)
                        z_ready.after(pe, i, j)
                        d_ready.freed(pe, i, j)
                        t_.matmul(pd[0:HID0, h, 0:P], w1[:, :], zt[:, h, :], start=True, stop=True).then_inc(decoded.sem(j), 1)
                        d_ready.after(pe, i, j)
                        finished.freed(pe, i, j)
                        t_.matmul(po[0:P, h, 0:D], dt[:, h, :], w2[:, :], start=True, stop=True).then_inc(multiplied.sem(j), 1)

            @block.scalar
            def _(act):
                act.wait_ge(ready, 16 * 7)
                z_ready.begin(act)
                d_ready.begin(act)
                with act.Fori(0, 5) as i:
                    for j in range(5):
                        h = j % 2
                        turned.after(act, i, j)
                        lined.freed(act, i, j)
                        nc.scalar.copy(ht[:, h, :], pt[:, h, 0:P]).then_inc(copied.sem(j), 1)
                        lined.after(act, i, j)
                        decoded.freed(act, i, j)
                        nc.scalar.activation(zt[:, h, :], pz[0:HID1, h, 0:P], ACT.Identity, bias=bl[:, :]).then_inc(z_ready.sem(j), 1)
                        decoded.after(act, i, j)
                        multiplied.freed(act, i, j)
                        nc.scalar.activation(dt[:, h, :], pd[0:HID0, h, 0:P], ACT.Relu, bias=b1[:, :]).then_inc(d_ready.sem(j), 1)
                        if j > 0:
                            nm.on_act(nc, act, i, j - 1)
                    nm.on_act(nc, act, i, 4)

            @block.vector
            def _(dve):
                v = nc.vector
                dve.wait_ge(ready, 16 * 7)
                with dve.Fori(0, 5) as i:
                    for j in range(5):
                        b, h = 5 * i + j, j % 2
                        chain = Chain(dve, chain_sem, b * PER)
                        multiplied.after(dve, i, j)
                        chain(v.tensor_tensor(r[:, h, :], po[0:P, h, 0:D], b2[:, :], ALU.add))
                        chain(v.tensor_tensor(r[:, h, :], r[:, h, :], X[:, ds(b, 1), :].rearrange("p a n -> p (a n)"), ALU.add))
                        stored.freed(dve, i, j)
                        nm.on_dve(nc, dve, chain, i, j, r[:, h, :], y[:, h, :])
                        assert chain.n == PER
                        dve.sem_inc(finished.sem(j), 1)
        clear_semaphores(nc, s)


def build_program(nc, a, out):
    ctx = ExitStack()
    with ctx:
        s = Scope(nc, ctx, "all")

        def dram(name, shape):
            return nc.dram_tensor(name, shape, fp32).ap()

        k = {
            "iota": s.sb("iota", [128, P]), "iota_bf": s.sb("iota_bf", [128, P], bf16),
            "ones": s.sb("ones", [128, P]), "zeros_bf": s.sb("zeros_bf", [128, 512], bf16),
            "ident": s.sb("ident", [128, 128]),
            "group_start": s.sb("group_start", [1, 32], i32), "tile_at": s.sb("tile_at", [1, NCA], i32),
            "parts_at": [s.sb(f"parts_at{f}", [1, NCA], i32) for f in (SRC, DST)],
            "dinv": s.sb("dinv", [P, NB]), "hs": s.sb("hs", [P, NB]),
            "hot": nc.dram_tensor("hot", [NGA, L, 2, G * P], bf16).ap(), "slots": dram("slots", [L, NCA, F]), "key_rows": dram("key_rows", [EC, P]), "dblk_rows": dram("dblk_rows", [EC, P]),
            "counts": dram("counts", [NB, P, NB * P]),
            "table": dram("table", [NB, P, 2 * D]), "cat": dram("cat", [NB, P, 3 * D]),
            "columns": 8, "spare": dram("spare", [8, P]), "spare_rows": 0, "sent": s.steps("sent", 2, 2, 16 * 8, head=16), "gemm_turn": 0, "apply_turn": 0,
        }
        k["gemm_steps"] = {n: s.steps(f"gemm_{n}", amount=16 if n in ("loaded", "stored") else 1,
                                           head={"loaded": 0, "stored": 16}.get(n, 1))
                           for n in ("loaded", "turned", "copied", "multiplied", "finished", "stored")}
        k["apply_steps"] = {n: s.steps(f"apply_{n}", amount=16 if n in ("loaded", "stored") else 1,
                                           head={"loaded": 0, "stored": 16}.get(n, 1))
                            for n in ("loaded", "summed", "finished", "stored")}
        x0 = a["x"].rearrange("(b p) n -> b p n", p=P)
        t1, t2, t3 = dram("t1", [NB, P, D]), dram("t2", [NB, P, D]), dram("t3", [NB, P, D + 1])
        h1, x1, x2, x3 = (dram(n, [NB, P, D]) for n in ("h1", "x1", "x2", "x3"))
        k["t3"] = t3
        t4, h3 = dram("t4", [NB, P, DE]), dram("h3", [NB, P, DE])
        v = nc.vector

        phase_order(nc, k, a["src"], a["dst"], a["edge_weight"], a["edge_weight_n2"], a["edge_attr_128"],
                    a["L1_gnn_We"], a["L1_gnn_be"], a["L1_gnn_attn"])
        with ExitStack() as inner:
            k["edges"] = inner.enter_context(nc.sbuf_tensor("edges", [L, NCA, F], fp32))
            phase_adjacency(nc, k)

            def scaled(width):
                def epilogue(dve, chain, b, po, y, tiles):
                    chain(v.tensor_scalar(y, po[:, 0:width], k["dinv"][:, ds(b, 1)], None, ALU.mult))
                return epilogue

            def hidden(dve, chain, i, j, b, t, y, tiles, x, nm):
                chain(v.tensor_scalar(y, t, k["dinv"][:, ds(b, 1)], 0.0, ALU.mult, ALU.max))

            def normed(dve, chain, i, j, b, t, y, tiles, x, nm):
                chain(v.scalar_tensor_tensor(t, t, k["dinv"][:, ds(b, 1)], x, ALU.mult, ALU.add))
                nm.on_dve(nc, dve, chain, i, j, t, y)

            phase_gemm(nc, k, "w1", x0, 2, [(a["L0_gnn_W1"], 0, D)], D, t1, D, {}, 1, scaled(D))
            phase_apply(nc, k, "c1", t1, D, h1, {}, 2, hidden)
            phase_gemm(nc, k, "w2", h1, 2, [(a["L0_gnn_W2"], 0, D)], D, t2, D, {}, 1, scaled(D))
            phase_apply(nc, k, "c2", t2, D, x1, {}, 2 + Norm.CHAINED, normed, resid=x0, norm=True)

            def with_logit(dve, chain, b, po, y, tiles):
                chain(v.tensor_tensor(y[:, 0:D], po[:, 0:D], tiles["bn"][:, :], ALU.add))
                chain(v.scalar_tensor_tensor(po[:, 0:D], y[:, 0:D], 1.0, tiles["attn"][:, :], ALU.mult, ALU.mult,
                                             accum_out=k["hs"][:, ds(b, 1)]))

            def ones_column(dve, y, sem):
                for h in range(2):
                    v.memset(y[:, h, D:D + 1], 1.0).then_inc(sem, 1)
                dve.wait_ge(sem, 2)

            phase_gemm(nc, k, "wn", x1, 2, [(a["L1_gnn_WnT"], 0, D)], D, t3, D + 1,
                       {"bn": a["L1_gnn_bn"], "attn": a["L1_gnn_attn"].rearrange("o h n -> (o h n)")}, 2, with_logit, ones_column)
            wide = k["table"]
            phase_attention(nc, k, x1, x2)

            phase_batch_norm(nc, k, x2, a["L2_gnn_gamma"], a["L2_gnn_beta"])

            def biased(dve, chain, b, po, y, tiles):
                chain(v.tensor_tensor(y[:, 0:D], po[:, 0:D], tiles["bi"][:, :], ALU.add))
                chain(v.tensor_tensor(y[:, D:2 * D], po[:, D:2 * D], tiles["bo"][:, :], ALU.add))

            phase_gemm(nc, k, "wio", k["cat"][:, :, 2 * D:3 * D], 2, [(a["L2_gnn_W_in"], 0, D), (a["L2_gnn_W_out"], D, D)], 2 * D,
                       wide, 2 * D, {"bi": a["L2_gnn_b_in"], "bo": a["L2_gnn_b_out"]}, 2, biased)
            phase_gated_in(nc, k, wide[:, :, 0:D])
            phase_gated_out(nc, k, wide[:, :, D:2 * D])
        phase_gates(nc, k, x2, a["L2_gnn_W_x2i"], a["L2_gnn_b_x2i"], a["L2_gnn_W_h2h"], x3)

        def relued(dve, chain, i, j, b, t, y, tiles, x, nm):
            chain(v.scalar_tensor_tensor(t, t, k["dinv"][:, ds(b, 1)], tiles["bc"][:, :], ALU.mult, ALU.add))
            chain(v.tensor_scalar(y, t, 0.0, None, ALU.max))

        phase_gemm(nc, k, "wc", x3, 2, [(a["L3_gnn_W_conv"], 0, DE)], DE, t4, DE, {}, 1, scaled(DE))
        phase_apply(nc, k, "c3", t4, DE, h3, {"bc": a["L3_gnn_b_conv"]}, 3, relued)
        phase_decoder(nc, k, h3, a["L3_gnn_W_lin"], a["L3_gnn_b_lin"], a["L3_gnn_W_dec1"], a["L3_gnn_b_dec1"],
                      a["L3_gnn_W_dec2"], a["L3_gnn_b_dec2"], x3, out.rearrange("(b p) n -> b p n", p=P))


_INS = ['x', 'src', 'dst', 'edge_attr_128', 'edge_weight', 'edge_weight_n2', 'L0_gnn_W1', 'L0_gnn_W2', 'L1_gnn_Wn',
        'L1_gnn_bn', 'L1_gnn_We', 'L1_gnn_be', 'L1_gnn_attn', 'L2_gnn_gamma', 'L2_gnn_beta', 'L2_gnn_W_in', 'L2_gnn_b_in',
        'L2_gnn_W_out', 'L2_gnn_b_out', 'L2_gnn_W_x2i', 'L2_gnn_b_x2i', 'L2_gnn_W_h2h', 'L3_gnn_W_conv', 'L3_gnn_b_conv',
        'L3_gnn_W_lin', 'L3_gnn_b_lin', 'L3_gnn_W_dec1', 'L3_gnn_b_dec1', 'L3_gnn_W_dec2', 'L3_gnn_b_dec2']


def kernel(**inputs):
    import numpy as _np
    import concourse.bacc as _bacc
    from concourse import mybir as _mybir
    from concourse.bass_utils import run_bass_kernel_spmd as _run

    nc = _bacc.Bacc("TRN2", target_bir_lowering=False, num_devices=1)
    arrays, args = {}, {}
    for name in _INS:
        a = _np.asarray(inputs[name])
        if name == 'L1_gnn_Wn':
            name, a = 'L1_gnn_WnT', a.T
        a = _np.ascontiguousarray(a)
        arrays[f"in_{name}_dram"] = a
        args[name] = nc.dram_tensor(f"in_{name}_dram", a.shape, _mybir.dt.from_np(a.dtype), kind="ExternalInput").ap()
    out = nc.dram_tensor("out_0_dram", (N, D), _mybir.dt.float32, kind="ExternalOutput").ap()
    build_program(nc, args, out)
    r = _run(nc, [arrays], core_ids=[0])
    return r.results[0]["out_0_dram"]
```
